# Optimizing a Trainium2 kernel written in Bass

```python
import numpy as np
import jax
import jax.numpy as jnp

def _softmax(x, axis=-1):
    return jax.nn.softmax(x, axis=axis)

def _gelu(x):
    return jax.nn.gelu(x, approximate=True)

def _silu(x):
    return jax.nn.silu(x)

def _sigmoid(x):
    return jax.nn.sigmoid(x)

def _layernorm(x, axis=-1, eps=1e-05):
    m = jnp.mean(x, axis=axis, keepdims=True)
    v = jnp.var(x, axis=axis, keepdims=True)
    return (x - m) / jnp.sqrt(v + eps)

def _scatter_add(tgt, idx, src, axis=0):
    return tgt.at[idx].add(src)

def _segment_sum(src, seg, n):
    return jax.ops.segment_sum(src, seg, n)
kernel_name = 'mk_prb_d1_jaxref_r4_63e233'

def setup_inputs(seed: int=0):
    np.random.seed(seed)
    _w = jnp.asarray

    def _L0_attn_setup():
        import jax, jax.numpy as jnp
        import numpy as np
        import math
        FEATURE_DIM = 16
        NUM_HEADS = 16
        HIDDEN = 256
        HEAD_DIM = HIDDEN // NUM_HEADS
        EPS = 1e-12
        IU, JU = np.triu_indices(FEATURE_DIM, 1)
        RD = math.sqrt(FEATURE_DIM)
        RRD = math.sqrt(RD)
        R2 = math.sqrt(2.0)

        def taylor_feature_map(x):
            x2 = x[..., :, None] * x[..., None, :]
            off = x2[..., IU, JU]
            diag = jnp.square(x)
            ones = jnp.ones_like(x[..., :1])
            return jnp.concatenate([ones, x / RRD, diag / (RD * R2), off / RD], axis=-1)
        key = jax.random.key(seed)
        k0, k1, k2, k3, k4 = jax.random.split(key, 5)
        b, t = (2, 128)
        s = 1.0 / math.sqrt(HIDDEN)
        return {'hidden_states': jax.random.normal(k0, (b, t, HIDDEN), jnp.float32), 'Wq': jax.random.normal(k1, (NUM_HEADS * FEATURE_DIM, HIDDEN), jnp.float32) * s, 'Wk': jax.random.normal(k2, (NUM_HEADS * FEATURE_DIM, HIDDEN), jnp.float32) * s, 'Wv': jax.random.normal(k3, (HIDDEN, HIDDEN), jnp.float32) * s, 'Wo': jax.random.normal(k4, (HIDDEN, HIDDEN), jnp.float32) * s}
    _L0_attn_in = _L0_attn_setup()

    def _L0_ffn_setup():
        import jax, jax.numpy as jnp
        import numpy as np
        DIM = 256
        DEPTH = 2
        HEADS = 8
        DIM_HEAD = 64
        WINDOW = 128
        INNER = HEADS * DIM_HEAD
        HID = int(DIM * 4 * 2 / 3)
        B, N = (2, 2048)
        QK_SCALE = 8.0

        def shift_token(t):
            t1, t2 = jnp.split(t, 2, axis=-1)
            t2 = jnp.pad(t2, ((0, 0), (1, 0), (0, 0)))[:, :-1]
            return jnp.concatenate([t1, t2], axis=-1)

        def l2norm(t):
            return t / jnp.clip(jnp.linalg.norm(t, axis=-1, keepdims=True), 1e-12)

        def rotate_half(x):
            x1, x2 = jnp.split(x, 2, axis=-1)
            return jnp.concatenate([-x2, x1], axis=-1)

        def rotary_xpos(q, k):
            n = q.shape[-2]
            half_idx = jnp.arange(0, DIM_HEAD, 2, dtype=jnp.float32)
            inv_freq = 1.0 / 10000.0 ** (half_idx / DIM_HEAD)
            t = jnp.arange(n, dtype=jnp.float32)
            freqs = t[:, None] * inv_freq[None, :]
            freqs = jnp.concatenate([freqs, freqs], axis=-1)
            base = (half_idx + 0.4 * DIM_HEAD) / (1.4 * DIM_HEAD)
            power = (t - n // 2) / float(WINDOW // 2)
            scale = base[None, :] ** power[:, None]
            scale = jnp.concatenate([scale, scale], axis=-1)
            cos, sin = (jnp.cos(freqs), jnp.sin(freqs))
            q = q * cos * scale + rotate_half(q) * sin * scale
            k = k * cos / scale + rotate_half(k) * sin / scale
            return (q, k)

        def local_attention(q, k, v):
            b, h, n, d = q.shape
            w = n // WINDOW
            bq = q.reshape(b, h, w, WINDOW, d) * QK_SCALE
            bk = k.reshape(b, h, w, WINDOW, d)
            bv = v.reshape(b, h, w, WINDOW, d)

            def look_around(t):
                p = jnp.pad(t, ((0, 0), (0, 0), (1, 0), (0, 0), (0, 0)))
                return jnp.concatenate([p[:, :, :w], p[:, :, 1:]], axis=3)
            bk, bv = (look_around(bk), look_around(bv))
            bt = jnp.arange(n).reshape(w, WINDOW)
            btp = jnp.pad(bt, ((1, 0), (0, 0)), constant_values=-1)
            btk = jnp.concatenate([btp[:w], btp[1:]], axis=1)
            sim = jnp.einsum('bhwid,bhwjd->bhwij', bq, bk)
            i = bt[:, :, None]
            j = btk[:, None, :]
            mask = (i < j) | (i > j + WINDOW) | (j == -1)
            sim = jnp.where(mask, -jnp.finfo(sim.dtype).max, sim)
            attn = jax.nn.softmax(sim, axis=-1)
            out = jnp.einsum('bhwij,bhwjd->bhwid', attn, bv)
            return out.reshape(b, h, n, d)

        def _layer(x, wqkv, qs, ksc, wo, lg, lb, w1, b1, w2, b2):
            b, n, _ = x.shape
            h = shift_token(x)
            qkv = h @ wqkv
            q, k, v = jnp.split(qkv, 3, axis=-1)
            to_heads = lambda t: t.reshape(b, n, HEADS, DIM_HEAD).transpose(0, 2, 1, 3)
            q, k, v = (to_heads(q), to_heads(k), to_heads(v))
            q = l2norm(q) * qs
            k = l2norm(k) * ksc
            q, k = rotary_xpos(q, k)
            o = local_attention(q, k, v)
            o = o.transpose(0, 2, 1, 3).reshape(b, n, INNER)
            x = x + o @ wo
            h = shift_token(x)
            mu = h.mean(-1, keepdims=True)
            var = h.var(-1, keepdims=True)
            h = (h - mu) / jnp.sqrt(var + 1e-05) * lg + lb
            h = h @ w1 + b1
            a, g = jnp.split(h, 2, axis=-1)
            h = a * jax.nn.gelu(g, approximate=False)
            x = x + h @ w2 + b2
            return x
        key = jax.random.key(seed)
        ks = jax.random.split(key, 6)
        return {'x': jax.random.normal(ks[0], (B, N, DIM), jnp.float32), 'wqkv': jax.random.normal(ks[1], (DEPTH, DIM, 3 * INNER), jnp.float32) * 0.02, 'q_scale': jnp.ones((DEPTH, DIM_HEAD), jnp.float32), 'k_scale': jnp.ones((DEPTH, DIM_HEAD), jnp.float32), 'wo': jax.random.normal(ks[2], (DEPTH, INNER, DIM), jnp.float32) * 0.02, 'ln_g': jnp.ones((DEPTH, DIM), jnp.float32), 'ln_b': jnp.zeros((DEPTH, DIM), jnp.float32), 'w1': jax.random.normal(ks[3], (DEPTH, DIM, 2 * HID), jnp.float32) * 0.02, 'b1': jnp.zeros((DEPTH, 2 * HID), jnp.float32), 'w2': jax.random.normal(ks[4], (DEPTH, HID, DIM), jnp.float32) * 0.02, 'b2': jnp.zeros((DEPTH, DIM), jnp.float32)}
    _L0_ffn_in = _L0_ffn_setup()
    _d = {'L0_attn_hidden_states': _L0_attn_in['hidden_states'], 'L0_attn_Wq': _L0_attn_in['Wq'], 'L0_attn_Wk': _L0_attn_in['Wk'], 'L0_attn_Wv': _L0_attn_in['Wv'], 'L0_attn_Wo': _L0_attn_in['Wo'], 'L0_ffn_wqkv': _L0_ffn_in['wqkv'], 'L0_ffn_q_scale': _L0_ffn_in['q_scale'], 'L0_ffn_k_scale': _L0_ffn_in['k_scale'], 'L0_ffn_wo': _L0_ffn_in['wo'], 'L0_ffn_ln_g': _L0_ffn_in['ln_g'], 'L0_ffn_ln_b': _L0_ffn_in['ln_b'], 'L0_ffn_w1': _L0_ffn_in['w1'], 'L0_ffn_b1': _L0_ffn_in['b1'], 'L0_ffn_w2': _L0_ffn_in['w2'], 'L0_ffn_b2': _L0_ffn_in['b2']}
    _x0 = _d['L0_attn_hidden_states']
    _d['L0_attn_hidden_states'] = jax.random.normal(jax.random.fold_in(jax.random.key(seed), 1), (8, 1024, 256), dtype=_x0.dtype)
    del _x0
    return _d

def reference(L0_attn_hidden_states, L0_attn_Wq, L0_attn_Wk, L0_attn_Wv, L0_attn_Wo, L0_ffn_wqkv, L0_ffn_q_scale, L0_ffn_k_scale, L0_ffn_wo, L0_ffn_ln_g, L0_ffn_ln_b, L0_ffn_w1, L0_ffn_b1, L0_ffn_w2, L0_ffn_b2):

    def _L0_attn_ref(hidden_states, Wq, Wk, Wv, Wo):
        import jax, jax.numpy as jnp
        import numpy as np
        import math
        FEATURE_DIM = 16
        NUM_HEADS = 16
        HIDDEN = 256
        HEAD_DIM = HIDDEN // NUM_HEADS
        EPS = 1e-12
        IU, JU = np.triu_indices(FEATURE_DIM, 1)
        RD = math.sqrt(FEATURE_DIM)
        RRD = math.sqrt(RD)
        R2 = math.sqrt(2.0)

        def taylor_feature_map(x):
            x2 = x[..., :, None] * x[..., None, :]
            off = x2[..., IU, JU]
            diag = jnp.square(x)
            ones = jnp.ones_like(x[..., :1])
            return jnp.concatenate([ones, x / RRD, diag / (RD * R2), off / RD], axis=-1)
        b, t, _ = hidden_states.shape
        q = (hidden_states @ Wq.T).reshape(b, t, NUM_HEADS, FEATURE_DIM).transpose(0, 2, 1, 3)
        k = (hidden_states @ Wk.T).reshape(b, t, NUM_HEADS, FEATURE_DIM).transpose(0, 2, 1, 3)
        v = (hidden_states @ Wv.T).reshape(b, t, NUM_HEADS, HEAD_DIM).transpose(0, 2, 1, 3)
        q = taylor_feature_map(q)
        k = taylor_feature_map(k)
        kv = jnp.cumsum(k[..., None, :] * v[..., :, None], axis=2)
        y = jnp.einsum('bhtD,bhtdD->bhtd', q, kv)
        z = jnp.cumsum(k, axis=2)
        denom = jnp.sum(q * z, axis=-1, keepdims=True) + EPS
        y = y / denom
        y = y.transpose(0, 2, 1, 3).reshape(b, t, NUM_HEADS * HEAD_DIM)
        return y @ Wo.T

    def _L0_ffn_ref(x, wqkv, q_scale, k_scale, wo, ln_g, ln_b, w1, b1, w2, b2):
        import jax, jax.numpy as jnp
        import numpy as np
        DIM = 256
        DEPTH = 2
        HEADS = 8
        DIM_HEAD = 64
        WINDOW = 128
        INNER = HEADS * DIM_HEAD
        HID = int(DIM * 4 * 2 / 3)
        B, N = (2, 2048)
        QK_SCALE = 8.0

        def shift_token(t):
            t1, t2 = jnp.split(t, 2, axis=-1)
            t2 = jnp.pad(t2, ((0, 0), (1, 0), (0, 0)))[:, :-1]
            return jnp.concatenate([t1, t2], axis=-1)

        def l2norm(t):
            return t / jnp.clip(jnp.linalg.norm(t, axis=-1, keepdims=True), 1e-12)

        def rotate_half(x):
            x1, x2 = jnp.split(x, 2, axis=-1)
            return jnp.concatenate([-x2, x1], axis=-1)

        def rotary_xpos(q, k):
            n = q.shape[-2]
            half_idx = jnp.arange(0, DIM_HEAD, 2, dtype=jnp.float32)
            inv_freq = 1.0 / 10000.0 ** (half_idx / DIM_HEAD)
            t = jnp.arange(n, dtype=jnp.float32)
            freqs = t[:, None] * inv_freq[None, :]
            freqs = jnp.concatenate([freqs, freqs], axis=-1)
            base = (half_idx + 0.4 * DIM_HEAD) / (1.4 * DIM_HEAD)
            power = (t - n // 2) / float(WINDOW // 2)
            scale = base[None, :] ** power[:, None]
            scale = jnp.concatenate([scale, scale], axis=-1)
            cos, sin = (jnp.cos(freqs), jnp.sin(freqs))
            q = q * cos * scale + rotate_half(q) * sin * scale
            k = k * cos / scale + rotate_half(k) * sin / scale
            return (q, k)

        def local_attention(q, k, v):
            b, h, n, d = q.shape
            w = n // WINDOW
            bq = q.reshape(b, h, w, WINDOW, d) * QK_SCALE
            bk = k.reshape(b, h, w, WINDOW, d)
            bv = v.reshape(b, h, w, WINDOW, d)

            def look_around(t):
                p = jnp.pad(t, ((0, 0), (0, 0), (1, 0), (0, 0), (0, 0)))
                return jnp.concatenate([p[:, :, :w], p[:, :, 1:]], axis=3)
            bk, bv = (look_around(bk), look_around(bv))
            bt = jnp.arange(n).reshape(w, WINDOW)
            btp = jnp.pad(bt, ((1, 0), (0, 0)), constant_values=-1)
            btk = jnp.concatenate([btp[:w], btp[1:]], axis=1)
            sim = jnp.einsum('bhwid,bhwjd->bhwij', bq, bk)
            i = bt[:, :, None]
            j = btk[:, None, :]
            mask = (i < j) | (i > j + WINDOW) | (j == -1)
            sim = jnp.where(mask, -jnp.finfo(sim.dtype).max, sim)
            attn = jax.nn.softmax(sim, axis=-1)
            out = jnp.einsum('bhwij,bhwjd->bhwid', attn, bv)
            return out.reshape(b, h, n, d)

        def _layer(x, wqkv, qs, ksc, wo, lg, lb, w1, b1, w2, b2):
            b, n, _ = x.shape
            h = shift_token(x)
            qkv = h @ wqkv
            q, k, v = jnp.split(qkv, 3, axis=-1)
            to_heads = lambda t: t.reshape(b, n, HEADS, DIM_HEAD).transpose(0, 2, 1, 3)
            q, k, v = (to_heads(q), to_heads(k), to_heads(v))
            q = l2norm(q) * qs
            k = l2norm(k) * ksc
            q, k = rotary_xpos(q, k)
            o = local_attention(q, k, v)
            o = o.transpose(0, 2, 1, 3).reshape(b, n, INNER)
            x = x + o @ wo
            h = shift_token(x)
            mu = h.mean(-1, keepdims=True)
            var = h.var(-1, keepdims=True)
            h = (h - mu) / jnp.sqrt(var + 1e-05) * lg + lb
            h = h @ w1 + b1
            a, g = jnp.split(h, 2, axis=-1)
            h = a * jax.nn.gelu(g, approximate=False)
            x = x + h @ w2 + b2
            return x
        for l in range(DEPTH):
            x = _layer(x, wqkv[l], q_scale[l], k_scale[l], wo[l], ln_g[l], ln_b[l], w1[l], b1[l], w2[l], b2[l])
        return x
    x = L0_attn_hidden_states
    xn = _layernorm(x, axis=-1)
    x = x + _L0_attn_ref(xn, L0_attn_Wq, L0_attn_Wk, L0_attn_Wv, L0_attn_Wo) + _L0_ffn_ref(xn, L0_ffn_wqkv, L0_ffn_q_scale, L0_ffn_k_scale, L0_ffn_wo, L0_ffn_ln_g, L0_ffn_ln_b, L0_ffn_w1, L0_ffn_b1, L0_ffn_w2, L0_ffn_b2)
    return x

_drawn_inputs = setup_inputs


def setup_inputs(seed=0):
    import zlib

    import numpy as np

    out = dict(_drawn_inputs(seed))
    spreads = {'L0_ffn_q_scale': (1.0, 0.6),
     'L0_ffn_k_scale': (1.0, 0.6),
     'L0_ffn_ln_g': (1.0, 0.6),
     'L0_ffn_ln_b': (0.0, 0.8),
     'L0_ffn_b1': (0.0, 0.8),
     'L0_ffn_b2': (0.0, 0.1)}
    factors = {'L0_ffn_wqkv': 3.362, 'L0_ffn_wo': 3.305}
    for name, (base, spread) in spreads.items():
        noise = np.random.default_rng([zlib.crc32(name.encode()), seed]).standard_normal(out[name].shape)
        drawn = base * np.exp(spread * noise) if base else spread * noise
        out[name] = jnp.asarray(drawn.astype(out[name].dtype))
    for name, factor in factors.items():
        out[name] = (out[name] * factor).astype(out[name].dtype)
    return out
```

```python
from contextlib import ExitStack

import numpy as np

import concourse.bass as bass
from concourse import mybir

F32 = mybir.dt.float32
BF16 = mybir.dt.bfloat16
ALU = mybir.AluOpType
ACT = mybir.ActivationFunctionType
AX = mybir.AxisListType.X

P = 128
DIM = 256
KC = DIM // P
TILES = 8
SEQ = P * TILES

TH, TD = 16, 16
GROUPS, GH = 4, 4
VP = 32
SLOTS = 6
SW = SLOTS * TD
TEPS2 = 2e-12

LAYERS, HEADS, HD = 2, 8, 64
INNER = HEADS * HD
HID = 682
FB = 6
FLAST = HID - (FB - 1) * P
LN_EPS = 1e-5


def taylor_block(nc, B, x, wqk, wv, wo, ident, ident_bf, causal, steps, tile_ones, den_rows, eps_rows,
                 xn_d, attn_d):
    with ExitStack() as ctx:
        def sb(name, shape, dt=F32):
            return ctx.enter_context(nc.sbuf_tensor(name, shape, dt))

        def sem(name):
            return ctx.enter_context(nc.semaphore("t_" + name))

        ps = ctx.enter_context(nc.psum_tensor("t_ps", [P, 8, 512], F32))

        wqk_s = sb("wqk_s", [P, KC, 512])
        wv_s = sb("wv_s", [P, KC, 256])
        wo_s = sb("two_s", [P, GROUPS, DIM])
        id_s = sb("t_id", [P, P])
        idb_s = sb("t_idb", [P, P], BF16)
        causal_s = sb("causal_s", [P, P])
        steps_s = sb("steps_s", [TILES, SEQ])
        tones_s = sb("tones_s", [P, TILES, TILES])
        denr_s = sb("denr_s", [P, P])
        eps_s = sb("eps_s", [P, 1])
        one_s = sb("one_s", [P, 1])
        mhalf = sb("mhalf", [P, TILES])
        xs = sb("xs", [P, TILES, DIM])
        xn = sb("xn", [P, TILES, DIM])
        xnT = sb("xnT", [P, KC, SEQ])
        st = sb("t_st", [P, TILES, 6])
        mv = sb("t_mv", [P, TILES, 2])
        ve = sb("t_ve", [P, TILES])
        rstd = sb("t_rstd", [P, TILES])
        parts = sb("parts", [P, TILES, 2, TH, SLOTS, TD], BF16)
        rest = sb("rest", [P, 2, 2, TH, TD])
        vals = sb("vals", [P, TILES, TH, VP])
        qkT = sb("qkT", [SW, 2, GH, SEQ], BF16)
        weights = sb("weights", [P, 4, 2, 512])
        bsum = sb("bsum", [TILES, TH * VP])
        yT = sb("yT", [P, GROUPS, SEQ])
        rden = sb("rden", [P, SEQ])
        ao = sb("ao", [P, TILES, DIM])

        const_in = sem("const_in")
        ones_set = sem("ones_set")
        x_in = sem("x_in")
        xn_out = sem("xn_out")
        attn_out = sem("attn_out")
        stats = sem("stats")
        var_ready = sem("var_ready")
        rstd_ready = sem("rstd_ready")
        xn_ready = sem("xn_ready")
        xnT_ps = sem("xnT_ps")
        xnT_ready = sem("xnT_ready")
        proj_ps = sem("proj_ps")
        high = sem("high")
        v_ready = sem("v_ready")
        rest_ready = sem("rest_ready")
        mid = sem("mid")
        low = sem("low")
        copies = sem("copies")
        bsum_ps = sem("bsum_ps")
        bsum_ready = sem("bsum_ready")
        qkT_ps = sem("qkT_ps")
        qT_ready = sem("qT_ready")
        kT_ready = sem("kT_ready")
        score_ps = sem("score_ps")
        squared = sem("squared")
        diag = sem("diag")
        pv_done = sem("pv_done")
        yT_ready = sem("yT_ready")
        den_ps = sem("den_ps")
        rden_ready = sem("rden_ready")
        y_ready = sem("y_ready")
        ao_ps = sem("ao_ps")
        ao_ready = sem("ao_ready")
        passed_pool = sem("passed_pool")
        passed_dve = sem("passed_dve")

        consts = [(wqk_s[:, :, :], wqk), (wv_s[:, :, :], wv), (wo_s[:, :, :], wo), (id_s[:, :], ident),
                  (idb_s[:, :], ident_bf), (causal_s[:, :], causal), (steps_s[:, :], steps),
                  (tones_s[:, :, :], tile_ones), (denr_s[:, :], den_rows), (eps_s[:, :], eps_rows)]
        CONST_IN = 16 * len(consts)

        STEPS = [(j, h, max(0, P * j - 512 * h)) for j in range(TILES) for h in range(2) if P * j < 512 * (h + 1)]
        NS = len(STEPS)
        NDIAG = 2 * TILES
        diag_no = {}
        for i, (j, h, c) in enumerate(STEPS):
            if j // 4 == h:
                diag_no[i] = len(diag_no)

        block = ctx.enter_context(nc.Block())

        @block.sync
        def _(sp):
            for dst, src in consts:
                sp.dma_start(dst, src).then_inc(const_in, 16)
            with sp.Fori(0, B) as b:
                sp.wait_ge(xn_ready, b * TILES)
                sp.dma_start(xs[:, :, :], x[b].rearrange("(t p) d -> p t d", p=P)).then_inc(x_in, 16)
                sp.wait_ge(xn_ready, b * TILES + TILES)
                sp.dma_start(xn_d[b].rearrange("(t p) d -> p t d", p=P), xn[:, :, :]).then_inc(xn_out, 16)
                sp.wait_ge(ao_ready, b * TILES + TILES)
                sp.dma_start(attn_d[b].rearrange("(t p) d -> p t d", p=P), ao[:, :, :]).then_inc(attn_out, 16)
            sp.wait_ge(xn_out, 16 * B)
            sp.wait_ge(attn_out, 16 * B)

        @block.gpsimd
        def _(pool):
            nc.gpsimd.memset(vals[:, :, :, TD:VP], 0.0).then_inc(ones_set, 1)
            nc.gpsimd.memset(mhalf[:, :], -0.5).then_inc(ones_set, 1)
            nc.gpsimd.memset(one_s[:, :], 1.0).then_inc(ones_set, 1)
            pool.wait_ge(ones_set, 3)
            nc.gpsimd.memset(vals[:, :, :, TD:TD + 1], 1.0).then_inc(ones_set, 1)
            with pool.Fori(0, B) as b:
                pool.wait_ge(var_ready, b + 1)
                nc.gpsimd.tensor_tensor(rstd[:, :], ve[:, :], mhalf[:, :], ALU.pow).then_inc(rstd_ready, 1)
                for t in range(TILES):
                    r = rest[:, t % 2]
                    pool.wait_ge(rest_ready, b * TILES + t + 1)
                    pool.sem_inc(passed_pool, 1)
                    nc.gpsimd.tensor_copy(parts[:, t, 0, :, 3:5, :], r[:, 0].unsqueeze(2).to_broadcast([P, TH, 2, TD])).then_inc(mid, 1)
                    nc.gpsimd.tensor_copy(parts[:, t, 1, :, 1, :], r[:, 1]).then_inc(mid, 1)
                    pool.wait_ge(mid, 2 * (b * TILES + t + 1))
                    nc.gpsimd.tensor_tensor(parts[:, t, 0, :, 5, :], r[:, 0], parts[:, t, 0, :, 3, :], ALU.subtract).then_inc(low, 1)
                    nc.gpsimd.tensor_tensor(parts[:, t, 1, :, 2, :], r[:, 1], parts[:, t, 1, :, 1, :], ALU.subtract).then_inc(low, 1)

        @block.vector
        def _(dve):
            dve.wait_ge(const_in, CONST_IN)
            with dve.Fori(0, B) as b:
                dve.wait_ge(x_in, 16 * b + 16)
                for t in range(TILES):
                    last = nc.vector.bn_stats(st[:, t, :], xs[:, t, :])
                last.then_inc(stats, 1)
                dve.wait_ge(stats, 2 * b + 1)
                dve.sem_inc(passed_dve, 1)
                for t in range(TILES):
                    last = nc.vector.bn_aggr(mv[:, t, :], st[:, t, :])
                last.then_inc(stats, 1)
                dve.wait_ge(stats, 2 * b + 2)
                nc.vector.tensor_scalar_add(ve[:, :], mv[:, :, 1], LN_EPS).then_inc(var_ready, 1)
                dve.wait_ge(rstd_ready, b + 1)
                dve.wait_ge(xn_out, 16 * b)
                for t in range(TILES):
                    nc.vector.tensor_scalar(xn[:, t, :], xs[:, t, :], mv[:, t, 0:1], rstd[:, t:t + 1],
                                            ALU.subtract, ALU.mult).then_inc(xn_ready, 1)

                def repeat_k(t):
                    dve.wait_ge(low, 2 * (b * TILES + t + 1))
                    nc.vector.tensor_copy(parts[:, t, 1, :, 3:5, :], parts[:, t, 1, :, 0:2, :]).then_inc(copies, 1)
                    nc.vector.tensor_copy(parts[:, t, 1, :, 5, :], parts[:, t, 1, :, 0, :]).then_inc(copies, 1)

                for t in range(TILES):
                    dve.wait_ge(high, b * TILES + t + 1)
                    if t >= 2:
                        dve.wait_ge(low, 2 * (b * TILES + t - 1))
                    nc.vector.tensor_tensor(rest[:, t % 2], ps[:, 4 + t % 2, :].rearrange("p (a h d) -> p a h d", a=2, h=TH),
                                            parts[:, t, :, :, 0, :], ALU.subtract).then_inc(rest_ready, 1)
                    if t >= 1:
                        repeat_k(t - 1)
                repeat_k(TILES - 1)

                for g in range(GROUPS):
                    for h in range(GH):
                        u = 2 * h
                        dve.wait_ge(qkT_ps, (b * GROUPS + g) * 2 * GH + u + 1)
                        nc.vector.tensor_copy(qkT[:, 0, h, :], ps[0:SW, 2 + u % 6, :].bitcast(BF16)).then_inc(qT_ready, 1)
                    for i, (j, half, c) in enumerate(STEPS):
                        if i in diag_no:
                            for pair in range(2):
                                u = 2 * i + pair
                                a = weights[:, u % 4, :, c:c + P]
                                dve.wait_ge(squared, (b * GROUPS + g) * 2 * NS + u + 1)
                                nc.vector.scalar_tensor_tensor(a, a, 1.0, causal_s[:, :].unsqueeze(1).to_broadcast([P, 2, P]),
                                                               ALU.add, ALU.mult).then_inc(diag, 1)
                    dve.wait_ge(den_ps, b * GROUPS + g + 1)
                    nc.vector.reciprocal(rden[:, :], ps[:, 2:4, :].rearrange("p a n -> p (a n)")).then_inc(rden_ready, 1)
                    dve.wait_ge(rden_ready, b * GROUPS + g + 1)
                    nc.vector.tensor_tensor(yT[:, g, :], yT[:, g, :], rden[:, :], ALU.mult).then_inc(y_ready, 1)

        @block.scalar
        def _(act):
            act.wait_ge(const_in, CONST_IN)
            act.wait_ge(ones_set, 4)
            with act.Fori(0, B) as b:
                for t in range(TILES):
                    act.wait_ge(xnT_ps, b * TILES + t + 1)
                    nc.scalar.activation(xnT[:, :, t * P:(t + 1) * P], ps[:, 2 + t % 2, 0:KC * P].rearrange("p (c n) -> p c n", c=KC),
                                         ACT.Copy).then_inc(xnT_ready, 1)
                for t in range(TILES):
                    act.wait_ge(proj_ps, b * TILES + t + 1)
                    qk = ps[:, 4 + t % 2, :].rearrange("p (a h d) -> p a h d", a=2, h=TH)
                    nc.scalar.activation(parts[:, t, 0, :, 0:3, :], qk[:, 0].unsqueeze(2).to_broadcast([P, TH, 3, TD]), ACT.Copy)
                    nc.scalar.activation(parts[:, t, 1, :, 0, :], qk[:, 1], ACT.Copy).then_inc(high, 1)
                    nc.scalar.activation(vals[:, t, :, 0:TD], ps[:, 6 + t % 2, 0:TH * TD].rearrange("p (h d) -> p h d", h=TH),
                                         ACT.Copy).then_inc(v_ready, 1)
                act.wait_ge(bsum_ps, b + 1)
                nc.scalar.activation(bsum[:, :], ps[0:TILES, 0, :], ACT.Copy).then_inc(bsum_ready, 1)
                for g in range(GROUPS):
                    for h in range(GH):
                        u = 2 * h + 1
                        act.wait_ge(qkT_ps, (b * GROUPS + g) * 2 * GH + u + 1)
                        nc.scalar.activation(qkT[:, 1, h, :], ps[0:SW, 2 + u % 6, :].bitcast(BF16), ACT.Copy).then_inc(kT_ready, 1)
                    for i, (j, half, c) in enumerate(STEPS):
                        for pair in range(2):
                            u = 2 * i + pair
                            act.wait_ge(score_ps, (b * GROUPS + g) * 2 * NS + u + 1)
                            if i >= 2:
                                act.wait_ge(pv_done, (b * GROUPS + g) * NS + i - 1)
                            s0 = 2 + 2 * (u % 3)
                            nc.scalar.activation(weights[:, u % 4, :, c:512], ps[:, s0:s0 + 2, c:512], ACT.Square,
                                                 bias=one_s[:, :], scale=0.25).then_inc(squared, 1)
                    act.wait_ge(pv_done, (b * GROUPS + g) * NS + NS)
                    nc.scalar.activation(yT[:, g, :], ps[:, 0:2, :].rearrange("p a n -> p (a n)"), ACT.Identity,
                                         bias=eps_s[:, :]).then_inc(yT_ready, 1)
                act.wait_ge(attn_out, 16 * b)
                for t in range(TILES):
                    act.wait_ge(ao_ps, b * TILES + t + 1)
                    nc.scalar.activation(ao[:, t, :], ps[:, 4 + t % 2, 0:DIM], ACT.Copy).then_inc(ao_ready, 1)

        @block.tensor
        def _(pe):
            mm = nc.tensor.matmul
            pe.wait_ge(const_in, CONST_IN)
            with pe.Fori(0, B) as b:
                for t in range(TILES):
                    pe.wait_ge(xn_ready, b * TILES + t + 1)
                    if t >= 2:
                        pe.wait_ge(xnT_ready, b * TILES + t - 1)
                    for c in range(KC):
                        last = nc.tensor.transpose(ps[:, 2 + t % 2, c * P:(c + 1) * P], xn[:, t, c * P:(c + 1) * P], id_s[:, :])
                    last.then_inc(xnT_ps, 1)
                pe.wait_ge(ao_ready, b * TILES)
                for t in range(TILES):
                    pe.wait_ge(xnT_ready, b * TILES + t + 1)
                    if t >= 2:
                        pe.wait_ge(rest_ready, b * TILES + t - 1)
                        pe.wait_ge(v_ready, b * TILES + t - 1)
                    for c in range(KC):
                        mm(ps[:, 4 + t % 2, :], xnT[:, c, t * P:(t + 1) * P], wqk_s[:, c, :], start=(c == 0), stop=(c == KC - 1))
                    for c in range(KC):
                        last = mm(ps[:, 6 + t % 2, 0:256], xnT[:, c, t * P:(t + 1) * P], wv_s[:, c, :], start=(c == 0), stop=(c == KC - 1))
                    last.then_inc(proj_ps, 1)
                pe.wait_ge(v_ready, b * TILES + TILES)
                for t in range(TILES):
                    last = mm(ps[0:TILES, 0, :], tones_s[:, t, :], vals[:, t].rearrange("p h d -> p (h d)"),
                              start=(t == 0), stop=(t == TILES - 1))
                last.then_inc(bsum_ps, 1)
                pe.wait_ge(copies, 2 * TILES * (b + 1))
                pe.wait_ge(bsum_ready, b + 1)
                for g in range(GROUPS):
                    if g >= 1:
                        pe.wait_ge(rden_ready, b * GROUPS + g)
                    for h in range(GH):
                        for a in range(2):
                            u = 2 * h + a
                            if u == 6:
                                pe.wait_ge(qT_ready, (b * GROUPS + g) * GH + 1)
                            if u == 7:
                                pe.wait_ge(kT_ready, (b * GROUPS + g) * GH + 1)
                            for t in range(TILES):
                                last = nc.tensor.transpose(ps[0:SW, 2 + u % 6, :].bitcast(BF16)[:, t * P:(t + 1) * P],
                                                           parts[:, t, a, g * GH + h].rearrange("p s d -> p (s d)"), idb_s[:, :])
                            last.then_inc(qkT_ps, 1)
                    if g >= 1:
                        pe.wait_ge(yT_ready, b * GROUPS + g)
                    for half in range(2):
                        mm(ps[:, half, :], bsum[:, g * P:(g + 1) * P], steps_s[:, half * 512:(half + 1) * 512],
                           start=True, stop=False, skip_group_check=True)
                    pe.wait_ge(qT_ready, (b * GROUPS + g) * GH + GH)
                    pe.wait_ge(kT_ready, (b * GROUPS + g) * GH + GH)

                    def scores(u):
                        j, half, c = STEPS[u // 2]
                        if u >= 3:
                            pe.wait_ge(squared, (b * GROUPS + g) * 2 * NS + u - 2)
                        for k in range(2):
                            h = 2 * (u % 2) + k
                            last = mm(ps[:, 2 + 2 * (u % 3) + k, c:512], qkT[:, 1, h, j * P:(j + 1) * P],
                                      qkT[:, 0, h, half * 512 + c:(half + 1) * 512], start=True, stop=True)
                        last.then_inc(score_ps, 1)

                    for u in range(3):
                        scores(u)
                    for i, (j, half, c) in enumerate(STEPS):
                        pe.wait_ge(squared, (b * GROUPS + g) * 2 * NS + 2 * i + 2)
                        if i in diag_no:
                            pe.wait_ge(diag, (b * GROUPS + g) * NDIAG + 2 * diag_no[i] + 2)
                        for h in range(GH):
                            last = mm(ps[h * VP:(h + 1) * VP, half, c:512], vals[:, j, g * GH + h, :],
                                      weights[:, (2 * i + h // 2) % 4, h % 2, c:512], start=False, stop=(j == 4 * half + 3),
                                      skip_group_check=True)
                        last.then_inc(pv_done, 1)
                        for u in (2 * i + 3, 2 * i + 4):
                            if u < 2 * NS:
                                scores(u)
                    pe.wait_ge(yT_ready, b * GROUPS + g + 1)
                    for half in range(2):
                        last = mm(ps[:, 2 + half, :], denr_s[:, :], yT[:, g, half * 512:(half + 1) * 512], start=True, stop=True)
                    last.then_inc(den_ps, 1)
                pe.wait_ge(y_ready, b * GROUPS + GROUPS)
                for t in range(TILES):
                    if t >= 2:
                        pe.wait_ge(ao_ready, b * TILES + t - 1)
                    for g in range(GROUPS):
                        last = mm(ps[:, 4 + t % 2, 0:DIM], yT[:, g, t * P:(t + 1) * P], wo_s[:, g, :], start=(g == 0), stop=(g == GROUPS - 1))
                    last.then_inc(ao_ps, 1)


def taylor_constants():
    k = np.arange(P)
    q = np.arange(SEQ)
    t = np.arange(TILES)
    causal = (k[:, None] <= k[None, :]).astype(np.float32)
    steps = (q[None, :] // P > t[:, None]).astype(np.float32)
    ones = np.zeros((P, TILES, TILES), np.float32)
    ones[:, t, t] = 1.0
    den = (k[:, None] == k[None, :] // VP * VP + TD).astype(np.float32)
    eps = np.where(k % VP == TD, TEPS2, 0.0).astype(np.float32)[:, None]
    return causal, steps, ones, den, eps


def transformer_block(nc, PAIRS, x, xn_d, attn_d, wqkv, wo, w1, b1, w2, ln, qk_scale, rotary, masks, ident, shift,
                      carry_row, out):
    with ExitStack() as ctx:
        def sb(name, shape, dt=F32):
            return ctx.enter_context(nc.sbuf_tensor(name, shape, dt))

        def sem(name):
            return ctx.enter_context(nc.semaphore("f_" + name))

        def sems(name):
            return [sem(f"{name}{s}") for s in range(2)]

        ps = ctx.enter_context(nc.psum_tensor("f_ps", [P, 8, 512], F32))

        def bank(s, i):
            return ps[:, 4 * s + i, :]

        wqkv_s = sb("wqkv_s", [P, LAYERS, KC, 3 * INNER])
        wo_s = sb("fwo_s", [P, LAYERS, INNER // P, DIM])
        w1_s = sb("w1_s", [P, LAYERS, KC, 2, HID])
        b1_s = sb("b1_s", [P, LAYERS, 2, FB])
        w2_s = sb("w2_s", [P, LAYERS, FB, DIM])
        ln_s = sb("ln_s", [P, LAYERS, 2, KC])
        qks_s = sb("qks_s", [P, LAYERS, 2, 2, HD])
        id_s = sb("f_id", [P, P])
        shift_s = sb("shift_s", [P, P])
        carry_s = sb("carry_s", [P, P])
        rot = sb("rot", [P, TILES, LAYERS, 2, 2, HD])
        masks_s = sb("masks_s", [P, TILES, 2 * P + 1])
        mhalf = sb("f_mhalf", [P, 2 * HEADS])

        def each(name, shape):
            return [[sb(f"{name}{s}{l}", shape) for l in range(LAYERS)] for s in range(2)]

        def both(name, shape):
            return [sb(f"{name}{s}", shape) for s in range(2)]

        mask = both("mask", [P, 2 * P + 1])
        xin = both("xin", [P, DIM])
        xres = both("xres", [P, 2, DIM])
        hT = each("hT", [P, 1 + 2 * P])
        kT = each("kT", [P, HEADS // 2, 2 * P])
        vw = each("vw", [P, 2, INNER])
        x1 = each("x1", [P, DIM])
        xmid = both("xmid", [P, DIM])
        yout = both("yout", [P, DIM])
        carry = each("carry", [P, P])
        qk = both("qk", [P, 2 * HEADS, HD])
        work = both("work", [P, 2, 2 * HEADS, HD])
        sq = [work[s][:, 0] for s in range(2)]
        turned = [work[s][:, 1] for s in range(2)]
        pT = [work[s][:, :, :, :].rearrange("p a h d -> p (a h d)").rearrange("p (i n) -> p i n", n=P) for s in range(2)]
        ssq = both("ssq", [P, 2 * HEADS])
        rnorm = both("rnorm", [P, 2 * HEADS])
        qT = both("qT", [P, HEADS // 2, P])
        pr = both("pr", [P, HEADS, 2 * P])
        tab = pr[0][:, :, :].rearrange("p t (a b d) -> p t a b d", a=2, b=2)
        nmax = both("nmax", [P, HEADS])
        psum = both("psum", [P, HEADS])
        rsum = both("rsum", [P, HEADS])
        oT = both("oT", [P, INNER // P, P])
        st = both("st", [P, 2, 6])
        mv = both("mv", [P, 2])
        ve = both("ve", [P, 1])
        rstd = both("rstd", [P, 1])
        hn = [qk[s][:, :, :].rearrange("p h d -> p (h d)")[:, FB * P:FB * P + DIM] for s in range(2)]
        hnT = both("hnT", [P, KC, P])
        gate = [qk[s][:, :, :].rearrange("p h d -> p (h d)")[:, 0:FB * P].rearrange("p (j n) -> p j n", n=P) for s in range(2)]
        act_u = both("act_u", [P, FB, P])
        xb = both("xb", [P, DIM])

        const_in = sem("const_in")
        init = sem("init")
        x_in = sems("x_in")
        y_out = sems("y_out")
        mask_set = sems("mask_set")
        kept = sems("kept")
        xT_ps = sems("xT_ps")
        edge = sems("edge")
        hT_ready = sems("hT_ready")
        qkv_ps = sems("qkv_ps")
        qk_ready = sems("qk_ready")
        v_ready = sems("v_ready")
        sq_ready = sems("sq_ready")
        ssq_sum = sems("ssq_sum")
        ssq_ready = sems("ssq_ready")
        rnorm_ready = sems("rnorm_ready")
        unit = sems("unit")
        turn = sems("turn")
        cosd = sems("cosd")
        rotated = sems("rotated")
        qkT_ps = sems("qkT_ps")
        qT_ready = sems("qT_ready")
        kT_ready = sems("kT_ready")
        score_ps = sems("score_ps")
        masked = sems("masked")
        nmax_ready = sems("nmax_ready")
        exped = sems("exped")
        rsum_ready = sems("rsum_ready")
        prob = sems("prob")
        pT_ps = sems("pT_ps")
        pT_act = sems("pT_act")
        pT_dve = sems("pT_dve")
        oT_ps = sems("oT_ps")
        oT_ready = sems("oT_ready")
        wo_ps = sems("wo_ps")
        x1_ready = sems("x1_ready")
        shift_ps = sems("shift_ps")
        stat1 = sems("stat1")
        stat2 = sems("stat2")
        var_ready = sems("var_ready")
        rstd_ready = sems("rstd_ready")
        hn_ready = sems("hn_ready")
        hnT_ps = sems("hnT_ps")
        hnT_ready = sems("hnT_ready")
        up_ps = sems("up_ps")
        gate_ready = sems("gate_ready")
        u_ready = sems("u_ready")
        xb_ready = sems("xb_ready")
        res_ready = sems("res_ready")
        down_ps = sems("down_ps")
        x2_ready = sems("x2_ready")
        passed_pool = sem("passed_pool")
        passed_dve = sem("passed_dve")

        consts = [(wqkv_s[:, :, :, :], wqkv), (wo_s[:, :, :, :], wo), (w1_s[:, :, :, :, :], w1), (b1_s[:, :, :, :], b1),
                  (w2_s[:, :, :, :], w2), (ln_s[:, :, :, :], ln), (qks_s[:, :, :, :, :], qk_scale.partition_broadcast(P)),
                  (tab[:, :, :, :, :], rotary), (masks_s[:, :, :], masks), (id_s[:, :], ident), (shift_s[:, :], shift),
                  (carry_s[:, :], carry_row)]
        CONST_IN = 16 * len(consts)
        N_TAB = TILES * LAYERS
        INIT_ZERO = 2 + 8 * LAYERS
        INIT = INIT_ZERO + N_TAB

        STREAMS = range(2)
        block = ctx.enter_context(nc.Block())

        @block.sync
        def _(sp):
            for dst, src in consts:
                sp.dma_start(dst, src).then_inc(const_in, 16)
            with sp.Fori(0, PAIRS) as b:
                with sp.Fori(0, TILES) as t:
                    it = b * TILES + t
                    for s in STREAMS:
                        row = bass.ds(t * P, P)
                        sp.wait_ge(x1_ready[s], LAYERS * it)
                        sp.dma_start(xin[s][:, :], xn_d[b + s * PAIRS, row, :]).then_inc(x_in[s], 16)
                        sp.wait_ge(xb_ready[s], it)
                        sp.dma_start(xres[s][:, 0, :], x[b + s * PAIRS, row, :]).then_inc(x_in[s], 16)
                        sp.dma_start(xres[s][:, 1, :], attn_d[b + s * PAIRS, row, :]).then_inc(x_in[s], 16)
                    for s in STREAMS:
                        row = bass.ds(t * P, P)
                        sp.wait_ge(x2_ready[s], LAYERS * it + LAYERS)
                        sp.dma_start(out[b + s * PAIRS, row, :], yout[s][:, :]).then_inc(y_out[s], 16)
            for s in STREAMS:
                sp.wait_ge(y_out[s], 16 * PAIRS * TILES)

        @block.gpsimd
        def _(pool):
            g = nc.gpsimd
            g.memset(mhalf[:, :], -0.5).then_inc(init, 1)
            pool.wait_ge(const_in, CONST_IN)
            for l in range(LAYERS):
                for s in STREAMS:
                    g.memset(hT[s][l][:, :], 0.0).then_inc(init, 1)
                    g.memset(kT[s][l][:, :, :], 0.0).then_inc(init, 1)
                    g.memset(vw[s][l][:, :, :], 0.0).then_inc(init, 1)
                    g.memset(x1[s][l][:, :], 0.0).then_inc(init, 1)
            for s in STREAMS:
                g.memset(act_u[s][:, FB - 1, :], 1.0).then_inc(init, 1)
            pool.wait_ge(init, INIT_ZERO + 1)
            for t in range(TILES):
                for l in range(LAYERS):
                    g.tensor_tensor(rot[:, t, l].rearrange("p a b d -> p (a b d)"), tab[:, t].rearrange("p a b d -> p (a b d)"),
                                    qks_s[:, l].rearrange("p a b d -> p (a b d)"), ALU.mult).then_inc(init, 1)
            pool.wait_ge(init, INIT + 1)
            with pool.Fori(0, PAIRS) as b:
                with pool.Fori(0, TILES) as t:
                    it = b * TILES + t
                    for l in range(LAYERS):
                        n = it * LAYERS + l
                        for s in STREAMS:
                            pool.wait_ge(mask_set[s], it + 1)
                            pool.wait_ge(shift_ps[s], n)
                            pool.sem_inc(passed_pool, 1)
                            g.tensor_copy(kT[s][l][:, :, 0:P], kT[s][l][:, :, P:2 * P]).then_inc(kept[s], 1)
                            g.tensor_copy(vw[s][l][:, 0, :], vw[s][l][:, 1, :]).then_inc(kept[s], 1)
                            g.tensor_scalar(carry[s][l][:, :], x1[s][l][:, P:DIM], mask[s][:, 2 * P:2 * P + 1], None,
                                            ALU.mult).then_inc(kept[s], 1)
                        for s in STREAMS:
                            pool.wait_ge(ssq_ready[s], n + 1)
                            g.tensor_tensor(rnorm[s][:, :], ssq[s][:, :], mhalf[:, :], ALU.pow).then_inc(rnorm_ready[s], 1)
                        for s in STREAMS:
                            pool.wait_ge(unit[s], n + 1)
                            pool.sem_inc(passed_pool, 1)
                            for half in range(2):
                                a, z = slice(half * 32, half * 32 + 32), slice(32 - half * 32, 64 - half * 32)
                                sines = rot[:, bass.ds(t, 1), l, 1, :, a].rearrange("p o a d -> p (o a) d")
                                g.tensor_tensor(turned[s][:, :, a].rearrange("p (a h) d -> p a h d", a=2),
                                                qk[s][:, :, z].rearrange("p (a h) d -> p a h d", a=2),
                                                sines.unsqueeze(2).to_broadcast([P, 2, HEADS, 32]), ALU.mult).then_inc(turn[s], 1)
                        for s in STREAMS:
                            pool.wait_ge(var_ready[s], n + 1)
                            g.tensor_tensor(rstd[s][:, :], ve[s][:, :], mhalf[:, 0:1], ALU.pow).then_inc(rstd_ready[s], 1)
                        if l == LAYERS - 1:
                            for s in STREAMS:
                                pool.wait_ge(x_in[s], 48 * it + 48)
                                g.tensor_tensor(xres[s][:, 0, :], xres[s][:, 0, :], xres[s][:, 1, :], ALU.add).then_inc(res_ready[s], 1)
                                pool.wait_ge(res_ready[s], it + 1)
                                pool.wait_ge(x1_ready[s], n + 1)
                                g.tensor_tensor(xb[s][:, :], xres[s][:, 0, :], x1[s][l][:, :], ALU.add).then_inc(xb_ready[s], 1)

        @block.vector
        def _(dve):
            v = nc.vector
            dve.wait_ge(const_in, CONST_IN)
            dve.wait_ge(init, INIT + 1)
            with dve.Fori(0, PAIRS) as b:
                with dve.Fori(0, TILES) as t:
                    it = b * TILES + t
                    for s in STREAMS:
                        dve.wait_ge(kept[s], 3 * LAYERS * it)
                        dve.sem_inc(passed_dve, 1)
                        v.tensor_copy(mask[s][:, :], masks_s[:, bass.ds(t, 1), :].rearrange("p o n -> p (o n)")).then_inc(mask_set[s], 1)
                    for l in range(LAYERS):
                        n = it * LAYERS + l
                        for s in STREAMS:
                            dve.wait_ge(sq_ready[s], n + 1)
                            v.reduce_sum(ssq[s][:, :], sq[s][:, :, :], AX).then_inc(ssq_sum[s], 1)
                            dve.wait_ge(ssq_sum[s], n + 1)
                            v.tensor_scalar_max(ssq[s][:, :], ssq[s][:, :], 1e-24).then_inc(ssq_ready[s], 1)
                        for s in STREAMS:
                            dve.wait_ge(rnorm_ready[s], n + 1)
                            v.tensor_tensor(qk[s][:, :, :], qk[s][:, :, :], rnorm[s][:, :].unsqueeze(2).to_broadcast([P, 2 * HEADS, HD]),
                                            ALU.mult).then_inc(unit[s], 1)
                        for s in STREAMS:
                            cosines = rot[:, bass.ds(t, 1), l, 0, :, :].rearrange("p o a d -> p (o a) d")
                            dve.wait_ge(unit[s], n + 1)
                            v.tensor_tensor(sq[s][:, :, :].rearrange("p (a h) d -> p a h d", a=2), qk[s][:, :, :].rearrange("p (a h) d -> p a h d", a=2),
                                            cosines.unsqueeze(2).to_broadcast([P, 2, HEADS, HD]), ALU.mult).then_inc(cosd[s], 1)
                        for s in STREAMS:
                            dve.wait_ge(cosd[s], n + 1)
                            dve.wait_ge(turn[s], 2 * n + 2)
                            v.tensor_tensor(qk[s][:, :, :], sq[s][:, :, :], turned[s][:, :, :], ALU.add).then_inc(rotated[s], 1)
                        for s in STREAMS:
                            for h in range(HEADS + 1):
                                if h < HEADS:
                                    sc = bank(s, 2 * (h % 2) + h // 4)[:, (h // 2 % 2) * 256:(h // 2 % 2) * 256 + 256]
                                    if h % 4 == 0:
                                        dve.wait_ge(score_ps[s], n * 2 + h // 4 + 1)
                                        dve.sem_inc(passed_dve, 1)
                                    v.tensor_tensor_reduce(out=pr[s][:, h, :], in0=sc, in1=mask[s][:, 0:2 * P], scale=1.0, scalar=-3.0e38,
                                                           op0=ALU.add, op1=ALU.max, accum_out=nmax[s][:, h:h + 1]).then_inc(masked[s], 1)
                                if h >= 1:
                                    dve.wait_ge(masked[s], n * HEADS + h)
                                    v.tensor_scalar_mul(nmax[s][:, h - 1:h], nmax[s][:, h - 1:h], -1.0).then_inc(nmax_ready[s], 1)
                        for s in STREAMS:
                            for h in range(HEADS):
                                dve.wait_ge(exped[s], n * HEADS + h + 1)
                                v.reciprocal(rsum[s][:, h:h + 1], psum[s][:, h:h + 1]).then_inc(rsum_ready[s], 1)
                                dve.wait_ge(rsum_ready[s], n * HEADS + h + 1)
                                v.tensor_scalar_mul(pr[s][:, h, :], pr[s][:, h, :], rsum[s][:, h:h + 1]).then_inc(prob[s], 1)
                        for s in STREAMS:
                            for i in range(2, 4):
                                dve.wait_ge(pT_ps[s], n * 4 + i + 1)
                                v.tensor_copy(pT[s][:, 4 * i:4 * i + 4, :].rearrange("p a n -> p (a n)"), bank(s, i)).then_inc(pT_dve[s], 1)
                        for s in STREAMS:
                            if l == 0:
                                dve.wait_ge(x_in[s], 48 * it + 48)
                            dve.wait_ge(wo_ps[s], n + 1)
                            dve.wait_ge(kept[s], 3 * n + 3)
                            xprev = xin[s] if l == 0 else xmid[s]
                            v.tensor_tensor(x1[s][l][:, :], bank(s, 1)[:, 0:DIM], xprev[:, :], ALU.add).then_inc(x1_ready[s], 1)
                        for s in STREAMS:
                            dve.wait_ge(x1_ready[s], n + 1)
                            v.bn_stats(st[s][:, 0, :], x1[s][l][:, 0:P])
                            dve.wait_ge(shift_ps[s], n + 1)
                            v.bn_stats(st[s][:, 1, :], bank(s, 2)[:, 0:P]).then_inc(stat1[s], 1)
                            dve.wait_ge(stat1[s], n + 1)
                            dve.sem_inc(passed_dve, 1)
                            v.bn_aggr(mv[s][:, :], st[s][:, :, :].rearrange("p a n -> p (a n)")).then_inc(stat2[s], 1)
                            dve.wait_ge(stat2[s], n + 1)
                            v.tensor_scalar_add(ve[s][:, :], mv[s][:, 1:2], LN_EPS).then_inc(var_ready[s], 1)
                        for s in STREAMS:
                            dve.wait_ge(rstd_ready[s], n + 1)
                            v.tensor_scalar(hn[s][:, 0:P], x1[s][l][:, 0:P], mv[s][:, 0:1], rstd[s][:, :], ALU.subtract, ALU.mult)
                            v.tensor_scalar(hn[s][:, P:DIM], bank(s, 2)[:, 0:P], mv[s][:, 0:1], rstd[s][:, :], ALU.subtract, ALU.mult)\
                                .then_inc(hn_ready[s], 1)
                        for s in STREAMS:
                            dve.wait_ge(hnT_ps[s], n + 1)
                            for c in range(KC):
                                last = v.tensor_scalar(hnT[s][:, c, :], bank(s, 3)[:, c * P:(c + 1) * P], ln_s[:, l, 0, c:c + 1],
                                                       ln_s[:, l, 1, c:c + 1], ALU.mult, ALU.add)
                            last.then_inc(hnT_ready[s], 1)
                        for s in STREAMS:
                            for j in range(FB):
                                rows = P if j < FB - 1 else FLAST
                                dve.wait_ge(gate_ready[s], n * FB + j // 2 * 2 + 2)
                                v.scalar_tensor_tensor(act_u[s][0:rows, j, :], bank(s, j // 2)[0:rows, (j % 2) * 256:(j % 2) * 256 + P],
                                                       b1_s[0:rows, l, 0, j:j + 1], gate[s][0:rows, j, :], ALU.add, ALU.mult).then_inc(u_ready[s], 1)
                        for s in STREAMS:
                            dve.wait_ge(down_ps[s], n + 1)
                            if l == 0:
                                v.tensor_tensor(xmid[s][:, :], bank(s, 3)[:, 0:DIM], x1[s][l][:, :], ALU.add).then_inc(x2_ready[s], 1)
                            else:
                                dve.wait_ge(xb_ready[s], it + 1)
                                dve.wait_ge(y_out[s], 16 * it)
                                v.tensor_tensor(yout[s][:, :], bank(s, 3)[:, 0:DIM], xb[s][:, :], ALU.add).then_inc(x2_ready[s], 1)

        @block.scalar
        def _(act):
            a = nc.scalar
            act.wait_ge(const_in, CONST_IN)
            act.wait_ge(init, INIT + 1)
            with act.Fori(0, PAIRS * TILES) as it:
                for l in range(LAYERS):
                    n = it * LAYERS + l
                    for s in STREAMS:
                        if l == 0:
                            act.wait_ge(mask_set[s], it + 1)
                        act.wait_ge(xT_ps[s], n + 1)
                        a.activation(hT[s][l][:, 0:1], hT[s][l][:, P:P + 1], ACT.Copy, scale=mask[s][:, 2 * P:2 * P + 1]).then_inc(edge[s], 1)
                        act.wait_ge(edge[s], n + 1)
                        a.activation(hT[s][l][:, 1:1 + 2 * P], bank(s, 3)[:, 0:2 * P], ACT.Copy).then_inc(hT_ready[s], 1)
                    for s in STREAMS:
                        act.wait_ge(qkv_ps[s], n + 1)
                        a.activation(qk[s][:, :, :].rearrange("p h d -> p (h d)"), ps[:, 4 * s:4 * s + 2, :].rearrange("p a n -> p (a n)"),
                                     ACT.Copy).then_inc(qk_ready[s], 1)
                        act.wait_ge(kept[s], 3 * n + 3)
                        a.activation(vw[s][l][:, 1, :], bank(s, 2), ACT.Copy).then_inc(v_ready[s], 1)
                        act.wait_ge(qk_ready[s], n + 1)
                        a.activation(sq[s][:, :, :], qk[s][:, :, :], ACT.Square).then_inc(sq_ready[s], 1)
                    for s in STREAMS:
                        act.wait_ge(qkT_ps[s], n + 1)
                        a.activation(qT[s][:, :, :], bank(s, 3).rearrange("p (c n) -> p c n", n=P), ACT.Copy).then_inc(qT_ready[s], 1)
                        a.activation(kT[s][l][:, :, P:2 * P], bank(s, 0).rearrange("p (c n) -> p c n", n=P), ACT.Copy).then_inc(kT_ready[s], 1)
                    for s in STREAMS:
                        for h in range(HEADS):
                            act.wait_ge(nmax_ready[s], n * HEADS + h + 1)
                            a.activation(pr[s][:, h, :], pr[s][:, h, :], ACT.Exp, bias=nmax[s][:, h:h + 1],
                                         accum_out=psum[s][:, h:h + 1]).then_inc(exped[s], 1)
                    for s in STREAMS:
                        for i in range(2):
                            act.wait_ge(pT_ps[s], n * 4 + i + 1)
                            a.activation(pT[s][:, 4 * i:4 * i + 4, :].rearrange("p a n -> p (a n)"), bank(s, i), ACT.Copy).then_inc(pT_act[s], 1)
                    for s in STREAMS:
                        act.wait_ge(oT_ps[s], n + 1)
                        a.activation(oT[s][:, :, :].rearrange("p a n -> p (a n)"), bank(s, 0), ACT.Copy).then_inc(oT_ready[s], 1)
                    for s in STREAMS:
                        for j in range(FB):
                            rows = P if j < FB - 1 else FLAST
                            act.wait_ge(up_ps[s], n * 3 + j // 2 + 1)
                            a.activation(gate[s][0:rows, j, :], bank(s, j // 2)[0:rows, (j % 2) * 256 + P:(j % 2) * 256 + 2 * P], ACT.Gelu,
                                         bias=b1_s[0:rows, l, 1, j:j + 1]).then_inc(gate_ready[s], 1)

        @block.tensor
        def _(pe):
            mm, tr = nc.tensor.matmul, nc.tensor.transpose
            pe.wait_ge(const_in, CONST_IN)
            pe.wait_ge(init, INIT + 1)
            with pe.Fori(0, PAIRS * TILES) as it:
                for l in range(LAYERS):
                    n = it * LAYERS + l
                    for s in STREAMS:
                        if l == 0:
                            pe.wait_ge(x_in[s], 48 * it + 48)
                            pe.wait_ge(x2_ready[s], n)
                        else:
                            pe.wait_ge(x2_ready[s], n)
                        xprev = xin[s] if l == 0 else xmid[s]
                        tr(bank(s, 3)[:, 0:P], xprev[:, P:DIM], id_s[:, :])
                        tr(bank(s, 3)[:, P:2 * P], xprev[:, 0:P], id_s[:, :]).then_inc(xT_ps[s], 1)
                    for s in STREAMS:
                        pe.wait_ge(hT_ready[s], n + 1)
                        for i in range(3):
                            mm(bank(s, i), hT[s][l][:, P + 1:2 * P + 1], wqkv_s[:, l, 0, i * INNER:(i + 1) * INNER], start=True, stop=False)
                            last = mm(bank(s, i), hT[s][l][:, 0:P], wqkv_s[:, l, 1, i * INNER:(i + 1) * INNER], start=False, stop=True)
                        last.then_inc(qkv_ps[s], 1)
                    for s in STREAMS:
                        pe.wait_ge(rotated[s], n + 1)
                        for i in range(HEADS):
                            last = tr(bank(s, 3 if i < 4 else 0)[:, (i % 4) * P:(i % 4 + 1) * P],
                                      qk[s][:, 2 * i:2 * i + 2, :].rearrange("p h d -> p (h d)"), id_s[:, :])
                        last.then_inc(qkT_ps[s], 1)
                    for s in STREAMS:
                        pe.wait_ge(qT_ready[s], n + 1)
                        pe.wait_ge(kT_ready[s], n + 1)
                        pe.wait_ge(v_ready[s], n + 1)
                        for h in range(HEADS):
                            r = slice(h % 2 * HD, h % 2 * HD + HD)
                            last = mm(bank(s, 2 * (h % 2) + h // 4)[:, (h // 2 % 2) * 256:(h // 2 % 2) * 256 + 256], qT[s][r, h // 2, :],
                                      kT[s][l][r, h // 2, :], start=True, stop=True)
                            if h % 4 == 3:
                                last.then_inc(score_ps[s], 1)
                    for s in STREAMS:
                        pe.wait_ge(masked[s], n * HEADS + HEADS)
                        for h in range(HEADS):
                            pe.wait_ge(prob[s], n * HEADS + h + 1)
                            for half in range(2):
                                i = 2 * h + half
                                last = tr(bank(s, i // 4)[:, (i % 4) * P:(i % 4 + 1) * P], pr[s][:, h, half * P:(half + 1) * P], id_s[:, :])
                            if h % 2:
                                last.then_inc(pT_ps[s], 1)
                    for s in STREAMS:
                        for i in range(HEADS // 2):
                            if i < 2:
                                pe.wait_ge(pT_act[s], n * 2 + i + 1)
                            else:
                                pe.wait_ge(pT_dve[s], n * 2 + i - 1)
                            for half in range(2):
                                for k in range(2):
                                    h = 2 * i + k
                                    last = mm(bank(s, 0)[k * HD:(k + 1) * HD, i * P:(i + 1) * P], vw[s][l][:, half, h * HD:(h + 1) * HD],
                                              pT[s][:, 2 * h + half, :], start=(half == 0), stop=(half == 1))
                        last.then_inc(oT_ps[s], 1)
                    for s in STREAMS:
                        pe.wait_ge(oT_ready[s], n + 1)
                        for c in range(INNER // P):
                            last = mm(bank(s, 1)[:, 0:DIM], oT[s][:, c, :], wo_s[:, l, c, :], start=(c == 0), stop=(c == INNER // P - 1))
                        last.then_inc(wo_ps[s], 1)
                    for s in STREAMS:
                        pe.wait_ge(x1_ready[s], n + 1)
                        pe.wait_ge(kept[s], 3 * n + 3)
                        mm(bank(s, 2)[:, 0:P], shift_s[:, :], x1[s][l][:, P:DIM], start=True, stop=False)
                        mm(bank(s, 2)[:, 0:P], carry_s[96:P, :], carry[s][l][96:P, :], start=False, stop=True).then_inc(shift_ps[s], 1)
                    for s in STREAMS:
                        pe.wait_ge(hn_ready[s], n + 1)
                        for c in range(KC):
                            last = tr(bank(s, 3)[:, c * P:(c + 1) * P], hn[s][:, c * P:(c + 1) * P], id_s[:, :])
                        last.then_inc(hnT_ps[s], 1)
                    for s in STREAMS:
                        pe.wait_ge(hnT_ready[s], n + 1)
                        for j in range(FB):
                            rows = P if j < FB - 1 else FLAST
                            for half in range(2):
                                o = (j % 2) * 256 + half * P
                                for c in range(KC):
                                    last = mm(bank(s, j // 2)[0:rows, o:o + P], w1_s[:, l, c, half, j * P:j * P + rows], hnT[s][:, c, :],
                                              start=(c == 0), stop=(c == KC - 1))
                            if j % 2:
                                last.then_inc(up_ps[s], 1)
                    for s in STREAMS:
                        for j in range(FB):
                            rows = P if j < FB - 1 else FLAST + 1
                            pe.wait_ge(u_ready[s], n * FB + j + 1)
                            last = mm(bank(s, 3)[:, 0:DIM], act_u[s][0:rows, j, :], w2_s[0:rows, l, j, :], start=(j == 0), stop=(j == FB - 1))
                        last.then_inc(down_ps[s], 1)


def transformer_constants():
    half = np.arange(0, HD, 2, dtype=np.float32)
    inv_freq = (1.0 / np.float32(10000.0) ** (half / np.float32(HD))).astype(np.float32)
    t = np.arange(SEQ, dtype=np.float32)
    freqs = np.concatenate([t[:, None] * inv_freq] * 2, 1)
    base = (half + np.float32(0.4 * HD)) / np.float32(1.4 * HD)
    power = (t - SEQ // 2) / np.float32(P // 2)
    scale = np.concatenate([base[None, :] ** power[:, None]] * 2, 1).astype(np.float32)
    cos, sin = np.cos(freqs), np.sin(freqs)
    sign = np.where(np.arange(HD) < HD // 2, -1.0, 1.0).astype(np.float32)
    tab = np.stack([np.stack([8 * cos * scale, cos / scale]), np.stack([8 * sign * sin * scale, sign * sin / scale])])
    tab = tab.reshape(2, 2, TILES, P, HD).transpose(3, 2, 0, 1, 4).astype(np.float32)
    i, j = np.arange(P)[:, None], np.arange(2 * P)[None, :] - P
    masks = np.zeros((P, TILES, 2 * P + 1), np.float32)
    masks[:, :, :2 * P] = np.where((i < j) | (i > j + P), -3e38, 0.0)[:, None, :]
    masks[:, 0, :P] = -3e38
    masks[:, 1:, 2 * P] = 1.0
    shift = np.eye(P, k=1, dtype=np.float32)
    carry = np.zeros((P, P), np.float32)
    carry[P - 1, 0] = 1.0
    return tab, masks, shift, carry


def chunked(w):
    return w.reshape(-1, P, w.shape[-1]).transpose(1, 0, 2)


def kernel(**inputs):
    import ml_dtypes
    import concourse.bacc as _bacc
    from concourse.bass_utils import run_bass_kernel_spmd as _run

    a = {k: np.asarray(v) for k, v in inputs.items()}
    x = a["L0_attn_hidden_states"]
    B = x.shape[0]
    f = {k[len("L0_ffn_"):]: v for k, v in a.items() if k.startswith("L0_ffn_")}

    two = np.zeros((TH, VP, DIM), np.float32)
    two[:, :TD] = a["L0_attn_Wo"].T.reshape(TH, TD, DIM)
    b1 = np.zeros((LAYERS, 2, FB * P), np.float32)
    b1[..., :HID] = f["b1"].reshape(LAYERS, 2, HID)
    w2 = np.zeros((LAYERS, FB * P, DIM), np.float32)
    w2[:, :HID] = f["w2"]
    w2[:, HID] = f["b2"]
    ln = np.stack([f["ln_g"], f["ln_b"]], 1)
    scales = np.stack([f["q_scale"], f["k_scale"]], 1)
    scales = np.stack([scales, np.roll(scales, HD // 2, -1)], 1)

    arrays = {
        "x": x,
        "t_wqk": chunked(np.concatenate([a["L0_attn_Wq"].T, a["L0_attn_Wk"].T], 1)),
        "t_wv": chunked(a["L0_attn_Wv"].T),
        "t_wo": chunked(two.reshape(TH * VP, DIM)),
        "wqkv": f["wqkv"].reshape(LAYERS, KC, P, 3 * INNER).transpose(2, 0, 1, 3),
        "wo": f["wo"].reshape(LAYERS, INNER // P, P, DIM).transpose(2, 0, 1, 3),
        "w1": f["w1"].reshape(LAYERS, KC, P, 2, HID).transpose(2, 0, 1, 3, 4),
        "b1": b1.reshape(LAYERS, 2, FB, P).transpose(3, 0, 1, 2),
        "w2": w2.reshape(LAYERS, FB, P, DIM).transpose(2, 0, 1, 3),
        "ln": ln.reshape(LAYERS, 2, KC, P).transpose(3, 0, 1, 2),
        "scales": scales,
        "ident": np.eye(P, dtype=np.float32),
        "ident_bf": np.eye(P, dtype=np.float32).astype(ml_dtypes.bfloat16),
    }
    for name, c in zip(("causal", "steps", "tile_ones", "den_rows", "eps_rows"), taylor_constants()):
        arrays[name] = c
    for name, c in zip(("rotary", "masks", "shift", "carry_row"), transformer_constants()):
        arrays[name] = c
    arrays = {f"{k}_dram": np.ascontiguousarray(v) for k, v in arrays.items()}

    nc = _bacc.Bacc("TRN2", target_bir_lowering=False, num_devices=1)
    d = {k[:-5]: nc.dram_tensor(k, v.shape, mybir.dt.from_np(v.dtype), kind="ExternalInput").ap() for k, v in arrays.items()}
    out = nc.dram_tensor("out_dram", x.shape, F32, kind="ExternalOutput").ap()
    xn_d = nc.dram_tensor("xn_dram", x.shape, F32).ap()
    attn_d = nc.dram_tensor("attn_dram", x.shape, F32).ap()

    taylor_block(nc, B, d["x"], d["t_wqk"], d["t_wv"], d["t_wo"], d["ident"], d["ident_bf"], d["causal"], d["steps"],
                 d["tile_ones"], d["den_rows"], d["eps_rows"], xn_d, attn_d)
    transformer_block(nc, B // 2, d["x"], xn_d, attn_d, d["wqkv"], d["wo"], d["w1"], d["b1"], d["w2"], d["ln"], d["scales"],
                      d["rotary"], d["masks"], d["ident"], d["shift"], d["carry_row"], out)
    return _run(nc, [arrays], core_ids=[0]).results[0]["out_dram"]
```

```python
from contextlib import ExitStack

import numpy as np

import concourse.bass as bass
from concourse import mybir

F32 = mybir.dt.float32
BF16 = mybir.dt.bfloat16
ALU = mybir.AluOpType
ACT = mybir.ActivationFunctionType
AX = mybir.AxisListType.X

P = 128
DIM = 256
KC = DIM // P
TILES = 8
SEQ = P * TILES

TH, TD = 16, 16
GROUPS, GH = 4, 4
VP = 32
SLOTS = 6
SW = SLOTS * TD
TEPS2 = 2e-12

LAYERS, HEADS, HD = 2, 8, 64
INNER = HEADS * HD
HID = 682
FB = 6
FLAST = HID - (FB - 1) * P
LN_EPS = 1e-5


def taylor_block(nc, B, x, wqk, wv, wo, ident, ident_bf, causal, earlier, eps_rows, xn_d, attn_d):
    with ExitStack() as ctx:
        def sb(name, shape, dt=F32):
            return ctx.enter_context(nc.sbuf_tensor(name, shape, dt))

        def sem(name):
            return ctx.enter_context(nc.semaphore("t_" + name))

        ps = ctx.enter_context(nc.psum_tensor("t_ps", [P, 8, 512], F32))

        UNITS = 6
        wqk_s = sb("wqk_s", [P, KC, 512])
        wv_s = sb("wv_s", [P, KC, TH * TD])
        wo_s = sb("two_s", [P, GROUPS, DIM])
        id_s = sb("t_id", [P, P])
        idb_s = sb("t_idb", [P, P], BF16)
        causal_s = sb("causal_s", [P, P])
        earlier_s = sb("earlier_s", [TILES, TILES])
        eps_s = sb("eps_s", [P, 1])
        one_s = sb("one_s", [P, 1])
        mhalf = sb("mhalf", [P, TILES])
        xs = sb("xs", [P, TILES, DIM])
        xn = sb("xn", [P, TILES, DIM])
        xnT = sb("xnT", [P, KC, SEQ])
        xsum = sb("xsum", [P, KC, TILES])
        st = sb("t_st", [P, TILES, 6])
        mv = sb("t_mv", [P, TILES, 2])
        ve = sb("t_ve", [P, TILES])
        rstd = sb("t_rstd", [P, TILES])
        parts = sb("parts", [P, TILES, 2, TH, SLOTS, TD], BF16)
        rest = sb("rest", [P, 2, 2, TH, TD])
        vals = sb("vals", [P, TILES, TH, VP])
        qkT = sb("qkT", [SW, 2, GH, SEQ], BF16)
        weights = sb("weights", [P, UNITS * 2, 512])
        bsum = sb("bsum", [TILES, TH, VP])
        before = sb("before", [P, GROUPS, TILES])
        yT = sb("yT", [P, GROUPS, SEQ])
        den = sb("den", [P, SEQ])
        ao = sb("ao", [P, TILES, DIM])

        const_in = sem("const_in")
        ones_set = sem("ones_set")
        x_in = sem("x_in")
        stored = sem("stored")
        stats = sem("stats")
        var_ready = sem("var_ready")
        rstd_ready = sem("rstd_ready")
        xn_ready = sem("xn_ready")
        xnT_ps = sem("xnT_ps")
        xnT_ready = sem("xnT_ready")
        proj_ps = sem("proj_ps")
        high = sem("high")
        v_ready = sem("v_ready")
        rest_ready = sem("rest_ready")
        mid = sem("mid")
        low = sem("low")
        copies = sem("copies")
        xsum_ready = sem("xsum_ready")
        bsum_ps = sem("bsum_ps")
        bsum_ready = sem("bsum_ready")
        before_ps = sem("before_ps")
        before_ready = sem("before_ready")
        qkT_ps = sem("qkT_ps")
        kT_ready = sem("kT_ready")
        qkT_ready = sem("qkT_ready")
        score_ps = sem("score_ps")
        squared = sem("squared")
        diag = sem("diag")
        pv_done = sem("pv_done")
        yT_ready = sem("yT_ready")
        den_ready = sem("den_ready")
        rden_ready = sem("rden_ready")
        y_ready = sem("y_ready")
        ao_ps = sem("ao_ps")
        ao_ready = sem("ao_ready")
        passed_pool = sem("passed_pool")
        passed_dve = sem("passed_dve")

        consts = [(wqk_s[:, :, :], wqk), (wv_s[:, :, :], wv), (wo_s[:, :, :], wo), (id_s[:, :], ident),
                  (idb_s[:, :], ident_bf), (causal_s[:, :], causal), (earlier_s[:, :], earlier), (eps_s[:, :], eps_rows)]
        CONST_IN = 16 * len(consts)

        STEPS = [(j, h, max(0, P * j - 512 * h)) for j in range(TILES) for h in range(2) if P * j < 512 * (h + 1)]
        NS = len(STEPS)
        diag_no = {i: j for i, (j, h, c) in enumerate(STEPS) if j // 4 == h}
        HEAD_BANK = [2, 3, 4, 5, 6, 7, 4, 5]

        ACT_HEADS, DVE_HEADS = (1, 3), (0, 2, 4, 5, 6, 7)

        def unit_bank(u):
            return 2 + 2 * (u % 3)

        block = ctx.enter_context(nc.Block())

        @block.sync
        def _(sp):
            def load(b):
                sp.dma_start(xs[:, :, :], x[b].rearrange("(t p) d -> p t d", p=P)).then_inc(x_in, 16)

            def store_xn(b):
                sp.wait_ge(xn_ready, b * TILES + TILES)
                sp.dma_start(xn_d[b].rearrange("(t p) d -> p t d", p=P), xn[:, :, :]).then_inc(stored, 16)

            def store_attn(b):
                sp.wait_ge(ao_ready, b * TILES + TILES)
                sp.dma_start(attn_d[b].rearrange("(t p) d -> p t d", p=P), ao[:, :, :]).then_inc(stored, 16)

            load(0)
            for dst, src in consts:
                sp.dma_start(dst, src).then_inc(const_in, 16)
            store_xn(0)
            load(1)
            with sp.Fori(0, B - 2) as b:
                store_xn(b + 1)
                load(b + 2)
                store_attn(b)
            store_xn(B - 1)
            store_attn(B - 2)
            store_attn(B - 1)
            sp.wait_ge(stored, 2 * 16 * B)

        @block.gpsimd
        def _(pool):
            g = nc.gpsimd
            g.memset(mhalf[:, :], -0.5).then_inc(ones_set, 1)
            g.memset(one_s[:, :], 1.0).then_inc(ones_set, 1)
            g.memset(vals[:, :, :, TD:VP], 0.0).then_inc(ones_set, 1)
            g.memset(bsum[:, :, TD:VP], 0.0).then_inc(ones_set, 1)
            pool.wait_ge(ones_set, 4)
            g.memset(vals[:, :, :, TD:TD + 1], 1.0).then_inc(ones_set, 1)
            g.memset(bsum[:, :, TD:TD + 1], float(P)).then_inc(ones_set, 1)

            def root(b):
                pool.wait_ge(var_ready, b + 1)
                g.tensor_tensor(rstd[:, :], ve[:, :], mhalf[:, :], ALU.pow).then_inc(rstd_ready, 1)

            def split(b):
                for t in range(TILES):
                    r = rest[:, t % 2]
                    pool.wait_ge(rest_ready, b * TILES + t + 1)
                    pool.sem_inc(passed_pool, 1)
                    g.tensor_copy(parts[:, t, 0, :, 3:5, :], r[:, 0].unsqueeze(2).to_broadcast([P, TH, 2, TD])).then_inc(mid, 1)
                    g.tensor_copy(parts[:, t, 1, :, 1, :], r[:, 1]).then_inc(mid, 1)
                    pool.wait_ge(mid, 2 * (b * TILES + t + 1))
                    g.tensor_tensor(parts[:, t, 0, :, 5, :], r[:, 0], parts[:, t, 0, :, 3, :], ALU.subtract).then_inc(low, 1)
                    g.tensor_tensor(parts[:, t, 1, :, 2, :], r[:, 1], parts[:, t, 1, :, 1, :], ALU.subtract).then_inc(low, 1)

            root(0)
            split(0)
            with pool.Fori(0, B - 1) as b:
                root(b + 1)
                split(b + 1)

        @block.vector
        def _(dve):
            v = nc.vector

            def tile_stats(b, t):
                if t == 0:
                    dve.wait_ge(x_in, 16 * b + 16)
                v.bn_stats(st[:, t, :], xs[:, t, :]).then_inc(stats, 1)

            def variances(b):
                dve.wait_ge(stats, (TILES + 1) * b + TILES)
                dve.sem_inc(passed_dve, 1)
                for t in range(TILES):
                    last = v.bn_aggr(mv[:, t, :], st[:, t, :])
                last.then_inc(stats, 1)
                dve.wait_ge(stats, (TILES + 1) * b + TILES + 1)
                v.tensor_scalar_add(ve[:, :], mv[:, :, 1], LN_EPS).then_inc(var_ready, 1)

            def layer_norm(b, t):
                if t == 0:
                    dve.wait_ge(rstd_ready, b + 1)
                    if not isinstance(b, int):
                        dve.wait_ge(stored, 16 * (2 * b - 1))
                v.tensor_scalar(xn[:, t, :], xs[:, t, :], mv[:, t, 0:1], rstd[:, t:t + 1],
                                ALU.subtract, ALU.mult).then_inc(xn_ready, 1)

            def normalise(b, g, t):
                cols = slice(t * P, (t + 1) * P)
                i = (b * GROUPS + g) * TILES + t
                if t == 0:
                    dve.wait_ge(yT_ready, b * GROUPS + g + 1)
                else:
                    dve.wait_ge(y_ready, i)
                dve.sem_inc(passed_dve, 1)
                v.stream_shuffle(den[:, cols], yT[:, g, cols], [TD] * 32).then_inc(den_ready, 1)
                dve.wait_ge(den_ready, i + 1)
                v.reciprocal(den[:, cols], den[:, cols]).then_inc(rden_ready, 1)
                dve.wait_ge(rden_ready, i + 1)
                v.tensor_tensor(yT[:, g, cols], yT[:, g, cols], den[:, cols], ALU.mult).then_inc(y_ready, 1)

            def repeat_k(b, t):
                dve.wait_ge(low, 2 * (b * TILES + t + 1))
                v.tensor_copy(parts[:, t, 1, :, 3:5, :], parts[:, t, 1, :, 0:2, :]).then_inc(copies, 1)
                v.tensor_copy(parts[:, t, 1, :, 5, :], parts[:, t, 1, :, 0, :]).then_inc(copies, 1)

            def project(b, last=None):
                for t in range(TILES):
                    if last is not None:
                        normalise(last, GROUPS - 1, t)
                    dve.wait_ge(high, b * TILES + t + 1)
                    if t >= 2:
                        dve.wait_ge(low, 2 * (b * TILES + t - 1))
                    v.tensor_tensor(rest[:, t % 2], ps[:, 4 + t % 2, :].rearrange("p (a h d) -> p a h d", a=2, h=TH),
                                    parts[:, t, :, :, 0, :], ALU.subtract).then_inc(rest_ready, 1)
                    if t >= 2:
                        repeat_k(b, t - 2)
                dve.wait_ge(xnT_ready, b * TILES + TILES)
                v.reduce_sum(xsum[:, :, :], xnT[:, :, :].rearrange("p c (t n) -> p c t n", n=P), AX).then_inc(xsum_ready, 1)
                repeat_k(b, TILES - 2)
                repeat_k(b, TILES - 1)

            def attention(b, following):
                def copy_heads(g):
                    for u in DVE_HEADS:
                        dve.wait_ge(qkT_ps, (b * GROUPS + g) * 2 * GH + u + 1)
                        v.tensor_copy(qkT[:, u % 2, u // 2, :], ps[0:SW, HEAD_BANK[u], :].bitcast(BF16)).then_inc(qkT_ready, 1)

                copy_heads(0)
                for g in range(GROUPS):
                    for i, t in diag_no.items():
                        c = STEPS[i][2]
                        a = weights[:, 4 * i % (2 * UNITS):4 * i % (2 * UNITS) + GH, c:c + P]
                        dve.wait_ge(squared, (b * GROUPS + g) * 2 * NS + 2 * i + 2)
                        v.scalar_tensor_tensor(a, a, 1.0, causal_s[:, :].unsqueeze(1).to_broadcast([P, GH, P]),
                                               ALU.add, ALU.mult).then_inc(diag, 1)
                        two = range(2 * t, 2 * t + 2) if t < TILES // 2 else ()
                        for tile in two:
                            if g >= 1:
                                normalise(b, g - 1, tile)
                            if following is not None and g == 0:
                                tile_stats(following, tile)
                        if following is not None:
                            if g == 1 and t == TILES // 2:
                                variances(following)
                            if g >= 2 and t < TILES // 2:
                                layer_norm(following, (g - 2) * TILES // 2 + t)
                    if g + 1 < GROUPS:
                        copy_heads(g + 1)
                    if g == 0:
                        dve.wait_ge(before_ready, b + 1)
                    dve.wait_ge(pv_done, (b * GROUPS + g) * NS + NS)
                    v.tensor_tensor(yT[:, g, :].rearrange("p (t n) -> p t n", n=P), ps[:, 0:2, :].rearrange("p a (t n) -> p (a t) n", n=P),
                                    before[:, g, :].unsqueeze(2).to_broadcast([P, TILES, P]), ALU.add).then_inc(yT_ready, 1)

            for t in range(TILES):
                tile_stats(0, t)
            variances(0)
            for t in range(TILES):
                layer_norm(0, t)
            dve.wait_ge(const_in, CONST_IN)
            project(0)
            with dve.Fori(0, B - 1) as b:
                attention(b, b + 1)
                project(b + 1, b)
            attention(B - 1, None)
            for t in range(TILES):
                normalise(B - 1, GROUPS - 1, t)

        @block.scalar
        def _(act):
            a = nc.scalar
            act.wait_ge(const_in, CONST_IN)
            act.wait_ge(ones_set, 6)

            def copy_xT(b, t):
                act.wait_ge(xnT_ps, b * TILES + t + 1)
                a.activation(xnT[:, :, t * P:(t + 1) * P], ps[:, 2 + t % 2, 0:KC * P].rearrange("p (c n) -> p c n", c=KC),
                             ACT.Copy).then_inc(xnT_ready, 1)

            def copy_out(b, t):
                if t == 0 and isinstance(b, int):
                    act.wait_ge(stored, 16 * (2 * b + 1))
                elif t == 0:
                    act.wait_ge(stored, 16 * (2 * b + 2))
                act.wait_ge(ao_ps, b * TILES + t + 1)
                a.activation(ao[:, t, :], ps[:, t % 2, 0:DIM], ACT.Copy).then_inc(ao_ready, 1)

            def project(b, last=None):
                copy_xT(b, 0)
                for t in range(TILES):
                    if t + 1 < TILES:
                        copy_xT(b, t + 1)
                    act.wait_ge(proj_ps, b * TILES + t + 1)
                    qk = ps[:, 4 + t % 2, :].rearrange("p (a h d) -> p a h d", a=2, h=TH)
                    a.activation(parts[:, t, 0, :, 0:3, :], qk[:, 0].unsqueeze(2).to_broadcast([P, TH, 3, TD]), ACT.Copy)
                    a.activation(parts[:, t, 1, :, 0, :], qk[:, 1], ACT.Copy).then_inc(high, 1)
                    a.activation(vals[:, t, :, 0:TD], ps[:, 6 + t % 2, 0:TH * TD].rearrange("p (h d) -> p h d", h=TH),
                                 ACT.Copy).then_inc(v_ready, 1)
                    if last is not None:
                        copy_out(last, t)
                act.wait_ge(bsum_ps, b + 1)
                a.activation(bsum[:, :, 0:TD], ps[0:TILES, 0, 0:TH * TD].rearrange("p (h d) -> p h d", h=TH), ACT.Copy).then_inc(bsum_ready, 1)
                act.wait_ge(before_ps, b + 1)
                a.activation(before[:, :, :].rearrange("p g t -> p (g t)"), ps[:, 1, 0:GROUPS * TILES], ACT.Identity,
                             bias=eps_s[:, :]).then_inc(before_ready, 1)

            def attention(b):
                for g in range(GROUPS):
                    for u in ACT_HEADS:
                        act.wait_ge(qkT_ps, (b * GROUPS + g) * 2 * GH + u + 1)
                        a.activation(qkT[:, 1, u // 2, :], ps[0:SW, HEAD_BANK[u], :].bitcast(BF16), ACT.Copy).then_inc(kT_ready, 1)
                    for i, (j, half, c) in enumerate(STEPS):
                        for u in (2 * i, 2 * i + 1):
                            act.wait_ge(score_ps, (b * GROUPS + g) * 2 * NS + u + 1)
                            if i >= UNITS // 2:
                                act.wait_ge(pv_done, (b * GROUPS + g) * NS + i - UNITS // 2 + 1)
                            a.activation(weights[:, 2 * (u % UNITS):2 * (u % UNITS) + 2, c:512], ps[:, unit_bank(u):unit_bank(u) + 2, c:512], ACT.Square,
                                         bias=one_s[:, :], scale=0.25).then_inc(squared, 1)

            project(0)
            with act.Fori(0, B - 1) as b:
                attention(b)
                project(b + 1, b)
            attention(B - 1)
            for t in range(TILES):
                copy_out(B - 1, t)

        @block.tensor
        def _(pe):
            mm, tr = nc.tensor.matmul, nc.tensor.transpose
            pe.wait_ge(const_in, CONST_IN)

            def x_T(b, t):
                pe.wait_ge(xn_ready, b * TILES + t + 1)
                if t >= 2:
                    pe.wait_ge(xnT_ready, b * TILES + t - 1)
                for c in range(KC):
                    last = tr(ps[:, 2 + t % 2, c * P:(c + 1) * P], xn[:, t, c * P:(c + 1) * P], id_s[:, :])
                last.then_inc(xnT_ps, 1)

            def out_project(b, t):
                pe.wait_ge(y_ready, (b * GROUPS + GROUPS - 1) * TILES + t + 1)
                if t >= 2:
                    pe.wait_ge(ao_ready, b * TILES + t - 1)
                for g in range(GROUPS):
                    last = mm(ps[:, t % 2, 0:DIM], yT[:, g, t * P:(t + 1) * P], wo_s[:, g, :], start=(g == 0), stop=(g == GROUPS - 1))
                last.then_inc(ao_ps, 1)

            def project(b, last_b=None):
                x_T(b, 0)
                for t in range(TILES):
                    if t + 1 < TILES:
                        x_T(b, t + 1)
                    pe.wait_ge(xnT_ready, b * TILES + t + 1)
                    if t >= 2:
                        pe.wait_ge(rest_ready, b * TILES + t - 1)
                        pe.wait_ge(v_ready, b * TILES + t - 1)
                    for c in range(KC):
                        mm(ps[:, 4 + t % 2, :], xnT[:, c, t * P:(t + 1) * P], wqk_s[:, c, :], start=(c == 0), stop=(c == KC - 1))
                    for c in range(KC):
                        last = mm(ps[:, 6 + t % 2, 0:TH * TD], xnT[:, c, t * P:(t + 1) * P], wv_s[:, c, :], start=(c == 0), stop=(c == KC - 1))
                    last.then_inc(proj_ps, 1)
                    if last_b is not None:
                        out_project(last_b, t)
                pe.wait_ge(xsum_ready, b + 1)
                if last_b is not None:
                    pe.wait_ge(ao_ready, last_b * TILES + TILES)
                for c in range(KC):
                    last = mm(ps[0:TILES, 0, 0:TH * TD], xsum[:, c, :], wv_s[:, c, :], start=(c == 0), stop=(c == KC - 1))
                last.then_inc(bsum_ps, 1)
                pe.wait_ge(bsum_ready, b + 1)
                for g in range(GROUPS):
                    last = mm(ps[:, 1, g * TILES:(g + 1) * TILES], bsum[:, g * GH:(g + 1) * GH, :].rearrange("p h d -> p (h d)"),
                              earlier_s[:, :], start=True, stop=True)
                last.then_inc(before_ps, 1)

            def attention(b):
                pe.wait_ge(copies, 2 * TILES * (b + 1))
                pe.wait_ge(v_ready, b * TILES + TILES)
                for g in range(GROUPS):
                    def heads_T(g, us):
                        for u in us:
                            if u == 6:
                                pe.wait_ge(qkT_ready, (b * GROUPS + g) * len(DVE_HEADS) + 2)
                            if u == 7:
                                pe.wait_ge(kT_ready, (b * GROUPS + g) * len(ACT_HEADS) + 2)
                            for t in range(TILES):
                                last = tr(ps[0:SW, HEAD_BANK[u], :].bitcast(BF16)[:, t * P:(t + 1) * P],
                                          parts[:, t, u % 2, g * GH + u // 2].rearrange("p s d -> p (s d)"), idb_s[:, :])
                            last.then_inc(qkT_ps, 1)

                    def scores(u):
                        j, half, c = STEPS[u // 2]
                        if u >= 3:
                            pe.wait_ge(squared, (b * GROUPS + g) * 2 * NS + u - 2)
                        elif u == 0:
                            pe.wait_ge(qkT_ready, (b * GROUPS + g) * len(DVE_HEADS) + 2)
                            pe.wait_ge(kT_ready, (b * GROUPS + g) * len(ACT_HEADS) + 2)
                        elif u == 1:
                            pe.wait_ge(qkT_ready, (b * GROUPS + g) * len(DVE_HEADS) + len(DVE_HEADS))
                        for k in range(2):
                            h = 2 * (u % 2) + k
                            last = mm(ps[:, unit_bank(u) + k, c:512], qkT[:, 1, h, j * P:(j + 1) * P],
                                      qkT[:, 0, h, half * 512 + c:(half + 1) * 512], start=True, stop=True)
                        last.then_inc(score_ps, 1)

                    def attend(i):
                        j, half, c = STEPS[i]
                        if i == 0 and g == 0:
                            pe.wait_ge(before_ready, b + 1)
                        if i == 0 and g >= 1:
                            pe.wait_ge(yT_ready, b * GROUPS + g)
                        pe.wait_ge(squared, (b * GROUPS + g) * 2 * NS + 2 * i + 2)
                        if i in diag_no:
                            pe.wait_ge(diag, (b * GROUPS + g) * TILES + diag_no[i] + 1)
                        for h in range(GH):
                            last = mm(ps[h * VP:(h + 1) * VP, half, c:512], vals[:, j, g * GH + h, :],
                                      weights[:, 4 * i % (2 * UNITS) + h, c:512], start=(j == 0), stop=(j == 4 * half + 3),
                                      skip_group_check=True)
                        last.then_inc(pv_done, 1)

                    def squares_done(u):
                        pe.wait_ge(squared, (b * GROUPS + g) * 2 * NS + u + 1)

                    if g == 0:
                        heads_T(0, range(2 * GH))
                    for u in range(3):
                        scores(u)
                    for i in range(NS):
                        if 2 * i + 3 < 2 * NS:
                            scores(2 * i + 3)
                        if 1 <= i < NS - 1:
                            attend(i - 1)
                        if 2 * i + 4 < 2 * NS:
                            scores(2 * i + 4)
                    following = g + 1 < GROUPS
                    if following:
                        squares_done(2 * NS - 3)
                        heads_T(g + 1, (0, 1))
                        squares_done(2 * NS - 2)
                        heads_T(g + 1, (2, 3))
                    attend(NS - 2)
                    if following:
                        squares_done(2 * NS - 1)
                        heads_T(g + 1, (4, 5))
                    attend(NS - 1)
                    if following:
                        heads_T(g + 1, (6, 7))

            project(0)
            with pe.Fori(0, B - 1) as b:
                attention(b)
                project(b + 1, b)
            attention(B - 1)
            for t in range(TILES):
                out_project(B - 1, t)


def taylor_constants():
    k = np.arange(P)
    t = np.arange(TILES)
    causal = (k[:, None] <= k[None, :]).astype(np.float32)
    earlier = (t[:, None] < t[None, :]).astype(np.float32)
    eps = np.where(k % VP == TD, TEPS2, 0.0).astype(np.float32)[:, None]
    return causal, earlier, eps




def transformer_block(nc, PAIRS, x, xn_d, attn_d, wqkv, wo, w1, b1, w2, ln, qk_scale, rotary, masks, ident, shift,
                      carry_row, out):
    with ExitStack() as ctx:
        def sb(name, shape, dt=F32):
            return ctx.enter_context(nc.sbuf_tensor(name, shape, dt))

        def sem(name):
            return ctx.enter_context(nc.semaphore("f_" + name))

        def sems(name):
            return [sem(f"{name}{s}") for s in range(2)]

        ps = ctx.enter_context(nc.psum_tensor("f_ps", [P, 8, 512], F32))

        def bank(s, i):
            return ps[:, 4 * s + i, :]

        wqkv_s = sb("wqkv_s", [P, LAYERS, KC, 3 * INNER])
        wo_s = sb("fwo_s", [P, LAYERS, INNER // P, DIM])
        w1_s = sb("w1_s", [P, LAYERS, KC, 2, HID])
        b1_s = sb("b1_s", [P, LAYERS, 2, FB])
        w2_s = sb("w2_s", [P, LAYERS, FB, DIM])
        ln_s = sb("ln_s", [P, LAYERS, 2, KC])
        qks_s = sb("qks_s", [P, LAYERS, 2, 2, HD])
        id_s = sb("f_id", [P, P])
        shift_s = sb("shift_s", [P, P])
        carry_s = sb("carry_s", [P, P])
        rot = sb("rot", [P, TILES, LAYERS, 2, 2, HD])
        masks_s = sb("masks_s", [P, TILES, 2 * P + 1])
        mhalf = sb("f_mhalf", [P, 2 * HEADS])

        def each(name, shape):
            return [[sb(f"{name}{s}{l}", shape) for l in range(LAYERS)] for s in range(2)]

        def both(name, shape):
            return [sb(f"{name}{s}", shape) for s in range(2)]

        mask = both("mask", [P, 2 * P + 1])
        xin = both("xin", [P, DIM])
        xres = both("xres", [P, 2, DIM])
        hT = each("hT", [P, 1 + 2 * P])
        kT = each("kT", [P, HEADS // 2, 2 * P])
        vw = each("vw", [P, 2, INNER])
        x1 = each("x1", [P, DIM])
        xmid = both("xmid", [P, DIM])
        yout = both("yout", [P, DIM])
        carry = each("carry", [P, P])
        qk = both("qk", [P, 2 * HEADS, HD])
        work = both("work", [P, 2, 2 * HEADS, HD])
        sq = [work[s][:, 0] for s in range(2)]
        turned = [work[s][:, 1] for s in range(2)]
        pT = [work[s][:, :, :, :].rearrange("p a h d -> p (a h d)").rearrange("p (i n) -> p i n", n=P) for s in range(2)]
        ssq = both("ssq", [P, 2 * HEADS])
        rnorm = both("rnorm", [P, 2 * HEADS])
        qT = both("qT", [P, HEADS // 2, P])
        pr = both("pr", [P, HEADS, 2 * P])
        tab = pr[0][:, :, :].rearrange("p t (a b d) -> p t a b d", a=2, b=2)
        nmax = both("nmax", [P, HEADS])
        psum = both("psum", [P, HEADS])
        rsum = both("rsum", [P, HEADS])
        oT = both("oT", [P, INNER // P, P])
        st = both("st", [P, 2, 6])
        mv = both("mv", [P, 2])
        ve = both("ve", [P, 1])
        rstd = both("rstd", [P, 1])
        hn = [qk[s][:, :, :].rearrange("p h d -> p (h d)")[:, FB * P:FB * P + DIM] for s in range(2)]
        hnT = both("hnT", [P, KC, P])
        gate = [qk[s][:, :, :].rearrange("p h d -> p (h d)")[:, 0:FB * P].rearrange("p (j n) -> p j n", n=P) for s in range(2)]
        act_u = both("act_u", [P, FB, P])
        xb = both("xb", [P, DIM])

        const_in = sem("const_in")
        init = sem("init")
        xn_in = sems("xn_in")
        res_in = sems("res_in")
        y_out = sems("y_out")
        mask_set = sems("mask_set")
        kept = sems("kept")
        xT_ps = sems("xT_ps")
        edge = sems("edge")
        hT_ready = sems("hT_ready")
        k_ps = sems("k_ps")
        q_ps = sems("q_ps")
        v_ps = sems("v_ps")
        k_ready = sems("k_ready")
        q_ready = sems("q_ready")
        v_ready = sems("v_ready")
        sq_ready = sems("sq_ready")
        ssq_sum = sems("ssq_sum")
        ssq_ready = sems("ssq_ready")
        knorm_ready = sems("knorm_ready")
        qnorm_ready = sems("qnorm_ready")
        turn = sems("turn")
        cosd = sems("cosd")
        q_rotated = sems("q_rotated")
        k_rotated = sems("k_rotated")
        unit = sems("unit")
        qT_ps = sems("qT_ps")
        kT_ps = sems("kT_ps")
        qT_ready = sems("qT_ready")
        kT_ready = sems("kT_ready")
        score_ps = sems("score_ps")
        masked = sems("masked")
        nmax_ready = sems("nmax_ready")
        exped = sems("exped")
        rsum_ready = sems("rsum_ready")
        prob = sems("prob")
        pT_ps = sems("pT_ps")
        pT_act = sems("pT_act")
        pT_dve = sems("pT_dve")
        oT_ps = sems("oT_ps")
        oT_ready = sems("oT_ready")
        wo_ps = sems("wo_ps")
        x1_ready = sems("x1_ready")
        shift_ps = sems("shift_ps")
        stat1 = sems("stat1")
        stat2 = sems("stat2")
        var_ready = sems("var_ready")
        rstd_ready = sems("rstd_ready")
        hn_ready = sems("hn_ready")
        hnT_ps = sems("hnT_ps")
        hnT_ready = sems("hnT_ready")
        up_ps = sems("up_ps")
        gate_ready = sems("gate_ready")
        u_ready = sems("u_ready")
        xb_ready = sems("xb_ready")
        res_ready = sems("res_ready")
        down_ps = sems("down_ps")
        x2_ready = sems("x2_ready")
        passed_pool = sem("passed_pool")
        passed_dve = sem("passed_dve")

        consts = [(wqkv_s[:, :, :, :], wqkv), (wo_s[:, :, :, :], wo), (w1_s[:, :, :, :, :], w1), (b1_s[:, :, :, :], b1),
                  (w2_s[:, :, :, :], w2), (ln_s[:, :, :, :], ln), (qks_s[:, :, :, :, :], qk_scale.partition_broadcast(P)),
                  (tab[:, :, :, :, :], rotary), (masks_s[:, :, :], masks), (id_s[:, :], ident), (shift_s[:, :], shift),
                  (carry_s[:, :], carry_row)]
        CONST_IN = 16 * len(consts)
        N_TAB = TILES * LAYERS
        INIT_ZERO = 2 + 8 * LAYERS
        INIT = INIT_ZERO + N_TAB

        STREAMS = range(2)
        PAIRS_OF_HEADS = [(0, 2), (1, 3), (4, 6), (5, 7)]
        STEPS = LAYERS * PAIRS * TILES
        block = ctx.enter_context(nc.Block())

        def rows_of(s, it):
            return bass.ds(it * P + s * PAIRS * SEQ, P)

        def before(step):
            n, l, it = step
            return n - 1, 1 - l, it if l else it - 1

        def after(step):
            n, l, it = step
            return n + 1, 1 - l, it + 1 if l else it

        def is_zero(count):
            return isinstance(count, int) and count == 0

        def run(eng, start, half, end):
            first, last = (0, 0, 0), (STEPS - 1, 1, STEPS // LAYERS - 1)

            def both_halves(step, first=False, last=False):
                half(0, step, 1, None if first else before(step), not first)
                half(1, step, 0, step, not last)

            start(first)
            both_halves(first, first=True)
            with eng.Fori(0, STEPS // LAYERS - 1) as i:
                both_halves((LAYERS * i + 1, 1, i))
                both_halves((LAYERS * i + 2, 0, i + 1))
            both_halves(last, last=True)
            end(last)

        x_rows, xn_rows, attn_rows, out_rows = [d.rearrange("b t d -> (b t) d") for d in (x, xn_d, attn_d, out)]

        @block.sync
        def _(sp):
            for dst, src in consts:
                sp.dma_start(dst, src).then_inc(const_in, 16)

            def load_xn(s, it):
                sp.dma_start(xin[s][:, :], xn_rows[rows_of(s, it), :]).then_inc(xn_in[s], 16)

            def load_residual(s, it):
                sp.dma_start(xres[s][:, 0, :], x_rows[rows_of(s, it), :]).then_inc(res_in[s], 16)
                sp.dma_start(xres[s][:, 1, :], attn_rows[rows_of(s, it), :]).then_inc(res_in[s], 16)

            def store(s, it):
                sp.wait_ge(x2_ready[s], LAYERS * it + LAYERS)
                sp.dma_start(out_rows[rows_of(s, it), :], yout[s][:, :]).then_inc(y_out[s], 16)

            for s in STREAMS:
                load_xn(s, 0)
                load_residual(s, 0)
            with sp.Fori(0, STEPS // LAYERS - 1) as it:
                for s in STREAMS:
                    sp.wait_ge(x1_ready[s], LAYERS * it + 1)
                    load_xn(s, it + 1)
                for s in STREAMS:
                    sp.wait_ge(xb_ready[s], it + 1)
                    load_residual(s, it + 1)
                    store(s, it)
            for s in STREAMS:
                store(s, STEPS // LAYERS - 1)
                sp.wait_ge(y_out[s], 16 * (STEPS // LAYERS))

        @block.gpsimd
        def _(pool):
            g = nc.gpsimd
            g.memset(mhalf[:, :], -0.5).then_inc(init, 1)
            pool.wait_ge(const_in, CONST_IN)
            for l in range(LAYERS):
                for s in STREAMS:
                    g.memset(hT[s][l][:, :], 0.0).then_inc(init, 1)
                    g.memset(kT[s][l][:, :, :], 0.0).then_inc(init, 1)
                    g.memset(vw[s][l][:, :, :], 0.0).then_inc(init, 1)
                    g.memset(x1[s][l][:, :], 0.0).then_inc(init, 1)
            for s in STREAMS:
                g.memset(act_u[s][:, FB - 1, :], 1.0).then_inc(init, 1)
            pool.wait_ge(init, INIT_ZERO + 1)
            for t in range(TILES):
                for l in range(LAYERS):
                    g.tensor_tensor(rot[:, t, l].rearrange("p a b d -> p (a b d)"), tab[:, t].rearrange("p a b d -> p (a b d)"),
                                    qks_s[:, l].rearrange("p a b d -> p (a b d)"), ALU.mult).then_inc(init, 1)
            pool.wait_ge(init, INIT + 1)

            def keep(s, step):
                n, l, it = step
                pool.wait_ge(mask_set[s], it + 1)
                if not is_zero(n):
                    pool.wait_ge(shift_ps[s], n)
                pool.sem_inc(passed_pool, 1)
                g.tensor_copy(kT[s][l][:, :, 0:P], kT[s][l][:, :, P:2 * P]).then_inc(kept[s], 1)
                g.tensor_copy(vw[s][l][:, 0, :], vw[s][l][:, 1, :]).then_inc(kept[s], 1)
                g.tensor_scalar(carry[s][l][:, :], x1[s][l][:, P:DIM], mask[s][:, 2 * P:2 * P + 1], None, ALU.mult).then_inc(kept[s], 1)

            def turn_part(s, step, a, ready):
                n, l, it = step
                t = it % TILES
                heads = slice(a * HEADS, a * HEADS + HEADS)
                pool.wait_ge(ready[s], n + 1)
                pool.sem_inc(passed_pool, 1)
                for half in range(2):
                    f, z = slice(half * 32, half * 32 + 32), slice(32 - half * 32, 64 - half * 32)
                    sines = rot[:, bass.ds(t, 1), l, 1, a, f].to_broadcast([P, HEADS, 32])
                    g.tensor_tensor(turned[s][:, heads, f], qk[s][:, heads, z], sines, ALU.mult).then_inc(turn[s], 1)

            def norms(s, step):
                n, l, it = step
                pool.wait_ge(ssq_ready[s], 2 * n + 1)
                g.tensor_tensor(rnorm[s][:, HEADS:], ssq[s][:, HEADS:], mhalf[:, HEADS:], ALU.pow).then_inc(knorm_ready[s], 1)
                pool.wait_ge(ssq_ready[s], 2 * n + 2)
                g.tensor_tensor(rnorm[s][:, 0:HEADS], ssq[s][:, 0:HEADS], mhalf[:, 0:HEADS], ALU.pow).then_inc(qnorm_ready[s], 1)

            def ln_root(s, step):
                n, l, it = step
                pool.wait_ge(var_ready[s], n + 1)
                g.tensor_tensor(rstd[s][:, :], ve[s][:, :], mhalf[:, 0:1], ALU.pow).then_inc(rstd_ready[s], 1)

            def residual(s, step):
                n, l, it = step
                pool.wait_ge(res_in[s], 32 * it + 32)
                g.tensor_tensor(xres[s][:, 0, :], xres[s][:, 0, :], xres[s][:, 1, :], ALU.add).then_inc(res_ready[s], 1)
                pool.wait_ge(res_ready[s], it + 1)
                pool.wait_ge(x1_ready[s], n + 1)
                g.tensor_tensor(xb[s][:, :], xres[s][:, 0, :], x1[s][l][:, :], ALU.add).then_inc(xb_ready[s], 1)

            def half(x, xs, y, ys, t):
                turn_part(x, xs, 1, k_ready)
                turn_part(x, xs, 0, q_ready)
                norms(x, xs)
                if ys:
                    ln_root(y, ys)
                    if ys[1] == LAYERS - 1:
                        residual(y, ys)
                    if t:
                        keep(y, after(ys))

            def start(step):
                for s in STREAMS:
                    keep(s, step)

            def end(step):
                ln_root(1, step)
                residual(1, step)

            run(pool, start, half, end)

        @block.vector
        def _(dve):
            v = nc.vector
            dve.wait_ge(const_in, CONST_IN)
            dve.wait_ge(init, INIT + 1)

            def set_mask(s, step):
                n, l, it = step
                if not is_zero(n):
                    dve.wait_ge(kept[s], 3 * n)
                    dve.wait_ge(edge[s], n)
                    dve.sem_inc(passed_dve, 1)
                v.tensor_copy(mask[s][:, :], masks_s[:, bass.ds(it % TILES, 1), :].rearrange("p o n -> p (o n)")).then_inc(mask_set[s], 1)

            def squares_and_cosines(s, step, a):
                n, l, it = step
                i = 2 * n + 2 - a
                heads = slice(a * HEADS, a * HEADS + HEADS)
                cosines = rot[:, bass.ds(it % TILES, 1), l, 0, a, :].to_broadcast([P, HEADS, HD])
                dve.wait_ge(sq_ready[s], i)
                v.reduce_sum(ssq[s][:, heads], sq[s][:, heads, :], AX).then_inc(ssq_sum[s], 1)
                dve.wait_ge(ssq_sum[s], i)
                v.tensor_scalar_max(ssq[s][:, heads], ssq[s][:, heads], 1e-24).then_inc(ssq_ready[s], 1)
                v.tensor_tensor(sq[s][:, heads, :], qk[s][:, heads, :], cosines, ALU.mult).then_inc(cosd[s], 1)

            def rotate(s, step):
                n, l, it = step
                dve.wait_ge(cosd[s], 2 * n + 2)
                dve.wait_ge(turn[s], 4 * n + 4)
                v.tensor_tensor(qk[s][:, 0:HEADS, :], sq[s][:, 0:HEADS, :], turned[s][:, 0:HEADS, :], ALU.add).then_inc(q_rotated[s], 1)
                v.tensor_tensor(qk[s][:, HEADS:, :], sq[s][:, HEADS:, :], turned[s][:, HEADS:, :], ALU.add).then_inc(k_rotated[s], 1)
                dve.wait_ge(k_rotated[s], n + 1)
                dve.wait_ge(knorm_ready[s], n + 1)
                v.tensor_tensor(qk[s][:, HEADS:, :], qk[s][:, HEADS:, :], rnorm[s][:, HEADS:].unsqueeze(2).to_broadcast([P, HEADS, HD]),
                                ALU.mult).then_inc(unit[s], 1)

            def mask_scores(s, step, p):
                n, l, it = step
                heads = PAIRS_OF_HEADS[p]
                both_heads = slice(heads[0], heads[1] + 1, 2)
                dve.wait_ge(score_ps[s], n * 4 + p + 1)
                dve.sem_inc(passed_dve, 1)
                for h in heads:
                    sc = bank(s, 2 * (h % 2) + h // 4)[:, (h // 2 % 2) * 256:(h // 2 % 2) * 256 + 256]
                    last = v.tensor_tensor_reduce(out=pr[s][:, h, :], in0=sc, in1=mask[s][:, 0:2 * P], scale=1.0, scalar=-3.0e38,
                                                  op0=ALU.add, op1=ALU.max, accum_out=nmax[s][:, h:h + 1])
                last.then_inc(masked[s], 1)
                dve.wait_ge(masked[s], n * 4 + p + 1)
                if p == 0:
                    dve.wait_ge(qnorm_ready[s], n + 1)
                v.scalar_tensor_tensor(nmax[s][:, both_heads], nmax[s][:, both_heads], -1.0, rnorm[s][:, both_heads],
                                       ALU.mult, ALU.mult).then_inc(nmax_ready[s], 1)

            def sums(s, step, q):
                n, l, it = step
                four = slice(4 * q, 4 * q + 4)
                dve.wait_ge(exped[s], n * 4 + 2 * q + 2)
                v.reciprocal(rsum[s][:, four], psum[s][:, four]).then_inc(rsum_ready[s], 1)

            def normalise(s, step, q):
                n, l, it = step
                dve.wait_ge(rsum_ready[s], n * 2 + q + 1)
                for h in range(4 * q, 4 * q + 4):
                    last = v.tensor_scalar_mul(pr[s][:, h, :], pr[s][:, h, :], rsum[s][:, h:h + 1])
                    if h % 2:
                        last.then_inc(prob[s], 1)

            def copy_pT(s, step):
                n, l, it = step
                for i in range(2, 4):
                    dve.wait_ge(pT_ps[s], n * 4 + i + 1)
                    v.tensor_copy(pT[s][:, 4 * i:4 * i + 4, :].rearrange("p a n -> p (a n)"), bank(s, i)).then_inc(pT_dve[s], 1)

            def add_attention(s, step):
                n, l, it = step
                xprev = xin[s] if l == 0 else xmid[s]
                if l == 0:
                    dve.wait_ge(xn_in[s], 16 * it + 16)
                dve.wait_ge(kept[s], 3 * n + 3)
                dve.wait_ge(wo_ps[s], n + 1)
                v.tensor_tensor(x1[s][l][:, :], bank(s, 1)[:, 0:DIM], xprev[:, :], ALU.add).then_inc(x1_ready[s], 1)

            def row_statistics(s, step):
                n, l, it = step
                dve.wait_ge(x1_ready[s], n + 1)
                v.bn_stats(st[s][:, 0, :], x1[s][l][:, 0:P])
                dve.wait_ge(shift_ps[s], n + 1)
                v.bn_stats(st[s][:, 1, :], bank(s, 2)[:, 0:P]).then_inc(stat1[s], 1)
                dve.wait_ge(stat1[s], n + 1)
                dve.sem_inc(passed_dve, 1)
                v.bn_aggr(mv[s][:, :], st[s][:, :, :].rearrange("p a n -> p (a n)")).then_inc(stat2[s], 1)
                dve.wait_ge(stat2[s], n + 1)
                v.tensor_scalar_add(ve[s][:, :], mv[s][:, 1:2], LN_EPS).then_inc(var_ready[s], 1)

            def layer_norm(s, step):
                n, l, it = step
                dve.wait_ge(rstd_ready[s], n + 1)
                v.tensor_scalar(hn[s][:, 0:P], x1[s][l][:, 0:P], mv[s][:, 0:1], rstd[s][:, :], ALU.subtract, ALU.mult)
                v.tensor_scalar(hn[s][:, P:DIM], bank(s, 2)[:, 0:P], mv[s][:, 0:1], rstd[s][:, :], ALU.subtract, ALU.mult)\
                    .then_inc(hn_ready[s], 1)

            def gated(s, step):
                n, l, it = step
                for j in range(FB):
                    rows = P if j < FB - 1 else FLAST
                    if j % 2 == 0:
                        dve.wait_ge(gate_ready[s], n * 3 + j // 2 + 1)
                    v.scalar_tensor_tensor(act_u[s][0:rows, j, :], bank(s, j // 2)[0:rows, (j % 2) * 256:(j % 2) * 256 + P],
                                           b1_s[0:rows, l, 0, j:j + 1], gate[s][0:rows, j, :], ALU.add, ALU.mult).then_inc(u_ready[s], 1)

            def add_ffn(s, step):
                n, l, it = step
                if l == 0:
                    dve.wait_ge(down_ps[s], n + 1)
                    v.tensor_tensor(xmid[s][:, :], bank(s, 3)[:, 0:DIM], x1[s][l][:, :], ALU.add).then_inc(x2_ready[s], 1)
                else:
                    dve.wait_ge(xb_ready[s], it + 1)
                    if not is_zero(it):
                        dve.wait_ge(y_out[s], 16 * it)
                    dve.wait_ge(down_ps[s], n + 1)
                    v.tensor_tensor(yout[s][:, :], bank(s, 3)[:, 0:DIM], xb[s][:, :], ALU.add).then_inc(x2_ready[s], 1)

            def half(x, xs, y, ys, t):
                if ys:
                    copy_pT(y, ys)
                squares_and_cosines(x, xs, 1)
                squares_and_cosines(x, xs, 0)
                rotate(x, xs)
                if ys:
                    add_attention(y, ys)
                    row_statistics(y, ys)
                mask_scores(x, xs, 0)
                if ys:
                    layer_norm(y, ys)
                for p in range(1, 4):
                    mask_scores(x, xs, p)
                sums(x, xs, 0)
                normalise(x, xs, 0)
                sums(x, xs, 1)
                if ys:
                    gated(y, ys)
                normalise(x, xs, 1)
                if ys:
                    if t and ys[1]:
                        set_mask(y, after(ys))
                    add_ffn(y, ys)

            def start(step):
                for s in STREAMS:
                    set_mask(s, step)

            def end(step):
                copy_pT(1, step)
                add_attention(1, step)
                row_statistics(1, step)
                layer_norm(1, step)
                gated(1, step)
                add_ffn(1, step)

            run(dve, start, half, end)

        @block.scalar
        def _(act):
            a = nc.scalar
            act.wait_ge(const_in, CONST_IN)
            act.wait_ge(init, INIT + 1)

            def copy_edge(s, step):
                n, l, it = step
                act.wait_ge(mask_set[s], it + 1)
                a.activation(hT[s][l][:, 0:1], hT[s][l][:, P:P + 1], ACT.Copy, scale=mask[s][:, 2 * P:2 * P + 1]).then_inc(edge[s], 1)

            def copy_hT(s, step):
                n, l, it = step
                act.wait_ge(edge[s], n + 1)
                act.wait_ge(xT_ps[s], n + 1)
                a.activation(hT[s][l][:, 1:1 + 2 * P], bank(s, 3)[:, 0:2 * P], ACT.Copy).then_inc(hT_ready[s], 1)

            def copy_part(s, step, i, ps_ready, ready):
                n, l, it = step
                heads = slice(i * HEADS, i * HEADS + HEADS)
                act.wait_ge(ps_ready[s], n + 1)
                a.activation(qk[s][:, heads, :].rearrange("p h d -> p (h d)"), bank(s, i), ACT.Copy).then_inc(ready[s], 1)
                act.wait_ge(ready[s], n + 1)
                a.activation(sq[s][:, heads, :], qk[s][:, heads, :], ACT.Square).then_inc(sq_ready[s], 1)

            def copy_v(s, step):
                n, l, it = step
                act.wait_ge(kept[s], 3 * n + 3)
                act.wait_ge(v_ps[s], n + 1)
                a.activation(vw[s][l][:, 1, :], bank(s, 2), ACT.Copy).then_inc(v_ready[s], 1)

            def copy_qT(s, step):
                n, l, it = step
                act.wait_ge(qT_ps[s], n + 1)
                a.activation(qT[s][:, :, :], bank(s, 3).rearrange("p (c n) -> p c n", n=P), ACT.Copy).then_inc(qT_ready[s], 1)

            def copy_kT(s, step):
                n, l, it = step
                act.wait_ge(kT_ps[s], n + 1)
                a.activation(kT[s][l][:, :, P:2 * P], bank(s, 1).rearrange("p (c n) -> p c n", n=P), ACT.Copy).then_inc(kT_ready[s], 1)

            def copy_hnT(s, step):
                n, l, it = step
                act.wait_ge(hnT_ps[s], n + 1)
                for c in range(KC):
                    last = a.activation(hnT[s][:, c, :], bank(s, 3)[:, c * P:(c + 1) * P], ACT.Identity, bias=ln_s[:, l, 1, c:c + 1],
                                        scale=ln_s[:, l, 0, c:c + 1])
                last.then_inc(hnT_ready[s], 1)

            def exps(s, step, p):
                n, l, it = step
                act.wait_ge(nmax_ready[s], n * 4 + p + 1)
                for h in PAIRS_OF_HEADS[p]:
                    last = a.activation(pr[s][:, h, :], pr[s][:, h, :], ACT.Exp, bias=nmax[s][:, h:h + 1], scale=rnorm[s][:, h:h + 1],
                                        accum_out=psum[s][:, h:h + 1])
                last.then_inc(exped[s], 1)

            def copy_pT(s, step, i):
                n, l, it = step
                act.wait_ge(pT_ps[s], n * 4 + i + 1)
                a.activation(pT[s][:, 4 * i:4 * i + 4, :].rearrange("p a n -> p (a n)"), bank(s, i), ACT.Copy).then_inc(pT_act[s], 1)

            def copy_oT(s, step):
                n, l, it = step
                act.wait_ge(oT_ps[s], n + 1)
                a.activation(oT[s][:, :, :].rearrange("p a n -> p (a n)"), bank(s, 0), ACT.Copy).then_inc(oT_ready[s], 1)

            def gelus(s, step):
                n, l, it = step
                for j in range(FB):
                    rows = P if j < FB - 1 else FLAST
                    if j % 2 == 0:
                        act.wait_ge(up_ps[s], n * 3 + j // 2 + 1)
                    last = a.activation(gate[s][0:rows, j, :], bank(s, j // 2)[0:rows, (j % 2) * 256 + P:(j % 2) * 256 + 2 * P], ACT.Gelu,
                                        bias=b1_s[0:rows, l, 1, j:j + 1])
                    if j % 2:
                        last.then_inc(gate_ready[s], 1)

            def half(x, xs, y, ys, t):
                if ys:
                    copy_pT(y, ys, 0)
                copy_hT(x, xs)
                if ys:
                    copy_pT(y, ys, 1)
                copy_part(x, xs, 1, k_ps, k_ready)
                copy_part(x, xs, 0, q_ps, q_ready)
                if ys:
                    copy_oT(y, ys)
                copy_qT(x, xs)
                copy_kT(x, xs)
                copy_v(x, xs)
                exps(x, xs, 0)
                if ys:
                    copy_hnT(y, ys)
                for p in range(1, 4):
                    exps(x, xs, p)
                if ys:
                    gelus(y, ys)
                    if t:
                        copy_edge(y, after(ys))

            def start(step):
                for s in STREAMS:
                    copy_edge(s, step)

            def end(step):
                copy_pT(1, step, 0)
                copy_pT(1, step, 1)
                copy_oT(1, step)
                copy_hnT(1, step)
                gelus(1, step)

            run(act, start, half, end)

        @block.tensor
        def _(pe):
            mm, tr = nc.tensor.matmul, nc.tensor.transpose
            pe.wait_ge(const_in, CONST_IN)
            pe.wait_ge(init, INIT + 1)

            def x_T(s, step):
                n, l, it = step
                xprev = xin[s] if l == 0 else xmid[s]
                if l == 0:
                    pe.wait_ge(xn_in[s], 16 * it + 16)
                if not is_zero(n):
                    pe.wait_ge(x2_ready[s], n)
                tr(bank(s, 3)[:, 0:P], xprev[:, P:DIM], id_s[:, :])
                tr(bank(s, 3)[:, P:2 * P], xprev[:, 0:P], id_s[:, :]).then_inc(xT_ps[s], 1)

            def project(s, step, i, done, chunks=(0, 1)):
                n, l, it = step
                pe.wait_ge(hT_ready[s], n + 1)
                for c in chunks:
                    rows = hT[s][l][:, 0:P] if c else hT[s][l][:, P + 1:2 * P + 1]
                    last = mm(bank(s, i), rows, wqkv_s[:, l, c, i * INNER:(i + 1) * INNER], start=(c == 0), stop=(c == KC - 1))
                if c == KC - 1:
                    last.then_inc(done[s], 1)

            def heads_T(s, step, i, b, ready, done):
                n, l, it = step
                pe.wait_ge(ready[s], n + 1)
                for h in range(0, HEADS, 2):
                    last = tr(bank(s, b)[:, h // 2 * P:(h // 2 + 1) * P],
                              qk[s][:, i * HEADS + h:i * HEADS + h + 2, :].rearrange("p h d -> p (h d)"), id_s[:, :])
                last.then_inc(done[s], 1)

            def scores(s, step, p):
                n, l, it = step
                if p == 0:
                    pe.wait_ge(qT_ready[s], n + 1)
                    pe.wait_ge(kT_ready[s], n + 1)
                if p == 1:
                    pe.wait_ge(v_ready[s], n + 1)
                for h in PAIRS_OF_HEADS[p]:
                    r = slice(h % 2 * HD, h % 2 * HD + HD)
                    last = mm(bank(s, 2 * (h % 2) + h // 4)[:, (h // 2 % 2) * 256:(h // 2 % 2) * 256 + 256], qT[s][r, h // 2, :],
                              kT[s][l][r, h // 2, :], start=True, stop=True)
                last.then_inc(score_ps[s], 1)

            def prob_T(s, step, q):
                n, l, it = step
                pe.wait_ge(masked[s], n * 4 + 4)
                for h in range(4 * q, 4 * q + 4):
                    if h % 2 == 0:
                        pe.wait_ge(prob[s], n * 4 + h // 2 + 1)
                    for half in range(2):
                        i = 2 * h + half
                        last = tr(bank(s, i // 4)[:, (i % 4) * P:(i % 4 + 1) * P], pr[s][:, h, half * P:(half + 1) * P], id_s[:, :])
                    if h % 2:
                        last.then_inc(pT_ps[s], 1)

            def attend(s, step):
                n, l, it = step
                for i in range(HEADS // 2):
                    if i < 2:
                        pe.wait_ge(pT_act[s], n * 2 + i + 1)
                    else:
                        pe.wait_ge(pT_dve[s], n * 2 + i - 1)
                    for half in range(2):
                        for k in range(2):
                            h = 2 * i + k
                            last = mm(bank(s, 0)[k * HD:(k + 1) * HD, i * P:(i + 1) * P], vw[s][l][:, half, h * HD:(h + 1) * HD],
                                      pT[s][:, 2 * h + half, :], start=(half == 0), stop=(half == 1))
                last.then_inc(oT_ps[s], 1)

            def out_project(s, step):
                n, l, it = step
                pe.wait_ge(oT_ready[s], n + 1)
                for c in range(INNER // P):
                    last = mm(bank(s, 1)[:, 0:DIM], oT[s][:, c, :], wo_s[:, l, c, :], start=(c == 0), stop=(c == INNER // P - 1))
                last.then_inc(wo_ps[s], 1)

            def shift_x1(s, step):
                n, l, it = step
                pe.wait_ge(kept[s], 3 * n + 3)
                pe.wait_ge(x1_ready[s], n + 1)
                mm(bank(s, 2)[:, 0:P], shift_s[:, :], x1[s][l][:, P:DIM], start=True, stop=False)
                mm(bank(s, 2)[:, 0:P], carry_s[96:P, :], carry[s][l][96:P, :], start=False, stop=True).then_inc(shift_ps[s], 1)

            def hn_T(s, step):
                n, l, it = step
                pe.wait_ge(hn_ready[s], n + 1)
                for c in range(KC):
                    last = tr(bank(s, 3)[:, c * P:(c + 1) * P], hn[s][:, c * P:(c + 1) * P], id_s[:, :])
                last.then_inc(hnT_ps[s], 1)

            def up(s, step):
                n, l, it = step
                pe.wait_ge(hnT_ready[s], n + 1)
                for j in range(FB):
                    rows = P if j < FB - 1 else FLAST
                    for half in range(2):
                        o = (j % 2) * 256 + half * P
                        for c in range(KC):
                            last = mm(bank(s, j // 2)[0:rows, o:o + P], w1_s[:, l, c, half, j * P:j * P + rows], hnT[s][:, c, :],
                                      start=(c == 0), stop=(c == KC - 1))
                    if j % 2:
                        last.then_inc(up_ps[s], 1)

            def down(s, step):
                n, l, it = step
                for j in range(FB):
                    rows = P if j < FB - 1 else FLAST + 1
                    pe.wait_ge(u_ready[s], n * FB + j + 1)
                    last = mm(bank(s, 3)[:, 0:DIM], act_u[s][0:rows, j, :], w2_s[0:rows, l, j, :], start=(j == 0), stop=(j == FB - 1))
                last.then_inc(down_ps[s], 1)

            def half(x, xs, y, ys, t):
                if ys:
                    prob_T(y, ys, 0)
                x_T(x, xs)
                if ys:
                    prob_T(y, ys, 1)
                project(x, xs, 1, k_ps)
                project(x, xs, 0, q_ps)
                if ys:
                    attend(y, ys)
                project(x, xs, 2, v_ps, (0,))
                if ys:
                    out_project(y, ys)
                heads_T(x, xs, 0, 3, q_rotated, qT_ps)
                heads_T(x, xs, 1, 1, unit, kT_ps)
                project(x, xs, 2, v_ps, (1,))
                if ys:
                    shift_x1(y, ys)
                for p in range(3):
                    scores(x, xs, p)
                if ys:
                    hn_T(y, ys)
                scores(x, xs, 3)
                if ys:
                    up(y, ys)
                    down(y, ys)

            def start(step):
                pass

            def end(step):
                prob_T(1, step, 0)
                prob_T(1, step, 1)
                attend(1, step)
                out_project(1, step)
                shift_x1(1, step)
                hn_T(1, step)
                up(1, step)
                down(1, step)

            run(pe, start, half, end)


def transformer_constants():
    half = np.arange(0, HD, 2, dtype=np.float32)
    inv_freq = (1.0 / np.float32(10000.0) ** (half / np.float32(HD))).astype(np.float32)
    t = np.arange(SEQ, dtype=np.float32)
    freqs = np.concatenate([t[:, None] * inv_freq] * 2, 1)
    base = (half + np.float32(0.4 * HD)) / np.float32(1.4 * HD)
    power = (t - SEQ // 2) / np.float32(P // 2)
    scale = np.concatenate([base[None, :] ** power[:, None]] * 2, 1).astype(np.float32)
    cos, sin = np.cos(freqs), np.sin(freqs)
    sign = np.where(np.arange(HD) < HD // 2, -1.0, 1.0).astype(np.float32)
    tab = np.stack([np.stack([8 * cos * scale, cos / scale]), np.stack([8 * sign * sin * scale, sign * sin / scale])])
    tab = tab.reshape(2, 2, TILES, P, HD).transpose(3, 2, 0, 1, 4).astype(np.float32)
    i, j = np.arange(P)[:, None], np.arange(2 * P)[None, :] - P
    masks = np.zeros((P, TILES, 2 * P + 1), np.float32)
    masks[:, :, :2 * P] = np.where((i < j) | (i > j + P), -3e38, 0.0)[:, None, :]
    masks[:, 0, :P] = -3e38
    masks[:, 1:, 2 * P] = 1.0
    shift = np.eye(P, k=1, dtype=np.float32)
    carry = np.zeros((P, P), np.float32)
    carry[P - 1, 0] = 1.0
    return tab, masks, shift, carry


def chunked(w):
    return w.reshape(-1, P, w.shape[-1]).transpose(1, 0, 2)


def kernel(**inputs):
    import ml_dtypes
    import concourse.bacc as _bacc
    from concourse.bass_utils import run_bass_kernel_spmd as _run

    a = {k: np.asarray(v) for k, v in inputs.items()}
    x = a["L0_attn_hidden_states"]
    B = x.shape[0]
    f = {k[len("L0_ffn_"):]: v for k, v in a.items() if k.startswith("L0_ffn_")}

    two = np.zeros((TH, VP, DIM), np.float32)
    two[:, :TD] = a["L0_attn_Wo"].T.reshape(TH, TD, DIM)
    b1 = np.zeros((LAYERS, 2, FB * P), np.float32)
    b1[..., :HID] = f["b1"].reshape(LAYERS, 2, HID)
    w2 = np.zeros((LAYERS, FB * P, DIM), np.float32)
    w2[:, :HID] = f["w2"]
    w2[:, HID] = f["b2"]
    ln = np.stack([f["ln_g"], f["ln_b"]], 1)
    scales = np.stack([f["q_scale"], f["k_scale"]], 1)
    scales = np.stack([scales, np.roll(scales, HD // 2, -1)], 1)

    arrays = {
        "x": x,
        "t_wqk": chunked(np.concatenate([a["L0_attn_Wq"].T, a["L0_attn_Wk"].T], 1)),
        "t_wv": chunked(a["L0_attn_Wv"].T),
        "t_wo": chunked(two.reshape(TH * VP, DIM)),
        "wqkv": f["wqkv"].reshape(LAYERS, KC, P, 3 * INNER).transpose(2, 0, 1, 3),
        "wo": f["wo"].reshape(LAYERS, INNER // P, P, DIM).transpose(2, 0, 1, 3),
        "w1": f["w1"].reshape(LAYERS, KC, P, 2, HID).transpose(2, 0, 1, 3, 4),
        "b1": b1.reshape(LAYERS, 2, FB, P).transpose(3, 0, 1, 2),
        "w2": w2.reshape(LAYERS, FB, P, DIM).transpose(2, 0, 1, 3),
        "ln": ln.reshape(LAYERS, 2, KC, P).transpose(3, 0, 1, 2),
        "scales": scales,
        "ident": np.eye(P, dtype=np.float32),
        "ident_bf": np.eye(P, dtype=np.float32).astype(ml_dtypes.bfloat16),
    }
    for name, c in zip(("causal", "earlier", "eps_rows"), taylor_constants()):
        arrays[name] = c
    for name, c in zip(("rotary", "masks", "shift", "carry_row"), transformer_constants()):
        arrays[name] = c
    arrays = {f"{k}_dram": np.ascontiguousarray(v) for k, v in arrays.items()}

    nc = _bacc.Bacc("TRN2", target_bir_lowering=False, num_devices=1)
    d = {k[:-5]: nc.dram_tensor(k, v.shape, mybir.dt.from_np(v.dtype), kind="ExternalInput").ap() for k, v in arrays.items()}
    out = nc.dram_tensor("out_dram", x.shape, F32, kind="ExternalOutput").ap()
    xn_d = nc.dram_tensor("xn_dram", x.shape, F32).ap()
    attn_d = nc.dram_tensor("attn_dram", x.shape, F32).ap()

    taylor_block(nc, B, d["x"], d["t_wqk"], d["t_wv"], d["t_wo"], d["ident"], d["ident_bf"], d["causal"], d["earlier"],
                 d["eps_rows"], xn_d, attn_d)
    transformer_block(nc, B // 2, d["x"], xn_d, attn_d, d["wqkv"], d["wo"], d["w1"], d["b1"], d["w2"], d["ln"], d["scales"],
                      d["rotary"], d["masks"], d["ident"], d["shift"], d["carry_row"], out)
    return _run(nc, [arrays], core_ids=[0]).results[0]["out_dram"]
```

```python
from contextlib import ExitStack

import numpy as np

import concourse.bass as bass
from concourse import mybir

F32 = mybir.dt.float32
BF16 = mybir.dt.bfloat16
ALU = mybir.AluOpType
ACT = mybir.ActivationFunctionType
AX = mybir.AxisListType.X

P = 128
DIM = 256
KC = DIM // P
TILES = 8
SEQ = P * TILES

TH, TD = 16, 16
GROUPS, GH = 4, 4
VP = 32
VALUES = (slice(0, TD), slice(TD, VP))
ONE = (TD, 0)
SLOTS = 6
SW = SLOTS * TD
TEPS = 32 * 1e-12

LAYERS, HEADS, HD = 2, 8, 64
INNER = HEADS * HD
HID = 682
FB = 6
FLAST = HID - (FB - 1) * P
LN_EPS = 1e-5

STEPS = [(j, h, max(0, P * j - 512 * h)) for j in range(TILES) for h in range(2) if P * j < 512 * (h + 1)]


def taylor_block(nc, B, x, wqk, wv, wo, ident, ident_bf, causal, earlier, eps_rows, keep_rows, later, xn_d, attn_d):
    with ExitStack() as ctx:
        def sb(name, shape, dt=F32):
            return ctx.enter_context(nc.sbuf_tensor(name, shape, dt))

        def sem(name):
            return ctx.enter_context(nc.semaphore("t_" + name))

        ps = ctx.enter_context(nc.psum_tensor("t_ps", [P, 8, 512], F32))

        LAG = 3
        LEAD = 3
        UNITS = 6
        wqk_s = sb("wqk_s", [P, KC, 512])
        wv_s = sb("wv_s", [P, KC, TH * TD])
        wo_s = sb("two_s", [P, GROUPS // 2, DIM])
        id_s = sb("t_id", [P, P])
        idb_s = sb("t_idb", [P, P], BF16)
        causal_s = sb("causal_s", [P, P])
        earlier_s = sb("earlier_s", [TILES, TILES])
        eps_s = sb("eps_s", [P, 2])
        keep_s = sb("keep_s", [P, 2])
        four_s = sb("four_s", [P, 1])
        mhalf = sb("mhalf", [P, TILES])
        xs = sb("xs", [P, TILES, DIM])
        xn = sb("xn", [P, TILES, DIM])
        xnT = sb("xnT", [P, KC, SEQ])
        xsum = sb("xsum", [P, KC, TILES])
        st = sb("t_st", [P, TILES, 6])
        mv = sb("t_mv", [P, TILES, 2])
        ve = sb("t_ve", [P, TILES])
        rstd = sb("t_rstd", [P, TILES])
        parts = sb("parts", [P, TILES, 2, TH, SLOTS, TD], BF16)
        rest = sb("rest", [P, 2, 2, TH, TD])
        vals = sb("vals", [P, TILES, TH, VP])
        qkT = sb("qkT", [SW, 2, GH + 1, SEQ], BF16)
        weights = sb("weights", [P, UNITS * 2, 512])
        bsum = sb("bsum", [TILES, TH, VP])
        before = sb("before", [P, GROUPS, TILES])
        yT = sb("yT", [P, GROUPS, SEQ])
        den = sb("den", [P, SEQ])
        den_flat = sb("den_flat", [P, GH * SEQ // P])
        ao = sb("ao", [P, TILES, DIM])

        const_in = sem("const_in")
        later_in = sem("later_in")
        ones_set = sem("ones_set")
        x_in = sem("x_in")
        stored = sem("stored")
        stats = sem("stats")
        var_ready = sem("var_ready")
        rstd_ready = sem("rstd_ready")
        xn_ready = sem("xn_ready")
        xnT_ps = sem("xnT_ps")
        xnT_ready = sem("xnT_ready")
        proj_ps = sem("proj_ps")
        high = sem("high")
        v_ready = sem("v_ready")
        rest_ready = sem("rest_ready")
        mid_q = sem("mid_q")
        mid_k = sem("mid_k")
        low = sem("low")
        copies = sem("copies")
        xsum_ready = sem("xsum_ready")
        bsum_ps = sem("bsum_ps")
        bsum_ready = sem("bsum_ready")
        before_ps = sem("before_ps")
        before_ready = sem("before_ready")
        qkT_ps = sem("qkT_ps")
        qT_ready = sem("qT_ready")
        qkT_ready = sem("qkT_ready")
        score_ps = sem("score_ps")
        squared = sem("squared")
        diag = sem("diag")
        pv_done = sem("pv_done")
        yT_ready = sem("yT_ready")
        den_in = sem("den_in")
        den_inverse = sem("den_inverse")
        den_out = sem("den_out")
        spread = sem("spread")
        y_group = sem("y_group")
        y_pair = sem("y_pair")
        den_ready = sem("den_ready")
        rden_ready = sem("rden_ready")
        y_tile = sem("y_tile")
        y_ready = sem("y_ready")
        ao_ps = sem("ao_ps")
        ao_ready = sem("ao_ready")
        passed_pool = sem("passed_pool")
        passed_dve = sem("passed_dve")

        consts = [(wqk_s[:, :, :], wqk), (wv_s[:, :, :], wv), (wo_s[:, :, :], wo), (id_s[:, :], ident),
                  (idb_s[:, :], ident_bf), (causal_s[:, :], causal), (earlier_s[:, :], earlier), (eps_s[:, :], eps_rows),
                  (keep_s[:, :], keep_rows)]
        CONST_IN = 16 * len(consts)

        NS = len(STEPS)
        diag_no = {i: j for i, (j, h, c) in enumerate(STEPS) if j // 4 == h}
        FIRST_BANK, HEAD_BANK = [0, 1, 2, 3, 4, 5, 6, 7], [0, 0, 2, 3, 6, 7, 0, 6]
        ACT_HEADS, DVE_HEADS = (2,), (0, 1, 3, 4, 5, 6, 7)

        SAME_BANK = {1: 1, 6: 2, 7: 4}

        def head_bank(g, u):
            return ps[0:SW, HEAD_BANK[u] if g else FIRST_BANK[u], :].bitcast(BF16)

        def head_place(g, h):
            return GH if h == 0 and g % 2 else h

        LAST_STEP = [max(i for i, (j, h, c) in enumerate(STEPS) if h == half) for half in range(2)]
        EARLY_HEADS = (4, 5, 6)
        ORDER = [0, 2, 1, 3] + list(range(4, 2 * NS))

        def units_of(i):
            return ORDER.index(2 * i), ORDER.index(2 * i + 1)

        def unit_bank(n):
            return 2 + 2 * (n % 3)

        def by_parity(heads, odd):
            return heads.rearrange("p (a o h) d -> p a o h d", o=2, h=GH)[:, :, odd]

        block = ctx.enter_context(nc.Block())

        @block.sync
        def _(sp):
            def load(b):
                sp.dma_start(xs[:, :, :], x[b].rearrange("(t p) d -> p t d", p=P)).then_inc(x_in, 16)

            def invert(b, g):
                i, row = b * (GROUPS - 1) + g, ONE[g % 2]
                sp.wait_ge(yT_ready, 2 * (b * GROUPS + g) + 2)
                sp.dma_start(den_flat[:, :], yT[row:P:VP, g, :]).then_inc(den_in, 16)
                sp.wait_ge(den_inverse, i + 1)
                if g >= 1:
                    sp.wait_ge(y_group, i)
                sp.dma_start(den[row:P:VP, :], den_flat[:, :]).then_inc(den_out, 16)

            def store_xn(b):
                sp.wait_ge(xn_ready, b * TILES + TILES)
                sp.dma_start(xn_d[b].rearrange("(t p) d -> p t d", p=P), xn[:, :, :]).then_inc(stored, 16)

            def store_attn(b):
                sp.wait_ge(ao_ready, b * TILES + TILES)
                sp.dma_start(attn_d[b].rearrange("(t p) d -> p t d", p=P), ao[:, :, :]).then_inc(stored, 16)

            load(0)
            for dst, src in consts:
                sp.dma_start(dst, src).then_inc(const_in, 16)
            store_xn(0)
            load(1)
            for dst, src in later:
                sp.dma_start(dst, src).then_inc(later_in, 16)
            with sp.Fori(0, B - 2) as b:
                for g in range(GROUPS - 1):
                    invert(b, g)
                store_xn(b + 1)
                load(b + 2)
                store_attn(b)
            for b in (B - 2, B - 1):
                for g in range(GROUPS - 1):
                    invert(b, g)
                if b + 1 < B:
                    store_xn(b + 1)
                store_attn(b)
            sp.wait_ge(stored, 2 * 16 * B)
            sp.wait_ge(later_in, 16 * len(later))

        @block.gpsimd
        def _(pool):
            g = nc.gpsimd
            g.memset(mhalf[:, :], -0.5).then_inc(ones_set, 1)
            g.memset(four_s[:, :], 4.0).then_inc(ones_set, 1)
            g.memset(vals[:, :, :, :], 0.0).then_inc(ones_set, 1)
            g.memset(den[:, :], 1.0).then_inc(ones_set, 1)
            g.memset(bsum[:, :, :], 0.0).then_inc(ones_set, 1)
            pool.wait_ge(ones_set, 5)
            for h in range(TH):
                one = ONE[h // GH % 2]
                g.memset(vals[:, :, h, one:one + 1], 1.0).then_inc(ones_set, 1)
                g.memset(bsum[:, h, one:one + 1], float(P)).then_inc(ones_set, 1)

            def root(b):
                pool.wait_ge(var_ready, b + 1)
                g.tensor_tensor(rstd[:, :], ve[:, :], mhalf[:, :], ALU.pow).then_inc(rstd_ready, 1)

            def split(b):
                for t in range(TILES):
                    r = rest[:, t % 2]
                    pool.wait_ge(rest_ready, b * TILES + t + 1)
                    pool.sem_inc(passed_pool, 1)
                    g.tensor_copy(parts[:, t, 0, :, 3, :], r[:, 0]).then_inc(mid_q, 1)
                    pool.wait_ge(mid_q, b * TILES + t + 1)
                    g.tensor_tensor(parts[:, t, 0, :, 5, :], r[:, 0], parts[:, t, 0, :, 3, :], ALU.subtract).then_inc(low, 1)
                    pool.wait_ge(mid_k, b * TILES + t + 1)
                    g.tensor_tensor(parts[:, t, 1, :, 2, :], r[:, 1], parts[:, t, 1, :, 1, :], ALU.subtract).then_inc(low, 1)

            def normalise(b):
                for n in range(GROUPS - 1):
                    pool.wait_ge(spread, 2 * (b * (GROUPS - 1) + n) + 2)
                    g.tensor_tensor(yT[:, n, :], yT[:, n, :], den[:, :], ALU.mult).then_inc(y_group, 1)
                    if n == 1:
                        pool.wait_ge(y_group, b * (GROUPS - 1) + 2)
                        g.tensor_tensor(yT[:, 1, :], yT[:, 0, :], yT[:, 1, :], ALU.add).then_inc(y_pair, 1)
                    if n == 0 and (not isinstance(b, int) or b + 1 < B):
                        root(b + 1)

            root(0)
            split(0)
            with pool.Fori(0, B - 1) as b:
                normalise(b)
                split(b + 1)
            normalise(B - 1)

        @block.vector
        def _(dve):
            v = nc.vector

            def tile_stats(b, t):
                if t == 0:
                    dve.wait_ge(x_in, 16 * b + 16)
                v.bn_stats(st[:, t, :], xs[:, t, :]).then_inc(stats, 1)

            def variances(b):
                dve.wait_ge(stats, (TILES + 1) * b + TILES)
                dve.sem_inc(passed_dve, 1)
                for t in range(TILES):
                    last = v.bn_aggr(mv[:, t, :], st[:, t, :])
                last.then_inc(stats, 1)
                dve.wait_ge(stats, (TILES + 1) * b + TILES + 1)
                v.tensor_scalar_add(ve[:, :], mv[:, :, 1], LN_EPS).then_inc(var_ready, 1)

            def layer_norm(b, t):
                if t == 0:
                    dve.wait_ge(rstd_ready, b + 1)
                    if not isinstance(b, int):
                        dve.wait_ge(stored, 16 * (2 * b - 1))
                v.tensor_scalar(xn[:, t, :], xs[:, t, :], mv[:, t, 0:1], rstd[:, t:t + 1],
                                ALU.subtract, ALU.mult).then_inc(xn_ready, 1)

            def invert_den(b, g):
                dve.wait_ge(den_in, 16 * (b * (GROUPS - 1) + g + 1))
                v.reciprocal(den_flat[:, :], den_flat[:, :]).then_inc(den_inverse, 1)

            def spread_den(b, g):
                dve.wait_ge(den_out, 16 * (b * (GROUPS - 1) + g + 1))
                dve.sem_inc(passed_dve, 1)
                v.stream_shuffle(den[:, :], den[:, :], [ONE[g % 2]] * 32).then_inc(spread, 1)
                dve.wait_ge(spread, 2 * (b * (GROUPS - 1) + g) + 1)
                v.tensor_scalar_mul(den[:, :], den[:, :], keep_s[:, g % 2:g % 2 + 1]).then_inc(spread, 1)

            def normalise(b, t):
                g, cols = GROUPS - 1, slice(t * P, (t + 1) * P)
                i, odd = b * TILES + t, g % 2
                if t == 0:
                    dve.wait_ge(yT_ready, 2 * (b * GROUPS + GROUPS))
                    dve.wait_ge(y_group, b * (GROUPS - 1) + g)
                else:
                    dve.wait_ge(y_tile, i)
                dve.sem_inc(passed_dve, 1)
                v.stream_shuffle(den[:, cols], yT[:, g, cols], [ONE[odd]] * 32).then_inc(den_ready, 1)
                dve.wait_ge(den_ready, i + 1)
                v.reciprocal(den[:, cols], den[:, cols]).then_inc(rden_ready, 1)
                dve.wait_ge(rden_ready, i + 1)
                v.scalar_tensor_tensor(yT[:, g, cols], yT[:, g, cols], keep_s[:, odd:odd + 1], den[:, cols], ALU.mult, ALU.mult)\
                    .then_inc(y_tile, 1)
                dve.wait_ge(y_tile, i + 1)
                v.tensor_tensor(yT[:, g, cols], yT[:, g - 1, cols], yT[:, g, cols], ALU.add).then_inc(y_ready, 1)

            def repeat(b, t):
                dve.wait_ge(low, 2 * (b * TILES + t + 1))
                v.tensor_copy(parts[:, t, 1, :, 3:5, :], parts[:, t, 1, :, 0:2, :]).then_inc(copies, 1)
                v.tensor_copy(parts[:, t, 1, :, 5, :], parts[:, t, 1, :, 0, :]).then_inc(copies, 1)
                v.tensor_copy(parts[:, t, 0, :, 4, :], parts[:, t, 0, :, 3, :]).then_inc(copies, 1)

            def project(b, last=None):
                if last is not None:
                    for t in range(LEAD):
                        normalise(last, t)
                for t in range(TILES):
                    if t == TILES - 1:
                        dve.wait_ge(xnT_ready, b * TILES + TILES)
                        v.reduce_sum(xsum[:, :, :], xnT[:, :, :].rearrange("p c (t n) -> p c t n", n=P), AX).then_inc(xsum_ready, 1)
                    dve.wait_ge(high, b * TILES + t + 1)
                    if t >= 2:
                        dve.wait_ge(low, 2 * (b * TILES + t - 1))
                    v.tensor_tensor(rest[:, t % 2], ps[:, 4 + t % 2, :].rearrange("p (a h d) -> p a h d", a=2, h=TH),
                                    parts[:, t, :, :, 0, :], ALU.subtract).then_inc(rest_ready, 1)
                    dve.wait_ge(rest_ready, b * TILES + t + 1)
                    dve.sem_inc(passed_dve, 1)
                    v.tensor_copy(parts[:, t, 1, :, 1, :], rest[:, t % 2, 1]).then_inc(mid_k, 1)
                    if last is not None and t + LEAD < TILES:
                        normalise(last, t + LEAD)
                    if t >= 2:
                        repeat(b, t - 2)
                repeat(b, TILES - 2)
                repeat(b, TILES - 1)

            def attention(b, following):
                def copy_heads(g, us):
                    for u in us:
                        dve.wait_ge(qkT_ps, (b * GROUPS + g) * 2 * GH + u + 1)
                        v.tensor_copy(qkT[:, u % 2, head_place(g, u // 2), :], head_bank(g, u)).then_inc(qkT_ready, 1)

                def add_before(g, half):
                    tiles = slice(half * TILES // 2, (half + 1) * TILES // 2)
                    if g == 0 and half == 0:
                        dve.wait_ge(before_ready, b + 1)
                    dve.wait_ge(pv_done, (b * GROUPS + g) * NS + LAST_STEP[half] + 1)
                    v.tensor_tensor(yT[:, g, half * 512:(half + 1) * 512].rearrange("p (t n) -> p t n", n=P),
                                    ps[:, half, :].rearrange("p (t n) -> p t n", n=P),
                                    before[:, g, tiles].unsqueeze(2).to_broadcast([P, TILES // 2, P]), ALU.add).then_inc(yT_ready, 1)

                copy_heads(0, DVE_HEADS)
                for g in range(GROUPS):
                    for i, t in diag_no.items():
                        c = STEPS[i][2]
                        a = weights[:, 4 * i % (2 * UNITS):4 * i % (2 * UNITS) + GH, c:c + P]
                        if t == TILES - 1 and g + 1 < GROUPS:
                            copy_heads(g + 1, DVE_HEADS[len(EARLY_HEADS):])
                        dve.wait_ge(squared, (b * GROUPS + g) * 2 * NS + max(units_of(i)) + 1)
                        v.scalar_tensor_tensor(a, a, 16.0, causal_s[:, :].unsqueeze(1).to_broadcast([P, GH, P]),
                                               ALU.add, ALU.mult).then_inc(diag, 1)
                        if g >= 1 and t == 1:
                            invert_den(b, g - 1)
                        if g >= 1 and t == 3:
                            spread_den(b, g - 1)
                        if following is not None and t < TILES // 2:
                            if g == 0:
                                tile_stats(following, 2 * t)
                                tile_stats(following, 2 * t + 1)
                            if g == 1 and t == 0:
                                variances(following)
                            if g >= 2:
                                layer_norm(following, (g - 2) * TILES // 2 + t)
                        if t == TILES // 2 - 1:
                            add_before(g, 0)
                        if t in EARLY_HEADS and g + 1 < GROUPS:
                            copy_heads(g + 1, (DVE_HEADS[EARLY_HEADS.index(t)],))
                    add_before(g, 1)

            for t in range(TILES):
                tile_stats(0, t)
            variances(0)
            for t in range(TILES):
                layer_norm(0, t)
            dve.wait_ge(const_in, CONST_IN)
            project(0)
            with dve.Fori(0, B - 1) as b:
                attention(b, b + 1)
                project(b + 1, b)
            attention(B - 1, None)
            for t in range(TILES):
                normalise(B - 1, t)

        @block.scalar
        def _(act):
            a = nc.scalar
            act.wait_ge(const_in, CONST_IN)
            act.wait_ge(ones_set, 5 + 2 * TH)

            def copy_xT(b, t):
                act.wait_ge(xnT_ps, b * TILES + t + 1)
                a.activation(xnT[:, :, t * P:(t + 1) * P], ps[:, 2 + t % 2, 0:KC * P].rearrange("p (c n) -> p c n", c=KC),
                             ACT.Copy).then_inc(xnT_ready, 1)

            def copy_out(b, t):
                if t == 0 and isinstance(b, int):
                    act.wait_ge(stored, 16 * (2 * b + 1))
                elif t == 0:
                    act.wait_ge(stored, 16 * (2 * b + 2))
                act.wait_ge(ao_ps, b * TILES + t + 1)
                a.activation(ao[:, t, :], ps[:, t % 2, 0:DIM], ACT.Copy).then_inc(ao_ready, 1)

            def project(b, last=None):
                copy_xT(b, 0)
                for t in range(TILES):
                    if t + 1 < TILES:
                        copy_xT(b, t + 1)
                    act.wait_ge(proj_ps, b * TILES + t + 1)
                    qk = ps[:, 4 + t % 2, :].rearrange("p (a h d) -> p a h d", a=2, h=TH)
                    a.activation(parts[:, t, 0, :, 0:3, :], qk[:, 0].unsqueeze(2).to_broadcast([P, TH, 3, TD]), ACT.Copy)
                    a.activation(parts[:, t, 1, :, 0, :], qk[:, 1], ACT.Copy).then_inc(high, 1)
                    for odd in range(2):
                        last_copy = a.activation(by_parity(vals[:, t], odd)[:, :, :, VALUES[odd]],
                                                 by_parity(ps[:, 6 + t % 2, 0:TH * TD].rearrange("p (h d) -> p h d", h=TH), odd), ACT.Copy)
                    last_copy.then_inc(v_ready, 1)
                    if last is not None and t >= LAG:
                        copy_out(last, t - LAG)
                if last is not None:
                    for t in range(TILES - LAG, TILES):
                        copy_out(last, t)

            def attention(b):
                for g in range(GROUPS):
                    for u in ACT_HEADS:
                        act.wait_ge(qkT_ps, (b * GROUPS + g) * 2 * GH + u + 1)
                        a.activation(qkT[:, u % 2, head_place(g, u // 2), :], head_bank(g, u), ACT.Copy).then_inc(qT_ready, 1)
                    for n, u in enumerate(ORDER):
                        i, c = u // 2, STEPS[u // 2][2]
                        if g == 0 and n == 2:
                            act.wait_ge(bsum_ps, b + 1)
                            for odd in range(2):
                                last = a.activation(by_parity(bsum[:, :, :], odd)[:, :, :, VALUES[odd]],
                                                    by_parity(ps[0:TILES, 0, 0:TH * TD].rearrange("p (h d) -> p h d", h=TH), odd), ACT.Copy)
                            last.then_inc(bsum_ready, 1)
                        if g == 0 and n == 4:
                            act.wait_ge(before_ps, b + 1)
                            for odd in range(2):
                                last = a.activation(before[:, odd:GROUPS:2, :],
                                                    ps[:, 1, 0:GROUPS * TILES].rearrange("p (g t) -> p g t", t=TILES)[:, odd:GROUPS:2, :],
                                                    ACT.Identity, bias=eps_s[:, odd:odd + 1])
                            last.then_inc(before_ready, 1)
                        act.wait_ge(score_ps, (b * GROUPS + g) * 2 * NS + n + 1)
                        if i >= UNITS // 2:
                            act.wait_ge(pv_done, (b * GROUPS + g) * NS + i - UNITS // 2 + 1)
                        a.activation(weights[:, 2 * (u % UNITS):2 * (u % UNITS) + 2, c:512], ps[:, unit_bank(n):unit_bank(n) + 2, c:512], ACT.Square,
                                     bias=four_s[:, :]).then_inc(squared, 1)

            project(0)
            with act.Fori(0, B - 1) as b:
                attention(b)
                project(b + 1, b)
            attention(B - 1)
            for t in range(TILES):
                copy_out(B - 1, t)

        @block.tensor
        def _(pe):
            mm, tr = nc.tensor.matmul, nc.tensor.transpose
            pe.wait_ge(const_in, CONST_IN)

            def x_T(b, t):
                pe.wait_ge(xn_ready, b * TILES + t + 1)
                if t >= 2:
                    pe.wait_ge(xnT_ready, b * TILES + t - 1)
                for c in range(KC):
                    last = tr(ps[:, 2 + t % 2, c * P:(c + 1) * P], xn[:, t, c * P:(c + 1) * P], id_s[:, :])
                last.then_inc(xnT_ps, 1)

            def out_project(b, t):
                if t == 0:
                    pe.wait_ge(y_pair, b + 1)
                pe.wait_ge(y_ready, b * TILES + t + 1)
                if t >= 2:
                    pe.wait_ge(ao_ready, b * TILES + t - 1)
                for n in range(GROUPS // 2):
                    last = mm(ps[:, t % 2, 0:DIM], yT[:, 2 * n + 1, t * P:(t + 1) * P], wo_s[:, n, :], start=(n == 0), stop=(n == GROUPS // 2 - 1))
                last.then_inc(ao_ps, 1)

            def project(b, last_b=None):
                x_T(b, 0)
                for t in range(TILES):
                    if t + 1 < TILES:
                        x_T(b, t + 1)
                    pe.wait_ge(xnT_ready, b * TILES + t + 1)
                    if t >= 2:
                        pe.wait_ge(rest_ready, b * TILES + t - 1)
                        pe.wait_ge(v_ready, b * TILES + t - 1)
                    for c in range(KC):
                        mm(ps[:, 4 + t % 2, :], xnT[:, c, t * P:(t + 1) * P], wqk_s[:, c, :], start=(c == 0), stop=(c == KC - 1))
                    for c in range(KC):
                        last = mm(ps[:, 6 + t % 2, 0:TH * TD], xnT[:, c, t * P:(t + 1) * P], wv_s[:, c, :], start=(c == 0), stop=(c == KC - 1))
                    last.then_inc(proj_ps, 1)
                    if last_b is not None and t >= LAG:
                        out_project(last_b, t - LAG)
                if last_b is not None:
                    for t in range(TILES - LAG, TILES):
                        out_project(last_b, t)
                    pe.wait_ge(ao_ready, last_b * TILES + TILES)

            def tile_sums(b):
                pe.wait_ge(xsum_ready, b + 1)
                for c in range(KC):
                    last = mm(ps[0:TILES, 0, 0:TH * TD], xsum[:, c, :], wv_s[:, c, :], start=(c == 0), stop=(c == KC - 1))
                last.then_inc(bsum_ps, 1)

            def sums_before(b):
                pe.wait_ge(bsum_ready, b + 1)
                for g in range(GROUPS):
                    last = mm(ps[:, 1, g * TILES:(g + 1) * TILES], bsum[:, g * GH:(g + 1) * GH, :].rearrange("p h d -> p (h d)"),
                              earlier_s[:, :], start=True, stop=True)
                last.then_inc(before_ps, 1)

            def attention(b):
                pe.wait_ge(copies, 3 * TILES * (b + 1))
                pe.wait_ge(v_ready, b * TILES + TILES)
                for g in range(GROUPS):
                    following = g + 1 < GROUPS

                    def heads_T(g, us):
                        for u in us:
                            if g >= 1 and u in SAME_BANK:
                                pe.wait_ge(qkT_ready, (b * GROUPS + g) * len(DVE_HEADS) + SAME_BANK[u])
                            for t in range(TILES):
                                last = tr(head_bank(g, u)[:, t * P:(t + 1) * P],
                                          parts[:, t, u % 2, g * GH + u // 2].rearrange("p s d -> p (s d)"), idb_s[:, :])
                            last.then_inc(qkT_ps, 1)

                    def wait_squares(n, g=g):
                        pe.wait_ge(squared, (b * GROUPS + g) * 2 * NS + n + 1)

                    def scores(n, g=g):
                        u = ORDER[n]
                        j, half, c = STEPS[u // 2]
                        if n >= 3:
                            wait_squares(n - 3, g)
                        elif n == 0:
                            pe.wait_ge(qkT_ready, (b * GROUPS + g) * len(DVE_HEADS) + 3)
                            pe.wait_ge(qT_ready, (b * GROUPS + g) * len(ACT_HEADS) + 1)
                        elif n == 1 and g == 0:
                            pe.wait_ge(qkT_ready, (b * GROUPS + g) * len(DVE_HEADS) + 5)
                        elif n == 2:
                            pe.wait_ge(qkT_ready, (b * GROUPS + g) * len(DVE_HEADS) + len(DVE_HEADS))
                        for k in range(2):
                            place = head_place(g, 2 * (u % 2) + k)
                            last = mm(ps[:, unit_bank(n) + k, c:512], qkT[:, 1, place, j * P:(j + 1) * P],
                                      qkT[:, 0, place, half * 512 + c:(half + 1) * 512], start=True, stop=True)
                        last.then_inc(score_ps, 1)

                    def attend(i, g=g):
                        j, half, c = STEPS[i]
                        if i == 0 and g == 0:
                            pe.wait_ge(before_ready, b + 1)
                        if i == 0 and g >= 1:
                            pe.wait_ge(yT_ready, 2 * (b * GROUPS + g))
                        wait_squares(max(units_of(i)), g)
                        if i in diag_no:
                            pe.wait_ge(diag, (b * GROUPS + g) * TILES + diag_no[i] + 1)
                        for h in range(GH):
                            last = mm(ps[h * VP:(h + 1) * VP, half, c:512], vals[:, j, g * GH + h, :],
                                      weights[:, 4 * i % (2 * UNITS) + h, c:512], start=(j == 0), stop=(j == 4 * half + 3),
                                      skip_group_check=True)
                        last.then_inc(pv_done, 1)

                    if g == 0:
                        heads_T(0, range(7))
                        scores(0)
                        scores(1)
                        heads_T(0, (7,))
                        tile_sums(b)
                    scores(2)
                    if g >= 1:
                        attend(NS - 1, g - 1)
                    for i in range(NS - 1):
                        if 2 * i + 3 < 2 * NS:
                            scores(2 * i + 3)
                        if g == 0 and i == 1:
                            sums_before(b)
                        if following and i == NS - 2:
                            wait_squares(2 * NS - 3)
                            heads_T(g + 1, (2, 3))
                        if i >= 1:
                            attend(i - 1)
                        if 2 * i + 4 < 2 * NS:
                            scores(2 * i + 4)
                        if following and i == NS - 4:
                            pe.wait_ge(yT_ready, 2 * (b * GROUPS + g) + 1)
                        if following and NS - 4 <= i < NS - 2:
                            heads_T(g + 1, (i - (NS - 4),))
                    if following:
                        wait_squares(2 * NS - 1)
                        heads_T(g + 1, (4,))
                        scores(0, g + 1)
                        heads_T(g + 1, (5, 6, 7))
                    attend(NS - 2)
                    if following:
                        scores(1, g + 1)
                    else:
                        attend(NS - 1)

            project(0)
            with pe.Fori(0, B - 1) as b:
                attention(b)
                project(b + 1, b)
            attention(B - 1)
            for t in range(TILES):
                out_project(B - 1, t)


def taylor_constants():
    k = np.arange(P)
    t = np.arange(TILES)
    causal = (k[:, None] <= k[None, :]).astype(np.float32)
    earlier = 16.0 * (t[:, None] < t[None, :])
    one = np.stack([k % VP == row for row in ONE], 1)
    return causal, earlier.astype(np.float32), np.where(one, TEPS, 0.0).astype(np.float32), np.where(one, 0.0, 1.0).astype(np.float32)




def transformer_block(nc, PAIRS, x, xn_d, attn_d, wqkv_s, wo, w1, b1, w2, ln, qk_scale, rotary, masks, ident, shift,
                      carry_row, out):
    with ExitStack() as ctx:
        def sb(name, shape, dt=F32):
            return ctx.enter_context(nc.sbuf_tensor(name, shape, dt))

        def sem(name):
            return ctx.enter_context(nc.semaphore("f_" + name))

        def sems(name):
            return [sem(f"{name}{s}") for s in range(2)]

        ps = ctx.enter_context(nc.psum_tensor("f_ps", [P, 8, 512], F32))

        def bank(s, i):
            return ps[:, 4 * s + i, :]

        wo_s = sb("fwo_s", [P, LAYERS, INNER // P, DIM])
        w1_s = sb("w1_s", [P, LAYERS, KC, 2, HID])
        b1_s = sb("b1_s", [P, LAYERS, 2, FB])
        w2_s = sb("w2_s", [P, LAYERS, FB, DIM])
        ln_s = sb("ln_s", [P, LAYERS, 2, KC])
        qks_s = sb("qks_s", [P, LAYERS, 2, 2, HD])
        id_s = sb("f_id", [P, P])
        shift_s = sb("shift_s", [P, P])
        carry_s = sb("carry_s", [P, P])
        rot = sb("rot", [P, TILES, LAYERS, 2, 2, HD])
        masks_s = sb("masks_s", [P, TILES, 2 * P + 1])
        mhalf = sb("f_mhalf", [P, 2 * HEADS])

        def each(name, shape):
            return [[sb(f"{name}{s}{l}", shape) for l in range(LAYERS)] for s in range(2)]

        def both(name, shape):
            return [sb(f"{name}{s}", shape) for s in range(2)]

        mask = both("mask", [P, 2 * P + 1])
        xin = both("xin", [P, DIM])
        xres = both("xres", [P, 2, DIM])
        hT = each("hT", [P, 1 + 2 * P])
        kT = each("kT", [P, HEADS // 2, 2 * P])
        vw = each("vw", [P, 2, INNER])
        x1 = each("x1", [P, DIM])
        xmid = both("xmid", [P, DIM])
        yout = both("yout", [P, DIM])
        carry = each("carry", [P, P])
        qk = both("qk", [P, 2 * HEADS, HD])
        work = both("work", [P, 2, 2 * HEADS, HD])
        cosine = [work[s][:, 0] for s in range(2)]
        turned = [work[s][:, 1] for s in range(2)]
        pT = [work[s][:, :, :, :].rearrange("p a h d -> p (a h d)").rearrange("p (i n) -> p i n", n=P) for s in range(2)]
        ssq = both("ssq", [P, 2 * HEADS])
        rnorm = both("rnorm", [P, 2 * HEADS])
        qT = both("qT", [P, HEADS // 2, P])
        pr = both("pr", [P, HEADS, 2 * P])
        sq = [pr[s][:, :, :].rearrange("p h n -> p (h n)")[:, 0:2 * INNER].rearrange("p (h d) -> p h d", d=HD) for s in range(2)]
        tab = pr[0][:, :, :].rearrange("p t (a b d) -> p t a b d", a=2, b=2)
        nmax = both("nmax", [P, HEADS])
        psum = both("psum", [P, HEADS])
        rsum = both("rsum", [P, HEADS])
        oT = both("oT", [P, INNER // P, P])
        st = both("st", [P, 2, 6])
        mv = both("mv", [P, 2])
        ve = both("ve", [P, 1])
        rstd = both("rstd", [P, 1])
        hn = [qk[s][:, :, :].rearrange("p h d -> p (h d)")[:, FB * P:FB * P + DIM] for s in range(2)]
        hnT = both("hnT", [P, KC, P])
        gate = [qk[s][:, :, :].rearrange("p h d -> p (h d)")[:, 0:FB * P].rearrange("p (j n) -> p j n", n=P) for s in range(2)]
        act_u = both("act_u", [P, FB, P])
        xb = both("xb", [P, DIM])

        first_in = sem("first_in")
        rest_in = sem("rest_in")
        init = sem("init")
        rot_ready = sem("rot_ready")
        xn_in = sems("xn_in")
        res_in = sems("res_in")
        y_out = sems("y_out")
        mask_set = sems("mask_set")
        kept = sems("kept")
        xT_ps = sems("xT_ps")
        edge = sems("edge")
        hT_ready = sems("hT_ready")
        k_ps = sems("k_ps")
        q_ps = sems("q_ps")
        v_ps = sems("v_ps")
        k_ready = sems("k_ready")
        q_ready = sems("q_ready")
        v_ready = sems("v_ready")
        sq_ready = sems("sq_ready")
        ssq_ready = sems("ssq_ready")
        knorm_ready = sems("knorm_ready")
        qnorm_ready = sems("qnorm_ready")
        turn = sems("turn")
        cosd = sems("cosd")
        q_rotated = sems("q_rotated")
        unit = sems("unit")
        qT_ps = sems("qT_ps")
        kT_ps = sems("kT_ps")
        qT_ready = sems("qT_ready")
        kT_ready = sems("kT_ready")
        score_ps = sems("score_ps")
        masked = sems("masked")
        nmax_ready = sems("nmax_ready")
        exped = sems("exped")
        rsum_ready = sems("rsum_ready")
        prob = sems("prob")
        pT_ps = sems("pT_ps")
        pT_act = sems("pT_act")
        pT_dve = sems("pT_dve")
        oT_ps = sems("oT_ps")
        oT_ready = sems("oT_ready")
        wo_ps = sems("wo_ps")
        x1_ready = sems("x1_ready")
        shift_ps = sems("shift_ps")
        stats = sems("stats")
        var_ready = sems("var_ready")
        rstd_ready = sems("rstd_ready")
        hn_ready = sems("hn_ready")
        hnT_ps = sems("hnT_ps")
        hnT_ready = sems("hnT_ready")
        up_ps = sems("up_ps")
        gate_ready = sems("gate_ready")
        u_ready = sems("u_ready")
        xb_ready = sems("xb_ready")
        down_ps = sems("down_ps")
        x2_ready = sems("x2_ready")
        passed_pool = sem("passed_pool")
        passed_dve = sem("passed_dve")

        first = [(tab[:, :, :, :, :], rotary), (qks_s[:, :, :, :, :], qk_scale.partition_broadcast(P)), (masks_s[:, :, :], masks),
                 (id_s[:, :], ident)]
        rest = [(wo_s[:, :, :, :], wo), (shift_s[:, :], shift), (carry_s[:, :], carry_row), (ln_s[:, :, :, :], ln), (w1_s[:, :, :, :, :], w1),
                (b1_s[:, :, :, :], b1), (w2_s[:, :, :, :], w2)]
        FIRST_IN, REST_IN = 16 * len(first), 16 * len(rest)
        INIT = 2 + 1 + 8 * LAYERS
        N_ROT = TILES * LAYERS

        STREAMS = range(2)
        PAIRS_OF_HEADS = [(0, 2), (1, 3), (4, 6), (5, 7)]
        STEPS = LAYERS * PAIRS * TILES
        block = ctx.enter_context(nc.Block())

        def rows_of(s, it):
            return bass.ds(it * P + s * PAIRS * SEQ, P)

        def before(step):
            n, l, it = step
            return n - 1, 1 - l, it if l else it - 1

        def after(step):
            n, l, it = step
            return n + 1, 1 - l, it + 1 if l else it

        def is_zero(count):
            return isinstance(count, int) and count == 0

        def run(eng, start, half, end):
            first, last = (0, 0, 0), (STEPS - 1, 1, STEPS // LAYERS - 1)

            def both_halves(step, last=False):
                half(0, step, 1, before(step), True)
                half(1, step, 0, step, not last)

            start(first)
            half(0, first, 1, None, False)
            eng.wait_ge(rest_in, REST_IN)
            half(1, first, 0, first, True)
            with eng.Fori(0, STEPS // LAYERS - 1) as i:
                both_halves((LAYERS * i + 1, 1, i))
                both_halves((LAYERS * i + 2, 0, i + 1))
            both_halves(last, last=True)
            end(last)

        x_rows, xn_rows, attn_rows, out_rows = [d.rearrange("b t d -> (b t) d") for d in (x, xn_d, attn_d, out)]

        @block.sync
        def _(sp):
            def load_xn(s, it):
                sp.dma_start(xin[s][:, :], xn_rows[rows_of(s, it), :]).then_inc(xn_in[s], 16)

            def load_residual(s, it):
                sp.dma_start(xres[s][:, 0, :], x_rows[rows_of(s, it), :]).then_inc(res_in[s], 16)
                sp.dma_start(xres[s][:, 1, :], attn_rows[rows_of(s, it), :]).then_inc(res_in[s], 16)

            def store(s, it):
                sp.wait_ge(x2_ready[s], LAYERS * it + LAYERS)
                sp.dma_start(out_rows[rows_of(s, it), :], yout[s][:, :]).then_inc(y_out[s], 16)

            for s in STREAMS:
                load_xn(s, 0)
            for dst, src in first:
                sp.dma_start(dst, src).then_inc(first_in, 16)
            for dst, src in rest:
                sp.dma_start(dst, src).then_inc(rest_in, 16)
            for s in STREAMS:
                load_residual(s, 0)
            with sp.Fori(0, STEPS // LAYERS - 1) as it:
                for s in STREAMS:
                    sp.wait_ge(x1_ready[s], LAYERS * it + 1)
                    load_xn(s, it + 1)
                for s in STREAMS:
                    sp.wait_ge(xb_ready[s], 2 * it + 2)
                    load_residual(s, it + 1)
                    store(s, it)
            for s in STREAMS:
                store(s, STEPS // LAYERS - 1)
                sp.wait_ge(y_out[s], 16 * (STEPS // LAYERS))

        @block.gpsimd
        def _(pool):
            g = nc.gpsimd
            g.memset(mhalf[:, :], -0.5).then_inc(init, 1)
            for l in range(LAYERS):
                for s in STREAMS:
                    g.memset(hT[s][l][:, :], 0.0).then_inc(init, 1)
                    g.memset(kT[s][l][:, :, :], 0.0).then_inc(init, 1)
                    g.memset(vw[s][l][:, :, :], 0.0).then_inc(init, 1)
                    g.memset(x1[s][l][:, :], 0.0).then_inc(init, 1)
            for s in STREAMS:
                g.memset(act_u[s][:, FB - 1, :], 1.0).then_inc(init, 1)
            pool.wait_ge(init, INIT)
            pool.wait_ge(rot_ready, N_ROT)

            def keep(s, step):
                n, l, it = step
                pool.wait_ge(mask_set[s], it + 1)
                if not is_zero(n):
                    pool.wait_ge(shift_ps[s], n)
                pool.sem_inc(passed_pool, 1)
                g.tensor_copy(kT[s][l][:, :, 0:P], kT[s][l][:, :, P:2 * P]).then_inc(kept[s], 1)
                g.tensor_copy(vw[s][l][:, 0, :], vw[s][l][:, 1, :]).then_inc(kept[s], 1)
                g.tensor_scalar(carry[s][l][:, :], x1[s][l][:, P:DIM], mask[s][:, 2 * P:2 * P + 1], None, ALU.mult).then_inc(kept[s], 1)

            def turn_part(s, step, a, ready):
                n, l, it = step
                t = it % TILES
                heads = slice(a * HEADS, a * HEADS + HEADS)
                pool.wait_ge(ready[s], n + 1)
                pool.sem_inc(passed_pool, 1)
                for half in range(2):
                    f, z = slice(half * 32, half * 32 + 32), slice(32 - half * 32, 64 - half * 32)
                    sines = rot[:, bass.ds(t, 1), l, 1, a, f].to_broadcast([P, HEADS, 32])
                    g.tensor_tensor(turned[s][:, heads, f], qk[s][:, heads, z], sines, ALU.mult).then_inc(turn[s], 1)

            def norms(s, step, a, ready):
                n, l, it = step
                heads = slice(a * HEADS, a * HEADS + HEADS)
                pool.wait_ge(ssq_ready[s], 4 * n + 4 - 2 * a)
                g.tensor_tensor(rnorm[s][:, heads], ssq[s][:, heads], mhalf[:, heads], ALU.pow).then_inc(ready[s], 1)

            def ln_root(s, step):
                n, l, it = step
                pool.wait_ge(var_ready[s], n + 1)
                g.tensor_tensor(rstd[s][:, :], ve[s][:, :], mhalf[:, 0:1], ALU.pow).then_inc(rstd_ready[s], 1)

            def residual(s, step):
                n, l, it = step
                pool.wait_ge(res_in[s], 32 * it + 32)
                g.tensor_tensor(xres[s][:, 0, :], xres[s][:, 0, :], xres[s][:, 1, :], ALU.add).then_inc(xb_ready[s], 1)
                pool.wait_ge(xb_ready[s], 2 * it + 1)
                pool.wait_ge(x1_ready[s], n + 1)
                g.tensor_tensor(xb[s][:, :], xres[s][:, 0, :], x1[s][l][:, :], ALU.add).then_inc(xb_ready[s], 1)

            def half(x, xs, y, ys, t):
                turn_part(x, xs, 1, k_ready)
                norms(x, xs, 1, knorm_ready)
                turn_part(x, xs, 0, q_ready)
                norms(x, xs, 0, qnorm_ready)
                if ys:
                    ln_root(y, ys)
                    if ys[1] == LAYERS - 1:
                        residual(y, ys)
                    if t:
                        keep(y, after(ys))

            def start(step):
                for s in STREAMS:
                    keep(s, step)

            def end(step):
                ln_root(1, step)
                residual(1, step)

            run(pool, start, half, end)

        @block.vector
        def _(dve):
            v = nc.vector
            dve.wait_ge(first_in, FIRST_IN)
            for t in range(TILES):
                for l in range(LAYERS):
                    v.tensor_tensor(rot[:, t, l].rearrange("p a b d -> p (a b d)"), tab[:, t].rearrange("p a b d -> p (a b d)"),
                                    qks_s[:, l].rearrange("p a b d -> p (a b d)"), ALU.mult).then_inc(rot_ready, 1)
            dve.wait_ge(rot_ready, N_ROT)
            dve.wait_ge(init, INIT)

            def set_mask(s, step):
                n, l, it = step
                if not is_zero(n):
                    dve.wait_ge(kept[s], 3 * n)
                    dve.wait_ge(edge[s], n)
                    dve.sem_inc(passed_dve, 1)
                v.tensor_copy(mask[s][:, :], masks_s[:, bass.ds(it % TILES, 1), :].rearrange("p o n -> p (o n)")).then_inc(mask_set[s], 1)

            def cosines_and_sums(s, step, a, ready):
                n, l, it = step
                i = 2 * n + 2 - a
                heads = slice(a * HEADS, a * HEADS + HEADS)
                cosines = rot[:, bass.ds(it % TILES, 1), l, 0, a, :].to_broadcast([P, HEADS, HD])
                dve.wait_ge(ready[s], n + 1)
                dve.sem_inc(passed_dve, 1)
                v.tensor_tensor(cosine[s][:, heads, :], qk[s][:, heads, :], cosines, ALU.mult).then_inc(cosd[s], 1)
                dve.wait_ge(sq_ready[s], i)
                v.reduce_sum(ssq[s][:, heads], sq[s][:, heads, :], AX).then_inc(ssq_ready[s], 1)
                dve.wait_ge(ssq_ready[s], 2 * i - 1)
                v.tensor_scalar_max(ssq[s][:, heads], ssq[s][:, heads], 1e-24).then_inc(ssq_ready[s], 1)

            def rotate(s, step, a, rotated):
                n, l, it = step
                heads = slice(a * HEADS, a * HEADS + HEADS)
                dve.wait_ge(cosd[s], 2 * n + 2 - a)
                dve.wait_ge(turn[s], 4 * n + 4 - 2 * a)
                v.tensor_tensor(qk[s][:, heads, :], cosine[s][:, heads, :], turned[s][:, heads, :], ALU.add).then_inc(rotated[s], 1)

            def unit_k(s, step):
                n, l, it = step
                dve.wait_ge(unit[s], 2 * n + 1)
                dve.wait_ge(knorm_ready[s], n + 1)
                v.tensor_tensor(qk[s][:, HEADS:, :], qk[s][:, HEADS:, :], rnorm[s][:, HEADS:].unsqueeze(2).to_broadcast([P, HEADS, HD]),
                                ALU.mult).then_inc(unit[s], 1)

            def mask_scores(s, step, p):
                n, l, it = step
                heads = PAIRS_OF_HEADS[p]
                both_heads = slice(heads[0], heads[1] + 1, 2)
                dve.wait_ge(score_ps[s], n * 4 + p + 1)
                dve.sem_inc(passed_dve, 1)
                for h in heads:
                    sc = bank(s, 2 * (h % 2) + h // 4)[:, (h // 2 % 2) * 256:(h // 2 % 2) * 256 + 256]
                    last = v.tensor_tensor_reduce(out=pr[s][:, h, :], in0=sc, in1=mask[s][:, 0:2 * P], scale=1.0, scalar=-3.0e38,
                                                  op0=ALU.add, op1=ALU.max, accum_out=nmax[s][:, h:h + 1])
                last.then_inc(masked[s], 1)
                dve.wait_ge(masked[s], n * 4 + p + 1)
                if p == 0:
                    dve.wait_ge(qnorm_ready[s], n + 1)
                v.scalar_tensor_tensor(nmax[s][:, both_heads], nmax[s][:, both_heads], -1.0, rnorm[s][:, both_heads],
                                       ALU.mult, ALU.mult).then_inc(nmax_ready[s], 1)

            def sums(s, step, q):
                n, l, it = step
                four = slice(4 * q, 4 * q + 4)
                dve.wait_ge(exped[s], n * 4 + 2 * q + 2)
                v.reciprocal(rsum[s][:, four], psum[s][:, four]).then_inc(rsum_ready[s], 1)

            def normalise(s, step, q):
                n, l, it = step
                dve.wait_ge(rsum_ready[s], n * 2 + q + 1)
                for h in range(4 * q, 4 * q + 4):
                    last = v.tensor_scalar_mul(pr[s][:, h, :], pr[s][:, h, :], rsum[s][:, h:h + 1])
                    if h % 2:
                        last.then_inc(prob[s], 1)

            def copy_pT(s, step):
                n, l, it = step
                for i in range(2, 4):
                    dve.wait_ge(pT_ps[s], n * 4 + i + 1)
                    v.tensor_copy(pT[s][:, 4 * i:4 * i + 4, :].rearrange("p a n -> p (a n)"), bank(s, i)).then_inc(pT_dve[s], 1)

            def add_attention(s, step):
                n, l, it = step
                xprev = xin[s] if l == 0 else xmid[s]
                if l == 0:
                    dve.wait_ge(xn_in[s], 16 * it + 16)
                dve.wait_ge(kept[s], 3 * n + 3)
                dve.wait_ge(wo_ps[s], n + 1)
                v.tensor_tensor(x1[s][l][:, :], bank(s, 1)[:, 0:DIM], xprev[:, :], ALU.add).then_inc(x1_ready[s], 1)

            def row_statistics(s, step):
                n, l, it = step
                dve.wait_ge(x1_ready[s], n + 1)
                v.bn_stats(st[s][:, 0, :], x1[s][l][:, 0:P])
                dve.wait_ge(shift_ps[s], n + 1)
                v.bn_stats(st[s][:, 1, :], bank(s, 2)[:, 0:P]).then_inc(stats[s], 1)
                dve.wait_ge(stats[s], 2 * n + 1)
                dve.sem_inc(passed_dve, 1)
                v.bn_aggr(mv[s][:, :], st[s][:, :, :].rearrange("p a n -> p (a n)")).then_inc(stats[s], 1)
                dve.wait_ge(stats[s], 2 * n + 2)
                v.tensor_scalar_add(ve[s][:, :], mv[s][:, 1:2], LN_EPS).then_inc(var_ready[s], 1)

            def layer_norm(s, step):
                n, l, it = step
                dve.wait_ge(rstd_ready[s], n + 1)
                v.tensor_scalar(hn[s][:, 0:P], x1[s][l][:, 0:P], mv[s][:, 0:1], rstd[s][:, :], ALU.subtract, ALU.mult)
                v.tensor_scalar(hn[s][:, P:DIM], bank(s, 2)[:, 0:P], mv[s][:, 0:1], rstd[s][:, :], ALU.subtract, ALU.mult)\
                    .then_inc(hn_ready[s], 1)

            def copy_hnT(s, step):
                n, l, it = step
                dve.wait_ge(hnT_ps[s], n + 1)
                for c in range(KC):
                    last = v.tensor_scalar(hnT[s][:, c, :], bank(s, 3)[:, c * P:(c + 1) * P], ln_s[:, l, 0, c:c + 1],
                                           ln_s[:, l, 1, c:c + 1], ALU.mult, ALU.add)
                last.then_inc(hnT_ready[s], 1)

            def gated(s, step):
                n, l, it = step
                for j in range(FB):
                    rows = P if j < FB - 1 else FLAST
                    if j % 2 == 0:
                        dve.wait_ge(gate_ready[s], n * 3 + j // 2 + 1)
                    v.scalar_tensor_tensor(act_u[s][0:rows, j, :], bank(s, j // 2)[0:rows, (j % 2) * 256:(j % 2) * 256 + P],
                                           b1_s[0:rows, l, 0, j:j + 1], gate[s][0:rows, j, :], ALU.add, ALU.mult).then_inc(u_ready[s], 1)

            def add_ffn(s, step):
                n, l, it = step
                if l == 0:
                    if not is_zero(it):
                        dve.wait_ge(y_out[s], 16 * it)
                    dve.wait_ge(down_ps[s], n + 1)
                    v.tensor_tensor(xmid[s][:, :], bank(s, 3)[:, 0:DIM], x1[s][l][:, :], ALU.add).then_inc(x2_ready[s], 1)
                else:
                    dve.wait_ge(xb_ready[s], 2 * it + 2)
                    dve.wait_ge(down_ps[s], n + 1)
                    v.tensor_tensor(yout[s][:, :], bank(s, 3)[:, 0:DIM], xb[s][:, :], ALU.add).then_inc(x2_ready[s], 1)

            def half(x, xs, y, ys, t):
                if ys:
                    copy_pT(y, ys)
                cosines_and_sums(x, xs, 1, k_ready)
                rotate(x, xs, 1, unit)
                unit_k(x, xs)
                cosines_and_sums(x, xs, 0, q_ready)
                if ys:
                    add_attention(y, ys)
                rotate(x, xs, 0, q_rotated)
                if ys:
                    row_statistics(y, ys)
                    layer_norm(y, ys)
                mask_scores(x, xs, 0)
                mask_scores(x, xs, 1)
                if ys:
                    copy_hnT(y, ys)
                mask_scores(x, xs, 2)
                mask_scores(x, xs, 3)
                sums(x, xs, 0)
                normalise(x, xs, 0)
                sums(x, xs, 1)
                if ys:
                    gated(y, ys)
                normalise(x, xs, 1)
                if ys:
                    if t and ys[1]:
                        set_mask(y, after(ys))
                    add_ffn(y, ys)

            def start(step):
                for s in STREAMS:
                    set_mask(s, step)

            def end(step):
                copy_pT(1, step)
                add_attention(1, step)
                row_statistics(1, step)
                layer_norm(1, step)
                copy_hnT(1, step)
                gated(1, step)
                add_ffn(1, step)

            run(dve, start, half, end)

        @block.scalar
        def _(act):
            a = nc.scalar
            act.wait_ge(first_in, FIRST_IN)
            act.wait_ge(init, INIT)
            act.wait_ge(rot_ready, N_ROT)

            def copy_edge(s, step):
                n, l, it = step
                act.wait_ge(mask_set[s], it + 1)
                a.activation(hT[s][l][:, 0:1], hT[s][l][:, P:P + 1], ACT.Copy, scale=mask[s][:, 2 * P:2 * P + 1]).then_inc(edge[s], 1)

            def copy_hT(s, step):
                n, l, it = step
                act.wait_ge(edge[s], n + 1)
                act.wait_ge(xT_ps[s], n + 1)
                a.activation(hT[s][l][:, 1:1 + 2 * P], bank(s, 3)[:, 0:2 * P], ACT.Copy).then_inc(hT_ready[s], 1)

            def copy_part(s, step, i, ps_ready, ready):
                n, l, it = step
                heads = slice(i * HEADS, i * HEADS + HEADS)
                act.wait_ge(ps_ready[s], n + 1)
                a.activation(qk[s][:, heads, :].rearrange("p h d -> p (h d)"), bank(s, i), ACT.Copy).then_inc(ready[s], 1)
                act.wait_ge(ready[s], n + 1)
                a.activation(sq[s][:, heads, :], qk[s][:, heads, :], ACT.Square).then_inc(sq_ready[s], 1)

            def copy_v(s, step):
                n, l, it = step
                act.wait_ge(kept[s], 3 * n + 3)
                act.wait_ge(v_ps[s], n + 1)
                a.activation(vw[s][l][:, 1, :], bank(s, 2), ACT.Copy).then_inc(v_ready[s], 1)

            def copy_qT(s, step):
                n, l, it = step
                act.wait_ge(qT_ps[s], n + 1)
                a.activation(qT[s][:, :, :], bank(s, 3).rearrange("p (c n) -> p c n", n=P), ACT.Copy).then_inc(qT_ready[s], 1)

            def copy_kT(s, step):
                n, l, it = step
                act.wait_ge(kT_ps[s], n + 1)
                a.activation(kT[s][l][:, :, P:2 * P], bank(s, 1).rearrange("p (c n) -> p c n", n=P), ACT.Copy).then_inc(kT_ready[s], 1)

            def exps(s, step, p):
                n, l, it = step
                act.wait_ge(nmax_ready[s], n * 4 + p + 1)
                for h in PAIRS_OF_HEADS[p]:
                    last = a.activation(pr[s][:, h, :], pr[s][:, h, :], ACT.Exp, bias=nmax[s][:, h:h + 1], scale=rnorm[s][:, h:h + 1],
                                        accum_out=psum[s][:, h:h + 1])
                last.then_inc(exped[s], 1)

            def copy_pT(s, step, i):
                n, l, it = step
                act.wait_ge(pT_ps[s], n * 4 + i + 1)
                a.activation(pT[s][:, 4 * i:4 * i + 4, :].rearrange("p a n -> p (a n)"), bank(s, i), ACT.Copy).then_inc(pT_act[s], 1)

            def copy_oT(s, step):
                n, l, it = step
                act.wait_ge(oT_ps[s], n + 1)
                a.activation(oT[s][:, :, :].rearrange("p a n -> p (a n)"), bank(s, 0), ACT.Copy).then_inc(oT_ready[s], 1)

            def gelus(s, step):
                n, l, it = step
                for j in range(FB):
                    rows = P if j < FB - 1 else FLAST
                    if j % 2 == 0:
                        act.wait_ge(up_ps[s], n * 3 + j // 2 + 1)
                    last = a.activation(gate[s][0:rows, j, :], bank(s, j // 2)[0:rows, (j % 2) * 256 + P:(j % 2) * 256 + 2 * P], ACT.Gelu,
                                        bias=b1_s[0:rows, l, 1, j:j + 1])
                    if j % 2:
                        last.then_inc(gate_ready[s], 1)

            def half(x, xs, y, ys, t):
                if ys:
                    copy_pT(y, ys, 0)
                copy_hT(x, xs)
                if ys:
                    copy_pT(y, ys, 1)
                copy_part(x, xs, 1, k_ps, k_ready)
                if ys:
                    copy_oT(y, ys)
                copy_part(x, xs, 0, q_ps, q_ready)
                copy_kT(x, xs)
                copy_qT(x, xs)
                copy_v(x, xs)
                for p in range(4):
                    exps(x, xs, p)
                if ys:
                    gelus(y, ys)
                    if t:
                        copy_edge(y, after(ys))

            def start(step):
                for s in STREAMS:
                    copy_edge(s, step)

            def end(step):
                copy_pT(1, step, 0)
                copy_pT(1, step, 1)
                copy_oT(1, step)
                gelus(1, step)

            run(act, start, half, end)

        @block.tensor
        def _(pe):
            mm, tr = nc.tensor.matmul, nc.tensor.transpose
            pe.wait_ge(first_in, FIRST_IN)
            pe.wait_ge(init, INIT)

            def x_T(s, step):
                n, l, it = step
                xprev = xin[s] if l == 0 else xmid[s]
                if l == 0:
                    pe.wait_ge(xn_in[s], 16 * it + 16)
                if not is_zero(n):
                    pe.wait_ge(x2_ready[s], n)
                tr(bank(s, 3)[:, 0:P], xprev[:, P:DIM], id_s[:, :])
                tr(bank(s, 3)[:, P:2 * P], xprev[:, 0:P], id_s[:, :]).then_inc(xT_ps[s], 1)

            def project(s, step, i, done, chunks=(0, 1)):
                n, l, it = step
                pe.wait_ge(hT_ready[s], n + 1)
                for c in chunks:
                    rows = hT[s][l][:, 0:P] if c else hT[s][l][:, P + 1:2 * P + 1]
                    last = mm(bank(s, i), rows, wqkv_s[:, l, c, i * INNER:(i + 1) * INNER], start=(c == 0), stop=(c == KC - 1))
                if c == KC - 1:
                    last.then_inc(done[s], 1)

            def heads_T(s, step, i, b, done):
                n, l, it = step
                if i == 0:
                    pe.wait_ge(q_rotated[s], n + 1)
                else:
                    pe.wait_ge(unit[s], 2 * n + 2)
                for h in range(0, HEADS, 2):
                    last = tr(bank(s, b)[:, h // 2 * P:(h // 2 + 1) * P],
                              qk[s][:, i * HEADS + h:i * HEADS + h + 2, :].rearrange("p h d -> p (h d)"), id_s[:, :])
                last.then_inc(done[s], 1)

            def scores(s, step, p):
                n, l, it = step
                if p == 0:
                    pe.wait_ge(qT_ready[s], n + 1)
                    pe.wait_ge(kT_ready[s], n + 1)
                if p == 1:
                    pe.wait_ge(v_ready[s], n + 1)
                for h in PAIRS_OF_HEADS[p]:
                    r = slice(h % 2 * HD, h % 2 * HD + HD)
                    last = mm(bank(s, 2 * (h % 2) + h // 4)[:, (h // 2 % 2) * 256:(h // 2 % 2) * 256 + 256], qT[s][r, h // 2, :],
                              kT[s][l][r, h // 2, :], start=True, stop=True)
                last.then_inc(score_ps[s], 1)

            def prob_T(s, step, q):
                n, l, it = step
                pe.wait_ge(masked[s], n * 4 + 4)
                for h in range(4 * q, 4 * q + 4):
                    if h % 2 == 0:
                        pe.wait_ge(prob[s], n * 4 + h // 2 + 1)
                    for half in range(2):
                        i = 2 * h + half
                        last = tr(bank(s, i // 4)[:, (i % 4) * P:(i % 4 + 1) * P], pr[s][:, h, half * P:(half + 1) * P], id_s[:, :])
                    if h % 2:
                        last.then_inc(pT_ps[s], 1)

            def attend(s, step):
                n, l, it = step
                for i in range(HEADS // 2):
                    if i < 2:
                        pe.wait_ge(pT_act[s], n * 2 + i + 1)
                    else:
                        pe.wait_ge(pT_dve[s], n * 2 + i - 1)
                    for half in range(2):
                        for k in range(2):
                            h = 2 * i + k
                            last = mm(bank(s, 0)[k * HD:(k + 1) * HD, i * P:(i + 1) * P], vw[s][l][:, half, h * HD:(h + 1) * HD],
                                      pT[s][:, 2 * h + half, :], start=(half == 0), stop=(half == 1))
                last.then_inc(oT_ps[s], 1)

            def out_project(s, step):
                n, l, it = step
                pe.wait_ge(oT_ready[s], n + 1)
                for c in range(INNER // P):
                    last = mm(bank(s, 1)[:, 0:DIM], oT[s][:, c, :], wo_s[:, l, c, :], start=(c == 0), stop=(c == INNER // P - 1))
                last.then_inc(wo_ps[s], 1)

            def shift_x1(s, step):
                n, l, it = step
                pe.wait_ge(kept[s], 3 * n + 3)
                pe.wait_ge(x1_ready[s], n + 1)
                mm(bank(s, 2)[:, 0:P], shift_s[:, :], x1[s][l][:, P:DIM], start=True, stop=False)
                mm(bank(s, 2)[:, 0:P], carry_s[96:P, :], carry[s][l][96:P, :], start=False, stop=True).then_inc(shift_ps[s], 1)

            def hn_T(s, step):
                n, l, it = step
                pe.wait_ge(hn_ready[s], n + 1)
                for c in range(KC):
                    last = tr(bank(s, 3)[:, c * P:(c + 1) * P], hn[s][:, c * P:(c + 1) * P], id_s[:, :])
                last.then_inc(hnT_ps[s], 1)

            def up(s, step):
                n, l, it = step
                pe.wait_ge(hnT_ready[s], n + 1)
                for j in range(FB):
                    rows = P if j < FB - 1 else FLAST
                    for half in range(2):
                        o = (j % 2) * 256 + half * P
                        for c in range(KC):
                            last = mm(bank(s, j // 2)[0:rows, o:o + P], w1_s[:, l, c, half, j * P:j * P + rows], hnT[s][:, c, :],
                                      start=(c == 0), stop=(c == KC - 1))
                    if j % 2:
                        last.then_inc(up_ps[s], 1)

            def down(s, step):
                n, l, it = step
                for j in range(FB):
                    rows = P if j < FB - 1 else FLAST + 1
                    pe.wait_ge(u_ready[s], n * FB + j + 1)
                    last = mm(bank(s, 3)[:, 0:DIM], act_u[s][0:rows, j, :], w2_s[0:rows, l, j, :], start=(j == 0), stop=(j == FB - 1))
                last.then_inc(down_ps[s], 1)

            def half(x, xs, y, ys, t):
                if ys:
                    prob_T(y, ys, 0)
                x_T(x, xs)
                if ys:
                    prob_T(y, ys, 1)
                project(x, xs, 1, k_ps)
                if ys:
                    attend(y, ys)
                project(x, xs, 0, q_ps)
                if ys:
                    out_project(y, ys)
                project(x, xs, 2, v_ps, (0,))
                heads_T(x, xs, 1, 1, kT_ps)
                if ys:
                    shift_x1(y, ys)
                heads_T(x, xs, 0, 3, qT_ps)
                project(x, xs, 2, v_ps, (1,))
                scores(x, xs, 0)
                scores(x, xs, 1)
                if ys:
                    hn_T(y, ys)
                scores(x, xs, 2)
                scores(x, xs, 3)
                if ys:
                    up(y, ys)
                    down(y, ys)

            def start(step):
                pass

            def end(step):
                prob_T(1, step, 0)
                prob_T(1, step, 1)
                attend(1, step)
                out_project(1, step)
                shift_x1(1, step)
                hn_T(1, step)
                up(1, step)
                down(1, step)

            run(pe, start, half, end)


def transformer_constants():
    half = np.arange(0, HD, 2, dtype=np.float32)
    inv_freq = (1.0 / np.float32(10000.0) ** (half / np.float32(HD))).astype(np.float32)
    t = np.arange(SEQ, dtype=np.float32)
    freqs = np.concatenate([t[:, None] * inv_freq] * 2, 1)
    base = (half + np.float32(0.4 * HD)) / np.float32(1.4 * HD)
    power = (t - SEQ // 2) / np.float32(P // 2)
    scale = np.concatenate([base[None, :] ** power[:, None]] * 2, 1).astype(np.float32)
    cos, sin = np.cos(freqs), np.sin(freqs)
    sign = np.where(np.arange(HD) < HD // 2, -1.0, 1.0).astype(np.float32)
    tab = np.stack([np.stack([8 * cos * scale, cos / scale]), np.stack([8 * sign * sin * scale, sign * sin / scale])])
    tab = tab.reshape(2, 2, TILES, P, HD).transpose(3, 2, 0, 1, 4).astype(np.float32)
    i, j = np.arange(P)[:, None], np.arange(2 * P)[None, :] - P
    masks = np.zeros((P, TILES, 2 * P + 1), np.float32)
    masks[:, :, :2 * P] = np.where((i < j) | (i > j + P), -3e38, 0.0)[:, None, :]
    masks[:, 0, :P] = -3e38
    masks[:, 1:, 2 * P] = 1.0
    shift = np.eye(P, k=1, dtype=np.float32)
    carry = np.zeros((P, P), np.float32)
    carry[P - 1, 0] = 1.0
    return tab, masks, shift, carry


def program(nc, B, d, xn_d, attn_d, out):
    with ExitStack() as ctx:
        wqkv_s = ctx.enter_context(nc.sbuf_tensor("wqkv_s", [P, LAYERS, KC, 3 * INNER], F32))
        later = [(wqkv_s[:, :, :, :], d["wqkv"])]
        taylor_block(nc, B, d["x"], d["t_wqk"], d["t_wv"], d["t_wo"], d["ident"], d["ident_bf"], d["causal"], d["earlier"],
                     d["eps_rows"], d["keep_rows"], later, xn_d, attn_d)
        transformer_block(nc, B // 2, d["x"], xn_d, attn_d, wqkv_s, d["wo"], d["w1"], d["b1"], d["w2"], d["ln"], d["scales"],
                          d["rotary"], d["masks"], d["ident"], d["shift"], d["carry_row"], out)


def chunked(w):
    return w.reshape(-1, P, w.shape[-1]).transpose(1, 0, 2)


def kernel(**inputs):
    import ml_dtypes
    import concourse.bacc as _bacc
    from concourse.bass_utils import run_bass_kernel_spmd as _run

    a = {k: np.asarray(v) for k, v in inputs.items()}
    x = a["L0_attn_hidden_states"]
    B = x.shape[0]
    f = {k[len("L0_ffn_"):]: v for k, v in a.items() if k.startswith("L0_ffn_")}

    two = a["L0_attn_Wo"].T.reshape(GROUPS // 2, 2, GH, TD, DIM).transpose(0, 2, 1, 3, 4)
    b1 = np.zeros((LAYERS, 2, FB * P), np.float32)
    b1[..., :HID] = f["b1"].reshape(LAYERS, 2, HID)
    w2 = np.zeros((LAYERS, FB * P, DIM), np.float32)
    w2[:, :HID] = f["w2"]
    w2[:, HID] = f["b2"]
    ln = np.stack([f["ln_g"], f["ln_b"]], 1)
    scales = np.stack([f["q_scale"], f["k_scale"]], 1)
    scales = np.stack([scales, np.roll(scales, HD // 2, -1)], 1)

    arrays = {
        "x": x,
        "t_wqk": chunked(np.concatenate([a["L0_attn_Wq"].T, a["L0_attn_Wk"].T], 1)),
        "t_wv": chunked(a["L0_attn_Wv"].T),
        "t_wo": chunked(two.reshape(TH * TD, DIM)),
        "wqkv": f["wqkv"].reshape(LAYERS, KC, P, 3 * INNER).transpose(2, 0, 1, 3),
        "wo": f["wo"].reshape(LAYERS, INNER // P, P, DIM).transpose(2, 0, 1, 3),
        "w1": f["w1"].reshape(LAYERS, KC, P, 2, HID).transpose(2, 0, 1, 3, 4),
        "b1": b1.reshape(LAYERS, 2, FB, P).transpose(3, 0, 1, 2),
        "w2": w2.reshape(LAYERS, FB, P, DIM).transpose(2, 0, 1, 3),
        "ln": ln.reshape(LAYERS, 2, KC, P).transpose(3, 0, 1, 2),
        "scales": scales,
        "ident": np.eye(P, dtype=np.float32),
        "ident_bf": np.eye(P, dtype=np.float32).astype(ml_dtypes.bfloat16),
    }
    for name, c in zip(("causal", "earlier", "eps_rows", "keep_rows"), taylor_constants()):
        arrays[name] = c
    for name, c in zip(("rotary", "masks", "shift", "carry_row"), transformer_constants()):
        arrays[name] = c
    arrays = {f"{k}_dram": np.ascontiguousarray(v) for k, v in arrays.items()}

    nc = _bacc.Bacc("TRN2", target_bir_lowering=False, num_devices=1)
    d = {k[:-5]: nc.dram_tensor(k, v.shape, mybir.dt.from_np(v.dtype), kind="ExternalInput").ap() for k, v in arrays.items()}
    out = nc.dram_tensor("out_dram", x.shape, F32, kind="ExternalOutput").ap()
    xn_d = nc.dram_tensor("xn_dram", x.shape, F32).ap()
    attn_d = nc.dram_tensor("attn_dram", x.shape, F32).ap()

    program(nc, B, d, xn_d, attn_d, out)
    return _run(nc, [arrays], core_ids=[0]).results[0]["out_dram"]
```
